# Optimizing a Trainium2 kernel written in Bass

```python
import numpy as np
import jax
import jax.numpy as jnp

def _softmax(x, axis=-1):
    return jax.nn.softmax(x, axis=axis)

def _gelu(x):
    return jax.nn.gelu(x, approximate=True)

def _silu(x):
    return jax.nn.silu(x)

def _sigmoid(x):
    return jax.nn.sigmoid(x)

def _layernorm(x, axis=-1, eps=1e-05):
    m = jnp.mean(x, axis=axis, keepdims=True)
    v = jnp.var(x, axis=axis, keepdims=True)
    return (x - m) / jnp.sqrt(v + eps)

def _scatter_add(tgt, idx, src, axis=0):
    return tgt.at[idx].add(src)

def _segment_sum(src, seg, n):
    return jax.ops.segment_sum(src, seg, n)
kernel_name = 'mk_gnn_preln_d4_gnn_r8_c975c9'

def setup_inputs(seed: int=0):
    np.random.seed(seed)
    _w = jnp.asarray

    def _rec_inputs():
        import jax
        import jax.numpy as jnp
        _gk = jax.random.key(seed)
        x = -0.0003713 + 1 * jax.random.normal(jax.random.fold_in(_gk, 1), (12500, 128), jnp.float32)
        src = jax.random.randint(jax.random.fold_in(_gk, 2), (200000,), 0, 12500, jnp.int32)
        dst = jax.random.randint(jax.random.fold_in(_gk, 3), (200000,), 0, 12500, jnp.int32)
        _o = jnp.argsort(dst, stable=True)
        src = src[_o]
        dst = dst[_o]
        edge_attr_32 = 0.000196303 + 1.00016 * jax.random.normal(jax.random.fold_in(_gk, 13), (200000, 32), jnp.float32)
        edge_weight = jax.random.uniform(jax.random.fold_in(_gk, 15), (200000,), jnp.float32, 0.0, 1)
        edge_weight1 = jax.random.uniform(jax.random.fold_in(_gk, 16), (200000, 1), jnp.float32, 0.0, 1)
        node_vec1 = jax.random.uniform(jax.random.fold_in(_gk, 17), (12500, 1), jnp.float32, 0.0, 1)
        return (x, src, dst, edge_attr_32, edge_weight, edge_weight1, node_vec1)
    x, src, dst, edge_attr_32, edge_weight, edge_weight1, node_vec1 = _rec_inputs()

    def _L0_gnn_setup():
        import jax, jax.numpy as jnp
        import numpy as np
        N = 12500
        E = 100000
        D = 128
        key = jax.random.key(seed)
        ks = jax.random.split(key, 12)
        s = lambda fan_in: 1.0 / np.sqrt(fan_in)
        return {'h': jax.random.normal(ks[0], (N, D), dtype=jnp.float32), 'w': jax.random.uniform(ks[1], (E,), dtype=jnp.float32), 'src': jax.random.randint(ks[2], (E,), 0, N, dtype=jnp.int32), 'dst': jax.random.randint(ks[3], (E,), 0, N, dtype=jnp.int32), 'W1': jax.random.uniform(ks[4], (2 * D + 1, D), jnp.float32, -s(2 * D + 1), s(2 * D + 1)), 'b1': jnp.zeros((D,), jnp.float32), 'W2': jax.random.uniform(ks[5], (D, D), jnp.float32, -s(D), s(D)), 'b2': jnp.zeros((D,), jnp.float32), 'U1': jax.random.uniform(ks[6], (2 * D, D), jnp.float32, -s(2 * D), s(2 * D)), 'c1': jnp.zeros((D,), jnp.float32), 'U2': jax.random.uniform(ks[7], (D, D), jnp.float32, -s(D), s(D)), 'c2': jnp.zeros((D,), jnp.float32)}
    _L0_gnn_all = _L0_gnn_setup()
    _L0_gnn_in = {k: v for k, v in _L0_gnn_all.items() if k in ('W1', 'b1', 'W2', 'b2', 'U1', 'c1', 'U2', 'c2')}
    del _L0_gnn_all

    def _L1_gnn_setup():
        import jax, jax.numpy as jnp
        import numpy as np
        N_NODES = 12500
        D_IN = 128
        D_OUT = 128
        N_EDGES = 200000
        BN_EPS = 1e-05

        def _glorot(key, fan_in, fan_out):
            limit = np.sqrt(6.0 / (fan_in + fan_out))
            return jax.random.uniform(key, (fan_in, fan_out), jnp.float32, -limit, limit)
        key = jax.random.key(seed)
        k_x, k_e, k0, k1, k2 = jax.random.split(key, 5)
        x = jax.random.normal(k_x, (N_NODES, D_IN), jnp.float32)
        edge_index = jax.random.randint(k_e, (2, N_EDGES), 0, N_NODES, jnp.int64)
        return {'x': x, 'edge_index': edge_index, 'kernel': _glorot(k0, D_IN, D_OUT), 'kernel1': _glorot(k1, D_IN, D_IN), 'kernel2': _glorot(k2, D_IN, D_IN), 'gamma': jnp.ones((D_IN,), jnp.float32), 'beta': jnp.zeros((D_IN,), jnp.float32)}
    _L1_gnn_all = _L1_gnn_setup()
    _L1_gnn_in = {k: v for k, v in _L1_gnn_all.items() if k in ('kernel', 'kernel1', 'kernel2', 'gamma', 'beta')}
    del _L1_gnn_all

    def _L2_gnn_setup():
        import jax, jax.numpy as jnp
        import numpy as np
        N, E = (6250, 100000)
        C, A_ALL, RAD_IN, FC1, FC2 = (128, 256, 32, 64, 64)
        H, AH, VH = (8, 16, 16)

        def _radial_mlp(x, w1, b1, w2, b2, w3, b3):
            x = jax.nn.silu(x @ w1 + b1)
            x = jax.nn.silu(x @ w2 + b2)
            return x @ w3 + b3

        def _smooth_leaky_relu(x, a=0.2):
            return 0.5 * (1.0 + a) * x + 0.5 * (1.0 - a) * x * (2.0 * jax.nn.sigmoid(x) - 1.0)

        def _segment_softmax(scores, seg, num_segments):
            m = jax.ops.segment_max(scores, seg, num_segments=num_segments)
            m = jnp.where(jnp.isfinite(m), m, 0.0)
            e = jnp.exp(scores - m[seg])
            s = jax.ops.segment_sum(e, seg, num_segments=num_segments)
            return e / (s[seg] + 1e-16)
        key = jax.random.key(seed)
        ks = jax.random.split(key, 16)

        def g(k, shape):
            scale = 1.0 / np.sqrt(shape[0])
            return jax.random.normal(k, shape, dtype=jnp.float32) * scale
        return {'node_input': jax.random.normal(ks[0], (N, C), dtype=jnp.float32), 'node_attr': jnp.ones((N, 1), jnp.float32), 'edge_attr': jax.random.uniform(ks[1], (E, 1), dtype=jnp.float32), 'edge_scalars': jax.random.normal(ks[2], (E, RAD_IN), dtype=jnp.float32), 'edge_src': jax.random.randint(ks[3], (E,), 0, N, dtype=jnp.int32), 'edge_dst': jax.random.randint(ks[4], (E,), 0, N, dtype=jnp.int32), 'batch': jnp.zeros((N,), jnp.int32), 'w_src': g(ks[5], (C, C)), 'b_src': jnp.zeros((C,), jnp.float32), 'w_dst': g(ks[6], (C, C)), 'fc_w1': g(ks[7], (RAD_IN, FC1)), 'fc_b1': jnp.zeros((FC1,), jnp.float32), 'fc_w2': g(ks[8], (FC1, FC2)), 'fc_b2': jnp.zeros((FC2,), jnp.float32), 'fc_w3': g(ks[9], (FC2, C)), 'fc_b3': jnp.zeros((C,), jnp.float32), 'w_sep': g(ks[10], (C, A_ALL)), 'b_sep': jnp.zeros((A_ALL,), jnp.float32), 'alpha_dot': jax.random.normal(ks[11], (1, H, AH), dtype=jnp.float32) * np.sqrt(2.0 / (H * AH)), 'w_proj': g(ks[12], (H * VH, C)), 'b_proj': jnp.zeros((C,), jnp.float32)}
    _L2_gnn_all = _L2_gnn_setup()
    _L2_gnn_in = {k: v for k, v in _L2_gnn_all.items() if k in ('w_src', 'b_src', 'w_dst', 'fc_w1', 'fc_b1', 'fc_w2', 'fc_b2', 'fc_w3', 'fc_b3', 'w_sep', 'b_sep', 'alpha_dot', 'w_proj', 'b_proj')}
    del _L2_gnn_all

    def _L3_gnn_setup():
        import jax, jax.numpy as jnp
        import numpy as np
        N_NODES = 6250
        N_EDGES = 75000
        D = 128
        key = jax.random.key(seed)
        k1, k2, k3, k4 = jax.random.split(key, 4)
        feature = jax.random.normal(k1, (N_NODES, D), dtype=jnp.float32)
        src = jax.random.randint(k2, (N_EDGES,), 0, N_NODES, dtype=jnp.int32)
        dst = jax.random.randint(k3, (N_EDGES,), 0, N_NODES, dtype=jnp.int32)
        W = jax.random.normal(k4, (D, D), dtype=jnp.float32) * (1.0 / np.sqrt(D))
        b = jnp.zeros((D,), dtype=jnp.float32)
        return {'feature': feature, 'src': src, 'dst': dst, 'W': W, 'b': b}
    _L3_gnn_all = _L3_gnn_setup()
    _L3_gnn_in = {k: v for k, v in _L3_gnn_all.items() if k in ('W', 'b')}
    del _L3_gnn_all
    return {'x': x, 'src': src, 'dst': dst, 'edge_attr_32': edge_attr_32, 'edge_weight': edge_weight, 'edge_weight1': edge_weight1, 'node_vec1': node_vec1, 'L0_gnn_W1': _L0_gnn_in['W1'], 'L0_gnn_b1': _L0_gnn_in['b1'], 'L0_gnn_W2': _L0_gnn_in['W2'], 'L0_gnn_b2': _L0_gnn_in['b2'], 'L0_gnn_U1': _L0_gnn_in['U1'], 'L0_gnn_c1': _L0_gnn_in['c1'], 'L0_gnn_U2': _L0_gnn_in['U2'], 'L0_gnn_c2': _L0_gnn_in['c2'], 'L1_gnn_kernel': _L1_gnn_in['kernel'], 'L1_gnn_kernel1': _L1_gnn_in['kernel1'], 'L1_gnn_kernel2': _L1_gnn_in['kernel2'], 'L1_gnn_gamma': _L1_gnn_in['gamma'], 'L1_gnn_beta': _L1_gnn_in['beta'], 'L2_gnn_w_src': _L2_gnn_in['w_src'], 'L2_gnn_b_src': _L2_gnn_in['b_src'], 'L2_gnn_w_dst': _L2_gnn_in['w_dst'], 'L2_gnn_fc_w1': _L2_gnn_in['fc_w1'], 'L2_gnn_fc_b1': _L2_gnn_in['fc_b1'], 'L2_gnn_fc_w2': _L2_gnn_in['fc_w2'], 'L2_gnn_fc_b2': _L2_gnn_in['fc_b2'], 'L2_gnn_fc_w3': _L2_gnn_in['fc_w3'], 'L2_gnn_fc_b3': _L2_gnn_in['fc_b3'], 'L2_gnn_w_sep': _L2_gnn_in['w_sep'], 'L2_gnn_b_sep': _L2_gnn_in['b_sep'], 'L2_gnn_alpha_dot': _L2_gnn_in['alpha_dot'], 'L2_gnn_w_proj': _L2_gnn_in['w_proj'], 'L2_gnn_b_proj': _L2_gnn_in['b_proj'], 'L3_gnn_W': _L3_gnn_in['W'], 'L3_gnn_b': _L3_gnn_in['b']}

def reference(x, src, dst, edge_attr_32, edge_weight, edge_weight1, node_vec1, L0_gnn_W1, L0_gnn_b1, L0_gnn_W2, L0_gnn_b2, L0_gnn_U1, L0_gnn_c1, L0_gnn_U2, L0_gnn_c2, L1_gnn_kernel, L1_gnn_kernel1, L1_gnn_kernel2, L1_gnn_gamma, L1_gnn_beta, L2_gnn_w_src, L2_gnn_b_src, L2_gnn_w_dst, L2_gnn_fc_w1, L2_gnn_fc_b1, L2_gnn_fc_w2, L2_gnn_fc_b2, L2_gnn_fc_w3, L2_gnn_fc_b3, L2_gnn_w_sep, L2_gnn_b_sep, L2_gnn_alpha_dot, L2_gnn_w_proj, L2_gnn_b_proj, L3_gnn_W, L3_gnn_b):
    import jax
    import jax.numpy as jnp

    def _L0_gnn_ref(h, w, src, dst, W1, b1, W2, b2, U1, c1, U2, c2):
        import jax, jax.numpy as jnp
        import numpy as np
        N = 12500
        E = 100000
        D = 128
        n = h.shape[0]
        msg_in = jnp.concatenate([h[src], h[dst], w[:, None]], axis=1)
        msg = jax.nn.relu(msg_in @ W1 + b1) @ W2 + b2
        agg = jax.ops.segment_max(msg, dst, num_segments=n)
        deg = jax.ops.segment_sum(jnp.ones((dst.shape[0],), jnp.int32), dst, num_segments=n)
        agg = jnp.where((deg > 0)[:, None], agg, jnp.zeros((), h.dtype))
        upd_in = jnp.concatenate([h, agg], axis=1)
        return jax.nn.relu(upd_in @ U1 + c1) @ U2 + c2

    def _L1_gnn_ref(x, edge_index, kernel, kernel1, kernel2, gamma, beta):
        import jax, jax.numpy as jnp
        import numpy as np
        N_NODES = 12500
        D_IN = 128
        D_OUT = 128
        N_EDGES = 200000
        BN_EPS = 1e-05

        def _glorot(key, fan_in, fan_out):
            limit = np.sqrt(6.0 / (fan_in + fan_out))
            return jax.random.uniform(key, (fan_in, fan_out), jnp.float32, -limit, limit)
        N = x.shape[0]
        mean = jnp.mean(x, axis=0)
        var = jnp.var(x, axis=0)
        xn = (x - mean) * jax.lax.rsqrt(var + BN_EPS) * gamma + beta
        mapped = xn @ kernel
        s1 = jnp.tanh(jnp.sum(xn @ kernel1 * xn, axis=1))
        s2 = jnp.tanh(jnp.sum(xn @ kernel2 * xn, axis=1))
        src, dst = (edge_index[0], edge_index[1])
        e = jax.nn.leaky_relu(s1[src] + s2[dst], negative_slope=0.01)
        emax = jax.ops.segment_max(e, src, num_segments=N)
        emax = jnp.where(jnp.isfinite(emax), emax, 0.0)
        ee = jnp.exp(e - emax[src])
        denom = jax.ops.segment_sum(ee, src, num_segments=N)
        attn = ee / jnp.maximum(denom[src], 1e-16)
        out = jax.ops.segment_sum(attn[:, None] * mapped[dst], src, num_segments=N)
        return jax.nn.relu(out)

    def _L2_gnn_ref(node_input, node_attr, edge_attr, edge_scalars, edge_src, edge_dst, batch, w_src, b_src, w_dst, fc_w1, fc_b1, fc_w2, fc_b2, fc_w3, fc_b3, w_sep, b_sep, alpha_dot, w_proj, b_proj):
        import jax, jax.numpy as jnp
        import numpy as np
        N, E = (6250, 100000)
        C, A_ALL, RAD_IN, FC1, FC2 = (128, 256, 32, 64, 64)
        H, AH, VH = (8, 16, 16)

        def _radial_mlp(x, w1, b1, w2, b2, w3, b3):
            x = jax.nn.silu(x @ w1 + b1)
            x = jax.nn.silu(x @ w2 + b2)
            return x @ w3 + b3

        def _smooth_leaky_relu(x, a=0.2):
            return 0.5 * (1.0 + a) * x + 0.5 * (1.0 - a) * x * (2.0 * jax.nn.sigmoid(x) - 1.0)

        def _segment_softmax(scores, seg, num_segments):
            m = jax.ops.segment_max(scores, seg, num_segments=num_segments)
            m = jnp.where(jnp.isfinite(m), m, 0.0)
            e = jnp.exp(scores - m[seg])
            s = jax.ops.segment_sum(e, seg, num_segments=num_segments)
            return e / (s[seg] + 1e-16)
        n_nodes = node_input.shape[0]
        n_edges = edge_src.shape[0]
        msg_src = node_input @ w_src + b_src
        msg_dst = node_input @ w_dst
        message = msg_src[edge_src] + msg_dst[edge_dst]
        rad_w = _radial_mlp(edge_scalars, fc_w1, fc_b1, fc_w2, fc_b2, fc_w3, fc_b3)
        message = message * edge_attr * rad_w
        message = message @ w_sep + b_sep
        msg_h = message.reshape(n_edges, H, AH + VH)
        alpha = _smooth_leaky_relu(msg_h[:, :, :AH])
        value = msg_h[:, :, AH:]
        score = jnp.einsum('ehk,ahk->eh', alpha, alpha_dot)
        att = _segment_softmax(score, edge_dst, n_nodes)[..., None]
        out = jax.ops.segment_sum(value * att, edge_dst, num_segments=n_nodes)
        out = out.reshape(n_nodes, H * VH)
        return out @ w_proj + b_proj

    def _L3_gnn_ref(feature, src, dst, W, b):
        import jax, jax.numpy as jnp
        import numpy as np
        N_NODES = 6250
        N_EDGES = 75000
        D = 128
        msgs = feature[src]
        agg = jax.ops.segment_sum(msgs, dst, num_segments=feature.shape[0])
        h = agg + feature
        return h @ W.T + b
    edge_index = jnp.stack([src, dst])
    batch0 = jnp.zeros((12500,), jnp.int32)
    h = jnp.maximum(_layernorm(x, axis=-1), 0.0)
    x = x + _L0_gnn_ref(h, edge_weight, src, dst, L0_gnn_W1, L0_gnn_b1, L0_gnn_W2, L0_gnn_b2, L0_gnn_U1, L0_gnn_c1, L0_gnn_U2, L0_gnn_c2)
    h = jnp.maximum(_layernorm(x, axis=-1), 0.0)
    x = x + _L1_gnn_ref(h, edge_index, L1_gnn_kernel, L1_gnn_kernel1, L1_gnn_kernel2, L1_gnn_gamma, L1_gnn_beta)
    h = jnp.maximum(_layernorm(x, axis=-1), 0.0)
    x = x + _L2_gnn_ref(h, node_vec1, edge_weight1, edge_attr_32, src, dst, batch0, L2_gnn_w_src, L2_gnn_b_src, L2_gnn_w_dst, L2_gnn_fc_w1, L2_gnn_fc_b1, L2_gnn_fc_w2, L2_gnn_fc_b2, L2_gnn_fc_w3, L2_gnn_fc_b3, L2_gnn_w_sep, L2_gnn_b_sep, L2_gnn_alpha_dot, L2_gnn_w_proj, L2_gnn_b_proj)
    h = jnp.maximum(_layernorm(x, axis=-1), 0.0)
    x = x + _L3_gnn_ref(h, src, dst, L3_gnn_W, L3_gnn_b)
    return x

_drawn_inputs = setup_inputs


def setup_inputs(seed=0):
    import zlib

    import numpy as np

    out = dict(_drawn_inputs(seed))
    spreads = {'L0_gnn_b1': (0.0, 0.8),
     'L0_gnn_b2': (0.0, 0.459),
     'L0_gnn_c1': (0.0, 0.1),
     'L0_gnn_c2': (0.0, 0.1),
     'L1_gnn_gamma': (1.0, 0.2),
     'L1_gnn_beta': (0.0, 0.1),
     'L2_gnn_b_src': (0.0, 0.749),
     'L2_gnn_fc_b1': (0.0, 0.8),
     'L2_gnn_fc_b2': (0.0, 0.505),
     'L2_gnn_fc_b3': (0.0, 0.1),
     'L2_gnn_b_sep': (0.0, 0.401),
     'L2_gnn_b_proj': (0.0, 0.589),
     'L3_gnn_b': (0.0, 0.613)}
    factors = {'edge_attr_32': 3.008,
     'edge_weight': 8.0,
     'edge_weight1': 5.153,
     'L0_gnn_W1': 4.205,
     'L2_gnn_alpha_dot': 8.0}
    for name, (base, spread) in spreads.items():
        noise = np.random.default_rng([zlib.crc32(name.encode()), seed]).standard_normal(out[name].shape)
        drawn = base * np.exp(spread * noise) if base else spread * noise
        out[name] = jnp.asarray(drawn.astype(out[name].dtype))
    for name, factor in factors.items():
        out[name] = (out[name] * factor).astype(out[name].dtype)
    return out
```

```python
from contextlib import ExitStack

import numpy as np
import concourse.bass as bass
from concourse import mybir

F32 = mybir.dt.float32
BF16 = mybir.dt.bfloat16
I32 = mybir.dt.int32
ALU = mybir.AluOpType
ACT = mybir.ActivationFunctionType
AX = mybir.AxisListType
ds = bass.ds

P = 128
TPG = 4
G = TPG * P
SLOTS = 4
NPG = 2
NG = NPG * P
ADDERS = 8
W1COLS = P + 2
W2COLS = P + 8
BIG = -1.0e30


def later(i):
    return not isinstance(i, int) or i > 0


def back(i, b, d, n):
    at = i - (d - b + 1) // 2
    return None if isinstance(at, int) and not 0 <= at < n else (at, (b - d) % 2)


def nth(i, b, less=0):
    return i * 2 + (b + 1 - less)


def nth4(i, b, less=0):
    return i * SLOTS + (b + 1 - less)


def after(i, b, d):
    return not isinstance(i, int) or i * SLOTS + b >= d


def uses(i, b, d):
    steps = 1 - (d - b + SLOTS - 1) // SLOTS
    return (b - d) % SLOTS, i if steps == 0 else i + steps


def stages(i, n, lags):
    for b in range(SLOTS):
        for stage, lag, *past in lags:
            at, slot = i - (lag - b + SLOTS - 1) // SLOTS, (b - lag) % SLOTS
            if not isinstance(at, int) or (at >= 0 and at * SLOTS + slot < n * SLOTS + sum(past)):
                stage(at, slot)


def pipelined4(eng, n, lags, deepest):
    extra = (deepest + SLOTS - 1) // SLOTS
    for i in range(min(n, extra + 1)):
        stages(i, n, lags)
    if n > extra + 1:
        with eng.Fori(extra + 1, n) as i:
            stages(i, n, lags)
    for i in range(n, n + extra):
        stages(i, n, lags)


def pipelined(eng, n, body, deepest=2):
    extra = (deepest + 1) // 2
    for i in range(min(n, extra + 1)):
        body(i)
    if n > extra + 1:
        with eng.Fori(extra + 1, n) as i:
            body(i)
    for i in range(n, n + extra):
        body(i)


class Kit:

    def __init__(self, nc, ctx, n, e):
        self.nc, self.ctx, self.N, self.E = nc, ctx, n, e
        self.held = []
        self.EP = -(-e // 2048) * 2048
        self.Q = self.EP // 2048
        self.NT = self.EP // P
        self.STEPS4 = self.EP // (SLOTS * G)
        self.STEPS = self.EP // (2 * G)
        self.NP = -(-(n + 1) // (2 * NG)) * 2 * NG
        self.TN = self.NP // P
        self.NSTEPS = self.NP // (2 * NG)

    def dram(self, name, shape, dt=F32):
        return self.nc.dram_tensor(name, shape, dt, kind="Internal").ap()

    def sb(self, ctx, name, shape, dt=F32):
        return ctx.enter_context(self.nc.sbuf_tensor(name, shape, dt))

    def ps(self, ctx, name, shape):
        t = ctx.enter_context(self.nc.psum_tensor(name, [P, 512], F32))
        t = t[0:shape[0], 0:int(np.prod(shape[1:]))]
        return t if len(shape) == 2 else t.rearrange("p (a b) -> p a b", a=shape[1])

    def sem(self, name):
        self.held.append(self.nc.alloc_semaphore(name=name))
        return self.held[-1]

    def release_semaphores(self):
        self.nc.all_engine_barrier()
        self.nc.clear_and_free_semaphores(self.held)
        self.nc.all_engine_barrier()
        self.held = []

    def constants(self, ctx):
        self.ident, self.below, self.ones = (self.sb(ctx, x, [P, P]) for x in ("ident", "below", "ones"))
        self.above = self.sb(ctx, "above", [P, P])
        self.lane, self.spare = self.sb(ctx, "lane", [P, 1]), self.sb(ctx, "spare", [P, 1])
        self.base_row = self.sb(ctx, "base_row", [1, self.NT], I32)
        self.src_col, self.src_int = self.sb(ctx, "src_col", [P, self.NT]), self.sb(ctx, "src_int", [P, self.NT], I32)
        self.rank_of, self.last_of = (self.sb(ctx, x, [P, self.TN], I32) for x in ("rank_of", "last_of"))
        self.has = self.sb(ctx, "has_edges", [P, self.TN])
        self.settled = ctx.enter_context(self.nc.semaphore("settled"))

    def settle(self, pool):
        pool.sem_inc(self.settled, 1)


def chain(eng, sem):
    count = [0]

    def link(instruction):
        count[0] += 1
        instruction.then_inc(sem, 1)
        eng.wait_ge(sem, count[0])
    return link


def setup_edges(k, a):
    nc, Q, N, E, EP, NT = k.nc, k.Q, k.N, k.E, k.EP, k.NT
    k.SRC, k.DST = k.dram("src_padded", (EP,), I32), k.dram("dst_padded", (1 + EP,), I32)
    k.SRCF, k.DSTF = k.dram("src_float", (EP,)), k.dram("dst_float", (NT, P))
    k.HEADS = k.dram("tile_heads", (NT,))
    k.KEEP, k.NEW = k.dram("same_run", (EP,), BF16), k.dram("new_run", (EP,), BF16)
    k.REL, k.BASE = k.dram("rank_in_window", (EP,), BF16), k.dram("window_base", (NT,), I32)
    k.LOW = k.dram("src_low", (EP,), BF16)
    k.EW, k.EA, k.EATT = k.dram("w0_padded", (EP,)), k.dram("w1_padded", (EP,)), k.dram("attr_padded", (EP, 32))
    k.ADD = [k.dram(f"added{t}", (k.NP + P, W1COLS)) for t in range(ADDERS)]
    k.TB0, k.TB1, k.TB2 = (k.dram(f"by_rank_{n}", (k.NP + P, w)) for n, w in enumerate((P, W1COLS, P)))
    s_fill, s_edge, s_in, s_f, s_dve, s_off, s_mask, s_out, s_tr, s_cp, s_head, s_zero, s_ident = (
        k.sem("se_" + x) for x in "fill edge in float dve off mask out tr cp head zero ident".split())
    with ExitStack() as c, nc.Block() as block:
        pad = EP - E
        fill_i = k.sb(c, "fill_i", [1, pad + 1], I32)
        fill_0 = k.sb(c, "fill_0", [32, pad])
        zero = k.sb(c, "zero", [P, 26 * W1COLS])
        cur, prv, srci = (k.sb(c, f"q_int{n}", [Q, 2048], I32) for n in range(3))
        curf, prvf, srcf, new, rank, nul = (k.sb(c, f"q_f{n}", [Q, 2048]) for n in range(6))
        keep_b, new_b, rel_b = (k.sb(c, f"q_b{n}", [Q, 2048], BF16) for n in range(3))
        low_i, low_b = k.sb(c, "q_low_int", [Q, 2048], I32), k.sb(c, "q_low", [Q, 2048], BF16)
        off = k.sb(c, "off", [Q, 1])
        base_f, heads = k.sb(c, "base_f", [Q, 16]), k.sb(c, "heads_q", [Q, 16])
        base_i = k.sb(c, "base_i", [Q, 16], I32)
        p_off = k.ps(c, "p_off", [Q, 1])
        p_tr = [k.ps(c, f"p_tr{n}", [P, Q]) for n in range(2)]

        @block.gpsimd
        def _(pool):
            pool.memset(fill_i[:, 0:pad], N).then_inc(s_fill, 1)
            pool.memset(fill_i[:, pad:pad + 1], -1).then_inc(s_fill, 1)
            pool.memset(fill_0[:], 0.0).then_inc(s_fill, 1)
            pool.memset(zero[:], 0.0).then_inc(s_fill, 1)
            pool.memset(nul[:], 0.0).then_inc(s_fill, 1)
            pool.memset(k.ident[:], 0.0).then_inc(s_ident, 1)
            pool.memset(k.below[:], 1.0).then_inc(s_ident, 1)
            pool.memset(k.above[:], 1.0).then_inc(s_ident, 1)
            pool.memset(k.ones[:], 1.0).then_inc(s_ident, 1)
            pool.wait_ge(s_ident, 4)
            pool.affine_select(out=k.ident[:], in_=k.ident[:], compare_op=ALU.not_equal, fill=1.0,
                               base=0, pattern=[[-1, P]], channel_multiplier=1).then_inc(s_ident, 1)
            pool.affine_select(out=k.below[:], in_=k.below[:], compare_op=ALU.is_gt, fill=0.0,
                               base=0, pattern=[[1, P]], channel_multiplier=-1).then_inc(s_ident, 1)
            pool.affine_select(out=k.above[:], in_=k.above[:], compare_op=ALU.is_gt, fill=0.0,
                               base=0, pattern=[[-1, P]], channel_multiplier=1).then_inc(s_ident, 1)
            pool.iota(k.lane[:], pattern=[[0, 1]], base=0, channel_multiplier=1,
                      allow_small_or_imprecise_dtypes=True).then_inc(s_ident, 1)
            pool.iota(k.spare[:], pattern=[[0, 1]], base=k.NP, channel_multiplier=1,
                      allow_small_or_imprecise_dtypes=True).then_inc(s_ident, 1)

        @block.sync
        def _(sp):
            sp.dma_start(k.SRC[0:E], a["src"]).then_inc(s_edge, 16)
            sp.dma_start(k.DST[1:1 + E], a["dst"]).then_inc(s_edge, 16)
            sp.dma_start(k.EW[0:E], a["edge_weight"]).then_inc(s_out, 16)
            sp.dma_start(k.EA[0:E], a["edge_weight1"].rearrange("e o -> (e o)")).then_inc(s_out, 16)
            sp.dma_start(k.EATT[0:E, :], a["edge_attr_32"]).then_inc(s_out, 16)
            sp.wait_ge(s_fill, 5)
            sp.dma_start(k.SRC[E:EP].unsqueeze(0), fill_i[:, 0:pad]).then_inc(s_edge, 16)
            sp.dma_start(k.DST[1 + E:].unsqueeze(0), fill_i[:, 0:pad]).then_inc(s_edge, 16)
            sp.dma_start(k.DST[0:1].unsqueeze(0), fill_i[:, pad:pad + 1]).then_inc(s_edge, 16)
            sp.dma_start(k.EW[E:].unsqueeze(0), fill_0[0:1, :]).then_inc(s_out, 16)
            sp.dma_start(k.EA[E:].unsqueeze(0), fill_0[0:1, :]).then_inc(s_out, 16)
            sp.dma_start(k.EATT[E:].rearrange("e f -> (e f)").rearrange("(p c) -> p c", p=32), fill_0[:]).then_inc(s_out, 16)
            sp.wait_ge(s_edge, 80)
            sp.dma_start(cur[:], k.DST[1:].rearrange("(q c) -> q c", q=Q)).then_inc(s_in, 16)
            sp.dma_start(prv[:], k.DST[0:EP].rearrange("(q c) -> q c", q=Q)).then_inc(s_in, 16)
            sp.dma_start(srci[:], k.SRC.rearrange("(q c) -> q c", q=Q)).then_inc(s_in, 16)
            sp.wait_ge(s_mask, 1)
            q2 = lambda t: t.rearrange("(q c) -> q c", q=Q)
            for to, of in ((q2(k.KEEP), keep_b), (q2(k.NEW), new_b), (q2(k.REL), rel_b), (q2(k.LOW), low_b), (q2(k.BASE), base_i),
                           (q2(k.SRCF), srcf), (k.DSTF.rearrange("(q t) p -> q (t p)", q=Q), curf)):
                sp.dma_start(to, of[:]).then_inc(s_out, 16)
            sp.dma_start(q2(k.HEADS), heads[:]).then_inc(s_head, 16)
            sp.wait_ge(s_head, 16)
            sp.wait_ge(s_out, 13 * 16)
            sp.dma_start(k.base_row[:], k.BASE.unsqueeze(0)).then_inc(s_in, 16)
            sp.wait_ge(s_in, 64)

        @block.scalar
        def _(act):
            act.wait_ge(s_fill, 5)
            rows, n = (k.NP + P) // P, 0
            for t in range(ADDERS):
                flat = k.ADD[t].rearrange("(p a) d -> p (a d)", p=P)
                for r in range(0, rows, 26):
                    w = min(26, rows - r) * W1COLS
                    act.dma_start(flat[:, r * W1COLS:r * W1COLS + w], zero[:, 0:w]).then_inc(s_zero, 16)
                    n += 1
            for t in (k.TB0, k.TB1, k.TB2):
                act.dma_start(t[k.NP:, :], zero[:, 0:t.shape[1]]).then_inc(s_zero, 16)
                n += 1
            for t in range(16):
                act.wait_ge(s_tr, t + 1)
                act.copy(k.src_col[:].rearrange("p (q t) -> p q t", t=16)[:, :, t], p_tr[t % 2][:]).then_inc(s_cp, 1)
            act.wait_ge(s_zero, 16 * n)

        @block.vector
        def _(dve):
            link = chain(dve, s_dve)
            dve.wait_ge(s_in, 48)
            dve.tensor_copy(curf[:], cur[:])
            dve.tensor_copy(prvf[:], prv[:])
            dve.tensor_scalar(low_i[:], srci[:], P - 1, None, ALU.bitwise_and)
            link(dve.tensor_copy(srcf[:], srci[:]))
            dve.tensor_copy(low_b[:], low_i[:])
            dve.tensor_scalar(heads[:], curf[:].rearrange("q (t p) -> q t p", p=P)[:, :, 0], 1.0, None, ALU.mult)
            dve.tensor_tensor(keep_b[:], curf[:], prvf[:], ALU.is_equal)
            link(dve.tensor_tensor(new[:], curf[:], prvf[:], ALU.not_equal))
            dve.tensor_scalar(new_b[:], new[:], BIG, None, ALU.mult)
            dve.wait_ge(s_fill, 5)
            dve.tensor_tensor_scan(out=rank[:], data0=new[:], data1=nul[:], initial=0.0,
                                   op0=ALU.add, op1=ALU.add).then_inc(s_off, 1)
            dve.wait_ge(s_tr, 17)
            link(dve.tensor_scalar(off[:], p_off[:], 1.0, None, ALU.subtract))
            link(dve.tensor_scalar(rank[:], rank[:], off[:], None, ALU.add))
            r3 = rank[:].rearrange("q (t p) -> q t p", p=P)
            link(dve.tensor_scalar(base_f[:], r3[:, :, 0], 1.0, None, ALU.mult))
            dve.tensor_copy(base_i[:], base_f[:])
            dve.tensor_tensor(rel_b[:].rearrange("q (t p) -> q t p", p=P), r3,
                              base_f[:].unsqueeze(2).to_broadcast([Q, 16, P]), ALU.subtract).then_inc(s_mask, 1)
            dve.wait_ge(s_cp, 16)
            dve.tensor_copy(k.src_int[:], k.src_col[:])

        @block.tensor
        def _(pe):
            pe.wait_ge(s_ident, 9)
            pe.wait_ge(s_dve, 1)
            for t in range(16):
                if t >= 2:
                    pe.wait_ge(s_cp, t - 1)
                pe.transpose(p_tr[t % 2][:], srcf[:, t * P:(t + 1) * P], k.ident[0:Q, 0:Q]).then_inc(s_tr, 1)
            pe.wait_ge(s_off, 1)
            pe.matmul(p_off[:], k.below[0:Q, 0:Q], rank[:, 2047:2048], start=True, stop=True).then_inc(s_tr, 1)


def setup_nodes(k):
    nc, NT, TN = k.nc, k.NT, k.TN
    ENDS = k.dram("run_ends", (1 + k.NP,))
    s_c1, s_in, s_id, s_idx, s_got, s_c2, s_dve, s_tr, s_st, s_mm, s_cp = (
        k.sem("sn_" + x) for x in "headed in id idx got counted dve tr starts mm cp".split())
    s_got = [s_got, k.sem("sn_got1")]
    with ExitStack() as c, nc.Block() as block:
        heads = k.sb(c, "heads", [P, NT])
        junk = k.sb(c, "junk", [P, NT])
        nid = k.sb(c, "node_id", [P, TN])
        c1, c2, rowf, ends = (k.sb(c, f"nd_{n}", [P, TN]) for n in range(4))
        rowi = k.sb(c, "row_i", [P, TN], I32)
        idx = [k.sb(c, f"ends_idx{b}", [P, 1], I32) for b in range(2)]
        got = [k.sb(c, f"ends_row{b}", [P, P]) for b in range(2)]
        junk2 = k.sb(c, "junk2", [P, P])
        endq, startq, flagq, preq, nq, t0, t1, zq = (k.sb(c, f"nq_{n}", [TN, P]) for n in range(8))
        offq = k.sb(c, "offq", [TN, 2])
        first = k.sb(c, "first_end", [1, 1])
        p_t = k.ps(c, "pn_t", [TN, P])
        p_o = k.ps(c, "pn_o", [TN, 2])
        p_b = [k.ps(c, f"pn_b{n}", [P, TN]) for n in range(3)]

        @block.gpsimd
        def _(pool):
            pool.iota(nid[:], pattern=[[P, TN]], base=0, channel_multiplier=1,
                      allow_small_or_imprecise_dtypes=True).then_inc(s_id, 1)
            pool.iota(nq[:], pattern=[[1, P]], base=0, channel_multiplier=P,
                      allow_small_or_imprecise_dtypes=True).then_inc(s_id, 1)
            pool.memset(first[:], 0.0).then_inc(s_id, 1)
            pool.memset(zq[:], 0.0).then_inc(s_id, 1)
            with pool.Fori(0, TN // 2) as i:
                for b in range(2):
                    pool.wait_ge(s_idx, i * 2 + (b + 1))
                    k.settle(pool)
                    pool.indirect_dma_start(out=got[b][:], out_offset=None, in_=k.DSTF,
                                            in_offset=bass.IndirectOffsetOnAxis(ap=idx[b][:], axis=0)
                                            ).then_inc(s_got[b], 16)

        @block.sync
        def _(sp):
            sp.dma_start(heads[:], k.HEADS.partition_broadcast(P)).then_inc(s_in, 16)
            sp.wait_ge(s_id, 4)
            sp.wait_ge(s_cp, 1)
            sp.dma_start(ENDS[1:].rearrange("(t p) -> t p", p=P), endq[:]).then_inc(s_st, 16)
            sp.dma_start(ENDS[0:1].unsqueeze(0), first[:]).then_inc(s_st, 16)
            sp.wait_ge(s_st, 32)
            sp.dma_start(startq[:], ENDS[0:k.NP].rearrange("(t p) -> t p", p=P)).then_inc(s_in, 16)

        @block.vector
        def _(dve):
            link = chain(dve, s_dve)
            dve.wait_ge(s_in, 16)
            dve.wait_ge(s_id, 4)
            with dve.Fori(0, TN) as i:
                dve.tensor_scalar(junk[:], heads[:], nid[:, ds(i, 1)], 0.0, ALU.is_le, ALU.add,
                                  accum_out=c1[:, ds(i, 1)]).then_inc(s_c1, 1)
                dve.wait_ge(s_c1, i + 1)
            link(dve.memset(junk2[:], 0.0))
            link(dve.tensor_scalar(rowf[:], c1[:], 1.0, 0.0, ALU.subtract, ALU.max))
            link(dve.tensor_copy(rowi[:], rowf[:]))
            dve.tensor_copy(idx[0][:], rowi[:, 0:1]).then_inc(s_idx, 1)
            dve.tensor_copy(idx[1][:], rowi[:, 1:2]).then_inc(s_idx, 1)

            def count(i, b):
                dve.wait_ge(s_got[b], (i + 1) * 16)
                dve.tensor_scalar(junk2[:], got[b][:], nid[:, ds(i * 2 + b, 1)], 0.0, ALU.is_le, ALU.add,
                                  accum_out=c2[:, ds(i * 2 + b, 1)]).then_inc(s_c2, 1)
            with dve.Fori(0, TN // 2 - 1) as i:
                for b in range(2):
                    count(i, b)
                    dve.wait_ge(s_c2, i * 2 + (b + 1))
                    dve.tensor_copy(idx[b][:], rowi[:, ds(i * 2 + (b + 2), 1)]).then_inc(s_idx, 1)
            count(TN // 2 - 1, 0)
            dve.wait_ge(s_c2, TN - 1)
            count(TN // 2 - 1, 1)
            dve.wait_ge(s_c2, TN)
            dve.scalar_tensor_tensor(out=ends[:], in0=rowf[:], scalar=float(P), in1=c2[:], op0=ALU.mult,
                                     op1=ALU.add).then_inc(s_mm, 1)
            dve.wait_ge(s_tr, 1)
            link(dve.tensor_copy(endq[:], p_t[:]))
            dve.sem_inc(s_cp, 1)
            dve.wait_ge(s_in, 32)
            link(dve.tensor_tensor(flagq[:], endq[:], startq[:], ALU.is_gt))
            dve.tensor_tensor_scan(out=preq[:], data0=flagq[:], data1=zq[:], initial=0.0, op0=ALU.add,
                                   op1=ALU.add).then_inc(s_mm, 1)
            dve.wait_ge(s_tr, 2)
            link(dve.tensor_copy(offq[:], p_o[:]))
            link(dve.tensor_scalar(preq[:], preq[:], offq[:, 0:1], None, ALU.add))
            link(dve.tensor_tensor(preq[:], preq[:], flagq[:], ALU.subtract))
            link(dve.tensor_tensor(t0[:], nq[:], preq[:], ALU.subtract))
            link(dve.tensor_scalar(t0[:], t0[:], offq[:, 1:2], None, ALU.add))
            link(dve.tensor_tensor(t1[:], preq[:], t0[:], ALU.subtract))
            link(dve.tensor_tensor(t1[:], t1[:], flagq[:], ALU.mult))
            link(dve.tensor_tensor(t0[:], t0[:], t1[:], ALU.add))
            dve.tensor_scalar(t1[:], endq[:], 1.0, 0.0, ALU.subtract, ALU.max).then_inc(s_mm, 1)
            dve.wait_ge(s_tr, 3)
            dve.tensor_copy(k.rank_of[:], p_b[0][:])
            dve.tensor_copy(k.last_of[:], p_b[1][:])
            dve.tensor_copy(k.has[:], p_b[2][:])

        @block.tensor
        def _(pe):
            pe.wait_ge(s_mm, 1)
            pe.transpose(p_t[:], ends[:], k.ident[:]).then_inc(s_tr, 1)
            pe.wait_ge(s_mm, 2)
            pe.matmul(p_o[:, 0:1], k.below[0:TN, 0:TN], preq[:, P - 1:P], start=True, stop=True)
            pe.matmul(p_o[:, 1:2], k.ones[0:TN, 0:TN], preq[:, P - 1:P], start=True, stop=True).then_inc(s_tr, 1)
            pe.wait_ge(s_mm, 3)
            pe.transpose(p_b[0][:], t0[:], k.ident[0:TN, 0:TN])
            pe.transpose(p_b[1][:], t1[:], k.ident[0:TN, 0:TN])
            pe.transpose(p_b[2][:], flagq[:], k.ident[0:TN, 0:TN]).then_inc(s_tr, 1)


def load_nodes(k, x):
    s_z, s_x = k.sem("x_zeroed"), k.sem("x_loaded")
    full, rest = k.N // P, k.N % P
    X3 = k.X[:].rearrange("p (t d) -> p t d", d=P)
    with k.nc.Block() as block:
        @block.vector
        def _(dve):
            dve.memset(k.X[:, full * P:], 0.0).then_inc(s_z, 1)

        @block.sync
        def _(sp):
            for t in range(0, full, 8):
                u = min(t + 8, full)
                sp.dma_start(X3[:, t:u, :], x[t * P:u * P].rearrange("(t p) d -> p t d", p=P)).then_inc(s_x, 16)
            sp.wait_ge(s_z, 1)
            if rest:
                sp.dma_start(X3[0:rest, full, :], x[full * P:, :]).then_inc(s_x, 16)
            sp.wait_ge(s_x, 16 * (-(-full // 8) + (rest > 0)))


class Norm:

    def __init__(self, k, c, tag, s_used):
        TN = k.TN
        self.s_used = s_used
        self.k = k
        self.st = k.sb(c, tag + "_stats", [P, TN * 6])
        self.mean, self.rstd, self.t0, self.t1 = (k.sb(c, f"{tag}_ln{n}", [P, TN]) for n in range(4))
        self.y = [k.sb(c, f"{tag}_y{b}", [P, NG]) for b in range(2)]
        self.hT = [k.sb(c, f"{tag}_hT{b}", [P, NG]) for b in range(2)]
        self.pT = [k.ps(c, f"{tag}_pT{b}", [P, NG]) for b in range(2)]
        self.s_dve, self.s_var, self.s_std, self.s_y, self.s_T, self.s_h = (
            k.sem(f"{tag}_{x}") for x in "chain variance deviation normalized transposed clipped".split())

    def statistics(self, dve):
        k = self.k
        link = chain(dve, self.s_dve)
        with dve.Fori(0, k.TN) as t:
            dve.bn_stats(self.st[:, ds(t * 6, 6)], k.X[:, ds(t * P, P)])
        link(dve.memset(self.t0[:], 0.0))
        s = self.st[:].rearrange("p (t s) -> p t s", s=6)
        dve.tensor_tensor(self.mean[:], s[:, :, 1], s[:, :, 4], ALU.add)
        link(dve.tensor_tensor(self.t0[:], s[:, :, 1], s[:, :, 4], ALU.subtract))
        link(dve.tensor_tensor(self.t1[:], s[:, :, 2], s[:, :, 5], ALU.add))
        link(dve.tensor_scalar(self.mean[:], self.mean[:], 0.5, None, ALU.mult))
        link(dve.tensor_tensor(self.t0[:], self.t0[:], self.t0[:], ALU.mult))
        link(dve.tensor_scalar(self.t1[:], self.t1[:], 1.0 / P, 1e-5, ALU.mult, ALU.add))
        dve.scalar_tensor_tensor(out=self.t1[:], in0=self.t0[:], scalar=0.25, in1=self.t1[:], op0=ALU.mult,
                                 op1=ALU.add).then_inc(self.s_var, 1)
        dve.wait_ge(self.s_std, 1)
        link(dve.reciprocal(self.rstd[:], self.t0[:]))

    def deviation(self, act):
        act.wait_ge(self.s_var, 1)
        act.activation(self.t0[:], self.t1[:], ACT.Sqrt).then_inc(self.s_std, 1)

    def normalize(self, dve, i, b, used=None):
        k = self.k
        if later(i):
            dve.wait_ge(used or self.s_T, nth(i, b, 2))
        for j in range(NPG):
            t = i * (2 * NPG) + (b * NPG + j)
            last = dve.tensor_scalar(self.y[b][:, j * P:(j + 1) * P], k.X[:, ds(t * P, P)],
                                     self.mean[:, ds(t, 1)], self.rstd[:, ds(t, 1)], ALU.subtract, ALU.mult)
        last.then_inc(self.s_y, 1)

    def transpose(self, pe, i, b):
        pe.wait_ge(self.s_y, nth(i, b))
        if later(i):
            pe.wait_ge(self.s_h, nth(i, b, 2))
        for j in range(NPG):
            last = pe.transpose(self.pT[b][:, j * P:(j + 1) * P], self.y[b][:, j * P:(j + 1) * P], self.k.ident[:])
        last.then_inc(self.s_T, 1)

    def clip(self, act, i, b):
        act.wait_ge(self.s_T, nth(i, b))
        if later(i):
            act.wait_ge(self.s_used, nth(i, b, 2))
        last = act.activation(self.hT[b][:], self.pT[b][:], ACT.Relu)
        if self.k.HT is None:
            last.then_inc(self.s_h, 1)
            return
        act.activation(self.k.HT[:, ds(i * (2 * NG) + b * NG, NG)], self.pT[b][:], ACT.Relu).then_inc(self.s_h, 1)


def pair_tables(k, tag, wa, wb, bias, plain, ranked):
    nc, n = k.nc, k.NSTEPS
    s_ld, s_R, s_A, s_B = (k.sem(f"{tag}_{x}") for x in "weights rows plain ranked".split())
    st = [k.sem(f"{tag}_stored{b}") for b in range(2)]
    sc = [k.sem(f"{tag}_scattered{b}") for b in range(2)]
    with ExitStack() as c, nc.Block() as block:
        m = Norm(k, c, tag, s_R)
        w = k.sb(c, tag + "_w", [P, 2 * P])
        bias_t = k.sb(c, tag + "_bias", [P, P])
        rowA = [k.sb(c, f"{tag}_A{b}", [P, NPG, P]) for b in range(2)]
        rowB = [k.sb(c, f"{tag}_B{b}", [P, NPG, P]) for b in range(2)]
        idx = [k.sb(c, f"{tag}_idx{b}", [P, NPG], I32) for b in range(2)]
        pA, pB = ([k.ps(c, f"{tag}_p{x}{b}", [P, NPG, P]) for b in range(2)] for x in "AB")

        @block.sync
        def _(sp):
            sp.dma_start(w[:, 0:P], wa).then_inc(s_ld, 16)
            sp.dma_start(w[:, P:], wb).then_inc(s_ld, 16)
            sp.dma_start(bias_t[:], bias.partition_broadcast(P)).then_inc(s_ld, 16)
            with sp.Fori(0, n) as i:
                for b in range(2):
                    sp.wait_ge(s_A, nth(i, b))
                    sp.dma_start(plain[ds(i * (2 * NG) + b * NG, NG), :].rearrange("(j p) d -> p j d", p=P),
                                 rowA[b][:]).then_inc(st[b], 16)
            for b in range(2):
                sp.wait_ge(st[b], 16 * n)

        @block.gpsimd
        def _(pool):
            with pool.Fori(0, n) as i:
                for b in range(2):
                    pool.wait_ge(s_B, nth(i, b))
                    k.settle(pool)
                    for j in range(NPG):
                        pool.indirect_dma_start(out=ranked, out_offset=bass.IndirectOffsetOnAxis(ap=idx[b][:, j:j + 1], axis=0),
                                                in_=rowB[b][:, j, :], in_offset=None).then_inc(sc[b], 16)
            for b in range(2):
                pool.wait_ge(sc[b], 16 * NPG * n)

        @block.vector
        def _(dve):
            m.statistics(dve)
            dve.wait_ge(s_ld, 48)

            def ranked_rows(i, b):
                dve.wait_ge(s_R, nth(i, b))
                if later(i):
                    dve.wait_ge(sc[b], i * (16 * NPG))
                dve.tensor_tensor(rowB[b][:], pB[b][:], bias_t[:].unsqueeze(1).to_broadcast([P, NPG, P]), ALU.add)
                dve.tensor_copy(idx[b][:], k.rank_of[:, ds(i * (2 * NPG) + b * NPG, NPG)]).then_inc(s_B, 1)

            def body(i):
                for b in range(2):
                    if back(i, b, 0, n):
                        m.normalize(dve, i, b)
                    if back(i, b, 1, n):
                        ranked_rows(*back(i, b, 1, n))
            pipelined(dve, n, body)

        @block.scalar
        def _(act):
            m.deviation(act)

            def plain_rows(i, b):
                act.wait_ge(s_R, nth(i, b))
                if later(i):
                    act.wait_ge(st[b], i * 16)
                act.copy(rowA[b][:], pA[b][:]).then_inc(s_A, 1)

            def body(i):
                for b in range(2):
                    if back(i, b, 0, n):
                        m.clip(act, i, b)
                    if back(i, b, 1, n):
                        plain_rows(*back(i, b, 1, n))
            pipelined(act, n, body)

        @block.tensor
        def _(pe):
            pe.wait_ge(s_ld, 48)

            def rows(i, b):
                pe.wait_ge(m.s_h, nth(i, b))
                if later(i):
                    pe.wait_ge(s_A, nth(i, b, 2))
                    pe.wait_ge(s_B, nth(i, b, 2))
                for j in range(NPG):
                    pe.matmul(pA[b][:, j, :], m.hT[b][:, j * P:(j + 1) * P], w[:, 0:P], start=True, stop=True)
                    last = pe.matmul(pB[b][:, j, :], m.hT[b][:, j * P:(j + 1) * P], w[:, P:], start=True, stop=True)
                last.then_inc(s_R, 1)

            def body(i):
                for b in range(2):
                    if back(i, b, 0, n):
                        m.transpose(pe, i, b)
                    if back(i, b, 1, n):
                        rows(*back(i, b, 1, n))
            pipelined(pe, n, body)


def layer0_edges(k, a, plain, out_rows):
    nc, n = k.nc, k.STEPS4
    (s_w, s_idx, s_oh, s_A, s_hid, s_B, s_scan, s_T, s_row) = (k.sem("e0_" + x) for x in
        "weights indices onehot summed hidden message scanned transposed rows".split())
    lw, gs, st = ([k.sem(f"e0_{x}{b}") for b in range(SLOTS)] for x in ("window", "gathered", "stored"))
    ld, ldn = ([k.sem(f"e0_{x}{h}") for h in range(SLOTS // 2)] for x in ("pair_loaded", "pair_masks"))
    DEEPEST = 8
    with ExitStack() as c, nc.Block() as block:
        w1w, w2 = k.sb(c, "e0_w1w", [1, P]), k.sb(c, "e0_w2", [P, P])
        two = lambda name, shape, dt=F32: [k.sb(c, f"e0_{name}{b}", shape, dt) for b in range(2)]
        four = lambda name, shape, dt=F32: [k.sb(c, f"e0_{name}{b}", shape, dt) for b in range(SLOTS)]
        new, rel, wrow = two("new", [P, 2 * G], BF16), two("rel", [P, 2 * G], BF16), two("wrow", [1, 2 * G])
        win, oh, got, idx = four("win", [P, TPG, P]), four("oh", [P, G]), four("got", [P, TPG, P]), four("idx", [P, TPG], I32)
        hid, scan, row = two("hid", [P, G]), two("scan", [P, G]), two("row", [P, TPG, P])
        pA, pB, pT = ([k.ps(c, f"e0_p{x}{b}", [P, G]) for b in range(2)] for x in "ABT")

        def load_windows(eng, i, b, tiles):
            if after(i, b, SLOTS):
                eng.wait_ge(s_A, nth4(i, b, SLOTS))
                k.settle(eng)
            for j in tiles:
                base = eng.value_load(k.base_row[0:1, ds(i * (SLOTS * TPG) + (b * TPG + j), 1)], min_val=0, max_val=k.NP)
                eng.dma_start(win[b][:, j, :], k.TB0[ds(base, P), :]).then_inc(lw[b], 16)

        @block.sync
        def _(sp):
            sp.dma_start(w1w[:], a["L0_gnn_W1"][2 * P:2 * P + 1, :]).then_inc(s_w, 16)
            sp.dma_start(w2[:], a["L0_gnn_W2"]).then_inc(s_w, 16)

            def load_pair(i, b):
                if b % 2:
                    return
                e = ds(i * (SLOTS * G) + b * G, 2 * G)
                if after(i, b, SLOTS):
                    sp.wait_ge(s_A, nth4(i, b + 1, SLOTS))
                    sp.wait_ge(s_oh, nth4(i, b + 1, SLOTS))
                    k.settle(sp)
                sp.dma_start(rel[b // 2][:], k.REL[e].partition_broadcast(P)).then_inc(ld[b // 2], 16)
                sp.dma_start(wrow[b // 2][:], k.EW[e].unsqueeze(0)).then_inc(ld[b // 2], 16)

            def load_masks(i, b):
                if b % 2:
                    return
                if after(i, b, SLOTS):
                    sp.wait_ge(s_scan, nth4(i, b + 1, SLOTS))
                    k.settle(sp)
                sp.dma_start(new[b // 2][:], k.NEW[ds(i * (SLOTS * G) + b * G, 2 * G)].partition_broadcast(P)).then_inc(ldn[b // 2], 16)

            def windows(i, b):
                load_windows(sp, i, b, (0, 1))

            def store(i, b):
                sp.wait_ge(s_row, nth4(i, b))
                sp.dma_start(out_rows[ds(i * (SLOTS * G) + b * G, G), :].rearrange("(j p) d -> p j d", p=P),
                             row[b % 2][:]).then_inc(st[b], 16)

            pipelined4(sp, n, ((store, 8), (load_masks, 2), (load_pair, 0), (windows, 0)), DEEPEST)
            for b in range(SLOTS):
                sp.wait_ge(st[b], 16 * n)

        @block.gpsimd
        def _(pool):
            def gather(i, b):
                pool.wait_ge(s_idx, nth4(i, b))
                if after(i, b, SLOTS):
                    pool.wait_ge(s_A, nth4(i, b, SLOTS))
                k.settle(pool)
                for j in range(TPG):
                    pool.indirect_dma_start(out=got[b][:, j, :], out_offset=None, in_=plain,
                                            in_offset=bass.IndirectOffsetOnAxis(ap=idx[b][:, j:j + 1], axis=0)
                                            ).then_inc(gs[b], 16)
            pipelined4(pool, n, ((gather, 0),), DEEPEST)

        @block.vector
        def _(dve):
            def indices(i, b):
                if after(i, b, SLOTS):
                    dve.wait_ge(gs[b], i * (16 * TPG))
                dve.tensor_copy(idx[b][:], k.src_int[:, ds(i * (SLOTS * TPG) + b * TPG, TPG)]).then_inc(s_idx, 1)

            def onehot(i, b):
                dve.wait_ge(ld[b // 2], (i + 1) * 32)
                if after(i, b, SLOTS):
                    dve.wait_ge(s_A, nth4(i, b, SLOTS))
                dve.tensor_scalar(oh[b][:], rel[b // 2][:, (b % 2) * G:(b % 2 + 1) * G], k.lane[:], None, ALU.is_equal).then_inc(s_oh, 1)

            def running_max(i, b):
                dve.wait_ge(s_B, nth4(i, b))
                dve.wait_ge(ldn[b // 2], i * 16 + 16)
                first = isinstance(i, int) and i == 0 and b == 0
                if after(i, b, 2):
                    dve.wait_ge(s_T, nth4(i, b, 2))
                if not first:
                    dve.wait_ge(s_scan, nth4(i, b, 1))
                dve.tensor_tensor_scan(out=scan[b % 2][:], data0=new[b // 2][:, (b % 2) * G:(b % 2 + 1) * G], data1=pB[b % 2][:], op0=ALU.add, op1=ALU.max,
                                       initial=BIG if first else scan[(b + 1) % 2][:, G - 1:G]).then_inc(s_scan, 1)

            pipelined4(dve, n, ((indices, 0), (running_max, 5), (onehot, 2)), DEEPEST)

        @block.scalar
        def _(act):
            def windows(i, b):
                load_windows(act, i, b, (2, 3))

            def hidden(i, b):
                act.wait_ge(s_A, nth4(i, b))
                if after(i, b, 2):
                    act.wait_ge(s_B, nth4(i, b, 2))
                act.activation(hid[b % 2][:], pA[b % 2][:], ACT.Relu).then_inc(s_hid, 1)

            def rows(i, b):
                act.wait_ge(s_T, nth4(i, b))
                if after(i, b, 2):
                    slot, times = uses(i, b, 2)
                    act.wait_ge(st[slot], times * 16)
                act.copy(row[b % 2][:].rearrange("p j d -> p (j d)"), pT[b % 2][:]).then_inc(s_row, 1)

            pipelined4(act, n, ((rows, 7), (hidden, 3), (windows, 0)), DEEPEST)

        @block.tensor
        def _(pe):
            pe.wait_ge(s_w, 32)

            def summed(i, b):
                pe.wait_ge(ld[b // 2], (i + 1) * 32)
                if after(i, b, 2):
                    pe.wait_ge(s_hid, nth4(i, b, 2))
                pe.matmul(pA[b % 2][:], w1w[:], wrow[b // 2][:, (b % 2) * G:(b % 2 + 1) * G], start=True, stop=False)
                pe.wait_ge(s_oh, nth4(i, b))
                pe.wait_ge(lw[b], (i + 1) * (16 * TPG))
                for j in range(TPG):
                    at = slice(j * P, (j + 1) * P)
                    pe.matmul(pA[b % 2][:, at], win[b][:, j, :], oh[b][:, at], start=False, stop=False)
                pe.wait_ge(gs[b], (i + 1) * (16 * TPG))
                for j in range(TPG):
                    at = slice(j * P, (j + 1) * P)
                    last = pe.matmul(pA[b % 2][:, at], got[b][:, j, :], k.ident[:], start=False, stop=(j == TPG - 1))
                last.then_inc(s_A, 1)

            def message(i, b):
                pe.wait_ge(s_hid, nth4(i, b))
                if after(i, b, 2):
                    pe.wait_ge(s_scan, nth4(i, b, 2))
                pe.matmul(pB[b % 2][:], w2[:], hid[b % 2][:], start=True, stop=True).then_inc(s_B, 1)

            def to_rows(i, b):
                pe.wait_ge(s_scan, nth4(i, b))
                if after(i, b, 2):
                    pe.wait_ge(s_row, nth4(i, b, 2))
                for j in range(TPG):
                    at = slice(j * P, (j + 1) * P)
                    last = pe.transpose(pT[b % 2][:, at], scan[b % 2][:, at], k.ident[:])
                last.then_inc(s_T, 1)

            pipelined4(pe, n, ((message, 4), (to_rows, 6), (summed, 3)), DEEPEST)


class SlotChain:

    def __init__(self, eng, sem, each, slots=2):
        self.eng, self.sem, self.each, self.slots = eng, sem, each, slots

    def __call__(self, instruction, i, b, nth_of_slot):
        instruction.then_inc(self.sem, 1)
        self.eng.wait_ge(self.sem, i * (self.slots * self.each) + (b * self.each + nth_of_slot))


def add_rows(k, tag, rows, width, each, setup, combine, project, bias, hidden=None, own_rows=None):
    nc, n = k.nc, k.NSTEPS
    (s_ld, s_idx, s_t, s_ag, s_T, s_c, s_u, s_hid, s_v, s_ch, s_b, s_own) = (k.sem(f"{tag}_{x}") for x in
        "weights indices temp combined transposed copied upper hidden projected chain bias own".split())
    gs = [k.sem(f"{tag}_gathered{b}") for b in range(2)]
    own_s = [k.sem(f"{tag}_ownrows{b}") for b in range(2)]
    with ExitStack() as c, nc.Block() as block:
        two = lambda name, shape, dt=F32: [k.sb(c, f"{tag}_{name}{b}", shape, dt) for b in range(2)]
        idx, got, ag, aT, t2 = two("idx", [P, NPG], I32), two("got", [P, NPG, width]), two("ag", [P, NPG, P]), two("aT", [P, NG]), two("t2", [P, NPG, P])
        own = two("own", [P, NPG, P]) if own_rows is not None else None
        wp, bias_t = k.sb(c, tag + "_wp", [P, P]), k.sb(c, tag + "_bias", [P, P])
        extra, loads = setup(c)
        loads = loads + [(bias_t[:], bias.partition_broadcast(P)), (wp[:], project)]
        if hidden:
            uh, ua, c1 = k.sb(c, tag + "_uh", [P, P]), k.sb(c, tag + "_ua", [P, P]), k.sb(c, tag + "_c1", [P, 1])
            uT = two("uT", [P, NG])
            loads += [(uh[:], hidden[0][0:P, :]), (ua[:], hidden[0][P:, :]), (c1[:], hidden[1].unsqueeze(1))]
            pU = [k.ps(c, f"{tag}_pU{b}", [P, NG]) for b in range(2)]
        pT = [k.ps(c, f"{tag}_pT{b}", [P, NG]) for b in range(2)]
        pV = [k.ps(c, f"{tag}_pV{b}", [P, NPG, P]) for b in range(2)]
        lag = 3 if hidden else 2
        seen, aT_read = (s_hid, s_u) if hidden else (s_c, s_v)

        @block.sync
        def _(sp):
            for to, of in loads:
                sp.dma_start(to, of).then_inc(s_ld, 16)
            if own_rows is not None:
                def load(i, b):
                    if later(i):
                        sp.wait_ge(s_ag, nth(i, b, 2))
                    sp.dma_start(own[b][:], own_rows[ds(i * (2 * NG) + b * NG, NG), :].rearrange("(j p) d -> p j d", p=P)
                                 ).then_inc(own_s[b], 16)

                def body(i):
                    for b in range(2):
                        if back(i, b, 0, n):
                            load(i, b)
                pipelined(sp, n, body, lag)
            sp.wait_ge(s_ld, 16 * len(loads))

        @block.gpsimd
        def _(pool):
            with pool.Fori(0, n) as i:
                for b in range(2):
                    pool.wait_ge(s_idx, nth(i, b))
                    k.settle(pool)
                    for j in range(NPG):
                        pool.indirect_dma_start(out=got[b][:, j, :], out_offset=None, in_=rows,
                                                in_offset=bass.IndirectOffsetOnAxis(ap=idx[b][:, j:j + 1], axis=0)
                                                ).then_inc(gs[b], 16)

        @block.vector
        def _(dve):
            slot_chain = SlotChain(dve, s_ch, each)
            dve.wait_ge(s_ld, 16 * len(loads))

            def indices(i, b):
                if later(i):
                    dve.wait_ge(gs[b], i * (16 * NPG))
                    dve.wait_ge(s_ag, nth(i, b, 2))
                dve.tensor_copy(idx[b][:], k.last_of[:, ds(i * (2 * NPG) + b * NPG, NPG)]).then_inc(s_idx, 1)

            def combined(i, b):
                dve.wait_ge(gs[b], (i + 1) * (16 * NPG))
                if own_rows is not None:
                    dve.wait_ge(own_s[b], i * 16 + 16)
                if later(i):
                    dve.wait_ge(s_T, nth(i, b, 2))
                combine(dve, extra, slot_chain, i, b, got[b], ag[b], own[b] if own else None).then_inc(s_ag, 1)

            def add(i, b):
                dve.wait_ge(s_v, nth(i, b))
                if later(i):
                    dve.wait_ge(s_b, nth(i, b, 2))
                dve.tensor_tensor(t2[b][:], pV[b][:], bias_t[:].unsqueeze(1).to_broadcast([P, NPG, P]), ALU.add).then_inc(s_t, 1)
                dve.wait_ge(s_t, nth(i, b))
                x = k.X[:, ds(i * (2 * NG) + b * NG, NG)]
                dve.tensor_tensor(x, x, t2[b][:].rearrange("p j d -> p (j d)"), ALU.add).then_inc(s_b, 1)

            def body(i):
                for b in range(2):
                    if back(i, b, 0, n):
                        indices(i, b)
                    if back(i, b, 1, n):
                        combined(*back(i, b, 1, n))
                    if back(i, b, lag + 1, n):
                        add(*back(i, b, lag + 1, n))
            pipelined(dve, n, body, lag + 1)

        @block.scalar
        def _(act):
            act.wait_ge(s_ld, 16 * len(loads))

            def copied(i, b):
                act.wait_ge(s_T, nth(i, b))
                if later(i):
                    act.wait_ge(aT_read, nth(i, b, 2))
                act.copy(aT[b][:], pT[b][:]).then_inc(s_c, 1)

            def hid(i, b):
                act.wait_ge(s_u, nth(i, b))
                if later(i):
                    act.wait_ge(s_v, nth(i, b, 2))
                act.activation(uT[b][:], pU[b][:], ACT.Relu, bias=c1[:]).then_inc(s_hid, 1)

            def body(i):
                for b in range(2):
                    if back(i, b, 1, n):
                        copied(*back(i, b, 1, n))
                    if hidden and back(i, b, 2, n):
                        hid(*back(i, b, 2, n))
            pipelined(act, n, body, lag + 1)

        @block.tensor
        def _(pe):
            pe.wait_ge(s_ld, 16 * len(loads))

            def transposed(i, b):
                pe.wait_ge(s_ag, nth(i, b))
                if later(i):
                    pe.wait_ge(s_c, nth(i, b, 2))
                for j in range(NPG):
                    last = pe.transpose(pT[b][:, j * P:(j + 1) * P], ag[b][:, j, :], k.ident[:])
                last.then_inc(s_T, 1)

            def upper(i, b):
                pe.wait_ge(s_c, nth(i, b))
                if later(i):
                    pe.wait_ge(s_hid, nth(i, b, 2))
                pe.matmul(pU[b][:], ua[:], aT[b][:], start=True, stop=False)
                pe.matmul(pU[b][:], uh[:], k.HT[:, ds(i * (2 * NG) + b * NG, NG)], start=False, stop=True).then_inc(s_u, 1)

            def projected(i, b):
                pe.wait_ge(seen, nth(i, b))
                if later(i):
                    pe.wait_ge(s_t, nth(i, b, 2))
                src = uT if hidden else aT
                for j in range(NPG):
                    last = pe.matmul(pV[b][:, j, :], src[b][:, j * P:(j + 1) * P], wp[:], start=True, stop=True)
                last.then_inc(s_v, 1)

            def body(i):
                for b in range(2):
                    if back(i, b, 1, n):
                        transposed(*back(i, b, 1, n))
                    if hidden and back(i, b, 2, n):
                        upper(*back(i, b, 2, n))
                    if back(i, b, lag, n):
                        projected(*back(i, b, lag, n))
            pipelined(pe, n, body, lag + 1)


def update0(k, a, rows):
    def setup(c):
        b2 = k.sb(c, "u0_b2", [P, P])
        tmp = [k.sb(c, f"u0_tmp{b}", [P, NPG, P]) for b in range(2)]
        return (b2, tmp), [(b2[:], a["L0_gnn_b2"].partition_broadcast(P))]

    def combine(dve, extra, link, i, b, got, ag, own):
        b2, tmp = extra
        link(dve.tensor_tensor(tmp[b][:], got[:], b2[:].unsqueeze(1).to_broadcast([P, NPG, P]), ALU.add), i, b, 1)
        t = i * (2 * NPG) + b * NPG
        return dve.tensor_tensor(ag[:], tmp[b][:], k.has[:, ds(t, NPG)].unsqueeze(2).to_broadcast([P, NPG, P]), ALU.mult)
    add_rows(k, "u0", rows, P, 1, setup, combine, a["L0_gnn_U2"], a["L0_gnn_c2"], hidden=(a["L0_gnn_U1"], a["L0_gnn_c1"]))


def normalize_only(k, tag, rows=None):
    nc, n = k.nc, k.NSTEPS
    s_r = k.sem(tag + "_rows")
    st = [k.sem(f"{tag}_stored{b}") for b in range(2)]
    with ExitStack() as c, nc.Block() as block:
        m = Norm(k, c, tag, None)
        h = [k.sb(c, f"{tag}_h{b}", [P, NG]) for b in range(2)]

        @block.sync
        def _(sp):
            if rows is None:
                return
            with sp.Fori(0, n) as i:
                for b in range(2):
                    sp.wait_ge(s_r, nth(i, b))
                    sp.dma_start(rows[ds(i * (2 * NG) + b * NG, NG), :].rearrange("(j p) d -> p j d", p=P),
                                 h[b][:].rearrange("p (j d) -> p j d", d=P)).then_inc(st[b], 16)
            for b in range(2):
                sp.wait_ge(st[b], 16 * n)

        @block.vector
        def _(dve):
            m.statistics(dve)

            def clipped(i, b):
                dve.wait_ge(m.s_y, nth(i, b))
                if later(i):
                    dve.wait_ge(st[b], i * 16)
                dve.tensor_scalar(h[b][:], m.y[b][:], 0.0, None, ALU.max).then_inc(s_r, 1)

            def body(i):
                for b in range(2):
                    if back(i, b, 0, n):
                        m.normalize(dve, i, b, s_r if rows is not None else m.s_T)
                        if rows is not None:
                            clipped(i, b)
            pipelined(dve, n, body)

        @block.scalar
        def _(act):
            m.deviation(act)
            if k.HT is None:
                return
            with act.Fori(0, n) as i:
                for b in range(2):
                    act.wait_ge(m.s_T, nth(i, b))
                    k.settle(act)
                    act.activation(k.HT[:, ds(i * (2 * NG) + b * NG, NG)], m.pT[b][:], ACT.Relu).then_inc(m.s_h, 1)

        @block.tensor
        def _(pe):
            if k.HT is None:
                return

            def body(i):
                for b in range(2):
                    if back(i, b, 0, n):
                        m.transpose(pe, i, b)
            pipelined(pe, n, body)


def layer1_tables(k, a):
    nc, n = k.nc, k.NSTEPS
    (s_ld, s_ch, s_var, s_std, s_one, s_xs, s_p, s_q, s_R, s_row, s_idx) = (k.sem("t1_" + x) for x in
        "weights chain variance deviation ones xn products squares rows done indices".split())
    sc = [k.sem(f"t1_scattered{b}") for b in range(2)]
    chunks = -(-k.N // 512)
    size = -(-k.N // chunks)
    cuts = [(at, min(at + size, k.N)) for at in range(0, k.N, size)]
    with ExitStack() as c, nc.Block() as block:
        two = lambda name, shape, dt=F32: [k.sb(c, f"t1_{name}{b}", shape, dt) for b in range(2)]
        k0, k1, k2 = (k.sb(c, f"t1_k{x}", [P, P]) for x in range(3))
        gamma, beta, dev, scale, shift, ms = (k.sb(c, "t1_" + x, [P, 1]) for x in "gamma beta dev scale shift ms".split())
        stats, agg = k.sb(c, "t1_stats", [P, len(cuts) * 6]), k.sb(c, "t1_agg", [P, 2])
        xs, q, row, idx = two("xs", [P, NG]), two("q", [P, 2, NG]), two("row", [P, NPG, W1COLS]), two("idx", [P, NPG], I32)
        pP = [k.ps(c, f"t1_pP{b}", [P, 2, NG]) for b in range(2)]
        pR = [k.ps(c, f"t1_pR{b}", [P, NG + 2 * NPG]) for b in range(2)]

        @block.sync
        def _(sp):
            for to, of in ((k0, a["L1_gnn_kernel"]), (k1, a["L1_gnn_kernel1"]), (k2, a["L1_gnn_kernel2"]),
                           (gamma, a["L1_gnn_gamma"].unsqueeze(1)), (beta, a["L1_gnn_beta"].unsqueeze(1))):
                sp.dma_start(to[:], of).then_inc(s_ld, 16)
            sp.wait_ge(s_ld, 80)

        @block.gpsimd
        def _(pool):
            with pool.Fori(0, n) as i:
                for b in range(2):
                    pool.wait_ge(s_row, nth(i, b))
                    pool.wait_ge(s_idx, nth(i, b))
                    k.settle(pool)
                    for j in range(NPG):
                        pool.indirect_dma_start(out=k.TB1, out_offset=bass.IndirectOffsetOnAxis(ap=idx[b][:, j:j + 1], axis=0),
                                                in_=row[b][:, j, :], in_offset=None).then_inc(sc[b], 16)
            for b in range(2):
                pool.wait_ge(sc[b], 16 * NPG * n)

        @block.vector
        def _(dve):
            link = chain(dve, s_ch)
            for b in range(2):
                dve.memset(row[b][:, :, P:P + 1], 1.0).then_inc(s_one, 1)
            for x, (at, to) in enumerate(cuts):
                last = dve.bn_stats(stats[:, x * 6:(x + 1) * 6], k.HT[:, at:to])
            link(last)
            link(dve.bn_aggr(agg[:], stats[:]))
            dve.tensor_scalar(dev[:], agg[:, 1:2], 1e-5, None, ALU.add).then_inc(s_var, 1)
            dve.wait_ge(s_std, 1)
            dve.wait_ge(s_ld, 80)
            link(dve.reciprocal(scale[:], shift[:]))
            link(dve.tensor_tensor(scale[:], scale[:], gamma[:], ALU.mult))
            link(dve.tensor_tensor(ms[:], agg[:, 0:1], scale[:], ALU.mult))
            link(dve.tensor_tensor(shift[:], beta[:], ms[:], ALU.subtract))

            def normed(i, b):
                if later(i):
                    dve.wait_ge(s_R, nth(i, b, 2))
                    dve.wait_ge(sc[b], i * (16 * NPG))
                dve.tensor_scalar(xs[b][:], k.HT[:, ds(i * (2 * NG) + b * NG, NG)], scale[:], shift[:], ALU.mult,
                                  ALU.add).then_inc(s_xs, 1)
                dve.tensor_copy(idx[b][:], k.rank_of[:, ds(i * (2 * NPG) + b * NPG, NPG)]).then_inc(s_idx, 1)

            def products(i, b):
                dve.wait_ge(s_p, nth(i, b))
                if later(i):
                    dve.wait_ge(s_R, nth(i, b, 2))
                dve.tensor_tensor(q[b][:], pP[b][:], xs[b][:].unsqueeze(1).to_broadcast([P, 2, NG]), ALU.mult).then_inc(s_q, 1)

            def body(i):
                for b in range(2):
                    if back(i, b, 0, n):
                        normed(i, b)
                    if back(i, b, 1, n):
                        products(*back(i, b, 1, n))
            pipelined(dve, n, body)

        @block.scalar
        def _(act):
            act.wait_ge(s_var, 1)
            act.activation(shift[:], dev[:], ACT.Sqrt).then_inc(s_std, 1)
            act.wait_ge(s_one, 2)

            def finish(i, b):
                act.wait_ge(s_R, nth(i, b))
                if later(i):
                    act.wait_ge(sc[b], i * (16 * NPG))
                act.copy(row[b][:, :, 0:P], pR[b][:, 0:NG].rearrange("p (j d) -> p j d", d=P))
                s = pR[b][:, NG:].rearrange("p (j w) -> p j w", w=2)
                act.activation(k.S1[:, ds(i * (2 * NPG) + b * NPG, NPG)], s[:, :, 0], ACT.Tanh)
                act.activation(row[b][:, :, P + 1], s[:, :, 1], ACT.Tanh).then_inc(s_row, 1)

            def body(i):
                for b in range(2):
                    if back(i, b, 1, n):
                        finish(*back(i, b, 1, n))
            pipelined(act, n, body)

        @block.tensor
        def _(pe):
            pe.wait_ge(s_ld, 80)

            def product(i, b):
                pe.wait_ge(s_xs, nth(i, b))
                if later(i):
                    pe.wait_ge(s_q, nth(i, b, 2))
                pe.matmul(pP[b][:, 0, :], k1[:], xs[b][:], start=True, stop=True)
                pe.matmul(pP[b][:, 1, :], k2[:], xs[b][:], start=True, stop=True).then_inc(s_p, 1)

            def rows(i, b):
                pe.wait_ge(s_q, nth(i, b))
                if later(i):
                    pe.wait_ge(s_row, nth(i, b, 2))
                for j in range(NPG):
                    at = slice(j * P, (j + 1) * P)
                    pe.matmul(pR[b][:, at], xs[b][:, at], k0[:], start=True, stop=True)
                    for w in range(2):
                        last = pe.matmul(pR[b][:, NG + 2 * j + w:NG + 2 * j + w + 1], q[b][:, w, at], k.ones[:, 0:1],
                                         start=True, stop=True)
                last.then_inc(s_R, 1)

            def body(i):
                for b in range(2):
                    if back(i, b, 0, n):
                        product(i, b)
                    if back(i, b, 1, n):
                        rows(*back(i, b, 1, n))
            pipelined(pe, n, body)


def layer1_edges(k):
    nc, n, TN = k.nc, k.STEPS4, k.TN
    (s_const, s_cch, s_oh, s_dup, s_to, s_ch, s_X, s_l, s_ee, s_mx, s_Y, s_py) = (k.sem("e1_" + x) for x in
        "constants const_chain onehots twins targets chain expanded leaky weight weighted joined copied".split())
    ld = [k.sem(f"e1_pair_loaded{h}") for h in range(SLOTS // 2)]
    lw = [k.sem(f"e1_windows{b}") for b in range(SLOTS)]
    sc = [[k.sem(f"e1_added{b}{j}") for j in range(TPG)] for b in range(SLOTS)]
    DEEPEST = 6
    H = TPG // 2
    with ExitStack() as c, nc.Block() as block:
        two = lambda name, shape, dt=F32: [k.sb(c, f"e1_{name}{b}", shape, dt) for b in range(2)]
        four = lambda name, shape, dt=F32: [k.sb(c, f"e1_{name}{b}", shape, dt) for b in range(SLOTS)]
        high_i = k.sb(c, "e1_high_int", [P, k.NT], I32)
        iota_t, high, away_all = k.sb(c, "e1_iota", [P, TN]), k.sb(c, "e1_high", [P, k.NT]), k.sb(c, "e1_away", [P, k.NT])
        rel, lrow, srow = two("rel", [P, 2 * G], BF16), two("lrow", [P, 2 * G], BF16), two("srow", [P, 2 * G])
        win, eq, py = four("win", [P, TPG, W1COLS]), four("eq", [P, TPG, P]), four("py", [P, TPG, W1COLS])
        oh, low, mx = two("oh", [P, G]), two("low", [P, G]), two("mx", [P, TPG, W1COLS])
        junk, unused = k.sb(c, "e1_junk", [P, TPG, P]), k.sb(c, "e1_unused", [P, TPG, TN])
        to = four("to", [P, TPG], I32)
        s1, u, l, ee, dup, away = (four(x, [P, TPG]) for x in "s1 u l ee dup away".split())
        pX = [[k.ps(c, f"e1_pX{b}{h}", [P, H, W1COLS + TN]) for h in range(2)] for b in range(2)]
        pY = [[k.ps(c, f"e1_pY{b}{h}", [P, H, W1COLS]) for h in range(2)] for b in range(2)]
        half = lambda t, h: t[:, h * H:(h + 1) * H]
        pair = lambda t, b: t[b // 2][:, (b % 2) * G:(b % 2 + 1) * G]

        def load_windows(eng, i, b, tiles):
            if after(i, b, SLOTS):
                eng.wait_ge(s_X, nth4(i, b, SLOTS))
                k.settle(eng)
            for j in tiles:
                base = eng.value_load(k.base_row[0:1, ds(i * (SLOTS * TPG) + (b * TPG + j), 1)], min_val=0, max_val=k.NP)
                eng.dma_start(win[b][:, j, :], k.TB1[ds(base, P), :]).then_inc(lw[b], 16)

        @block.sync
        def _(sp):
            def line_pair(i, b):
                if b % 2:
                    return
                e = ds(i * (SLOTS * G) + b * G, 2 * G)
                if after(i, b, SLOTS):
                    sp.wait_ge(s_dup, nth4(i, b + 1, SLOTS))
                    k.settle(sp)
                sp.dma_start(rel[b // 2][:], k.REL[e].partition_broadcast(P)).then_inc(ld[b // 2], 16)
                sp.dma_start(lrow[b // 2][:], k.LOW[e].partition_broadcast(P)).then_inc(ld[b // 2], 16)
                sp.dma_start(srow[b // 2][:], k.SRCF[e].partition_broadcast(P)).then_inc(ld[b // 2], 16)

            def windows(i, b):
                load_windows(sp, i, b, (0, 1))
            pipelined4(sp, n, ((line_pair, 0), (windows, 0)), DEEPEST)

        @block.gpsimd
        def _(pool):
            pool.iota(iota_t[:], pattern=[[1, TN]], base=0, channel_multiplier=0,
                      allow_small_or_imprecise_dtypes=True).then_inc(s_const, 1)

            def add(i, b):
                pool.wait_ge(s_to, nth4(i, b))
                pool.wait_ge(s_py, nth4(i, b))
                if after(i, b, 2):
                    slot, times = uses(i, b, 2)
                    for j in range(TPG):
                        pool.wait_ge(sc[slot][j], times * 16)
                k.settle(pool)
                for j in range(TPG):
                    pool.indirect_dma_start(out=k.ADD[(b % 2) * TPG + j],
                                            out_offset=bass.IndirectOffsetOnAxis(ap=to[b][:, j:j + 1], axis=0),
                                            in_=py[b][:, j, :], in_offset=None, compute_op=ALU.add).then_inc(sc[b][j], 16)
            pipelined4(pool, n, ((add, 6),), DEEPEST)
            for b in range(SLOTS):
                for j in range(TPG):
                    pool.wait_ge(sc[b][j], 16 * n)

        @block.vector
        def _(dve):
            fixed = chain(dve, s_cch)
            fixed(dve.tensor_scalar(high_i[:], k.src_int[:], P.bit_length() - 1, None, ALU.logical_shift_right))
            dve.tensor_copy(high[:], high_i[:])
            fixed(dve.tensor_scalar(away_all[:], k.src_col[:], -1.0, k.spare[:], ALU.mult, ALU.add))
            dve.wait_ge(s_const, 1)
            link = SlotChain(dve, s_ch, 3, SLOTS)

            def prepare(i, b):
                t = i * (SLOTS * TPG) + b * TPG
                dve.wait_ge(ld[b // 2], (i + 1) * 48)
                if after(i, b, 2):
                    dve.wait_ge(s_X, nth4(i, b, 2))
                dve.tensor_scalar(oh[b % 2][:], pair(rel, b), k.lane[:], None, ALU.is_equal)
                dve.tensor_scalar(low[b % 2][:], pair(lrow, b), k.lane[:], None, ALU.is_equal).then_inc(s_oh, 1)
                if after(i, b, SLOTS):
                    dve.wait_ge(s_Y, nth4(i, b, SLOTS))
                if after(i, b, 1):
                    dve.wait_ge(s_dup, nth4(i, b, 1))
                for j in range(TPG):
                    line = pair(srow, b)[:, j * P:(j + 1) * P]
                    dve.tensor_scalar(eq[b][:, j, :], line, k.src_col[:, ds(t + j, 1)], None, ALU.is_equal)
                    last = dve.scalar_tensor_tensor(out=junk[:, j, :], in0=line, scalar=k.src_col[:, ds(t + j, 1)], in1=k.above[:],
                                                    op0=ALU.is_equal, op1=ALU.mult, accum_out=dup[b][:, j:j + 1])
                last.then_inc(s_dup, 1)

            def targets(i, b):
                t = i * (SLOTS * TPG) + b * TPG
                dve.wait_ge(s_dup, nth4(i, b))
                link(dve.scalar_tensor_tensor(out=away[b][:], in0=dup[b][:], scalar=0.0, in1=away_all[:, ds(t, TPG)],
                                              op0=ALU.is_gt, op1=ALU.mult), i, b, 3)
                if after(i, b, SLOTS):
                    for j in range(TPG):
                        dve.wait_ge(sc[b][j], i * 16)
                dve.tensor_tensor(to[b][:], away[b][:], k.src_col[:, ds(t, TPG)], ALU.add).then_inc(s_to, 1)

            def scores(i, b):
                t = i * (SLOTS * TPG) + b * TPG
                dve.wait_ge(s_X, nth4(i, b))
                for j in range(TPG):
                    last = dve.scalar_tensor_tensor(out=unused[:, j, :], in0=iota_t[:], scalar=high[:, ds(t + j, 1)],
                                                    in1=pX[b % 2][j // H][:, j % H, W1COLS:], op0=ALU.is_equal, op1=ALU.mult,
                                                    accum_out=s1[b][:, j:j + 1])
                link(last, i, b, 1)
                for h in range(2):
                    last = dve.tensor_tensor(half(u[b], h), pX[b % 2][h][:, :, P + 1], half(s1[b], h), ALU.add)
                link(last, i, b, 2)
                if after(i, b, SLOTS):
                    dve.wait_ge(s_ee, nth4(i, b, SLOTS))
                dve.scalar_tensor_tensor(out=l[b][:], in0=u[b][:], scalar=0.01, in1=u[b][:], op0=ALU.mult,
                                         op1=ALU.max).then_inc(s_l, 1)

            def weigh(i, b):
                dve.wait_ge(s_ee, nth4(i, b))
                if after(i, b, 2):
                    dve.wait_ge(s_Y, nth4(i, b, 2))
                for h in range(2):
                    last = dve.tensor_tensor(half(mx[b % 2], h), pX[b % 2][h][:, :, 0:W1COLS],
                                             half(ee[b], h).unsqueeze(2).to_broadcast([P, H, W1COLS]), ALU.mult)
                last.then_inc(s_mx, 1)
            pipelined4(dve, n, ((scores, 4), (targets, 4), (prepare, 2), (weigh, 4)), DEEPEST)

        @block.scalar
        def _(act):
            def windows(i, b):
                load_windows(act, i, b, (2, 3))

            def weight(i, b):
                act.wait_ge(s_l, nth4(i, b))
                if after(i, b, SLOTS):
                    act.wait_ge(s_mx, nth4(i, b, SLOTS))
                act.activation(ee[b][:], l[b][:], ACT.Exp).then_inc(s_ee, 1)

            def rows(i, b):
                act.wait_ge(s_Y, nth4(i, b))
                if after(i, b, SLOTS):
                    for j in range(TPG):
                        act.wait_ge(sc[b][j], i * 16)
                for h in range(2):
                    last = act.copy(half(py[b], h), pY[b % 2][h][:])
                last.then_inc(s_py, 1)
            pipelined4(act, n, ((weight, 4), (rows, 5), (windows, 0)), DEEPEST)

        @block.tensor
        def _(pe):
            def expand(i, b):
                pe.wait_ge(s_oh, nth4(i, b))
                pe.wait_ge(lw[b], (i + 1) * (16 * TPG))
                if after(i, b, 2):
                    pe.wait_ge(s_mx, nth4(i, b, 2))
                for j in range(TPG):
                    at, bank = slice(j * P, (j + 1) * P), pX[b % 2][j // H]
                    pe.matmul(bank[:, j % H, 0:W1COLS], oh[b % 2][:, at], win[b][:, j, :], start=True, stop=True)
                    last = pe.matmul(bank[:, j % H, W1COLS:], low[b % 2][:, at], k.S1[:], start=True, stop=True)
                last.then_inc(s_X, 1)

            def join(i, b):
                pe.wait_ge(s_mx, nth4(i, b))
                if after(i, b, 2):
                    pe.wait_ge(s_py, nth4(i, b, 2))
                for j in range(TPG):
                    last = pe.matmul(pY[b % 2][j // H][:, j % H, :], eq[b][:, j, :], mx[b % 2][:, j, :], start=True, stop=True)
                last.then_inc(s_Y, 1)
            pipelined4(pe, n, ((join, 5), (expand, 3)), DEEPEST)


def update1(k):
    nc, n = k.nc, k.NSTEPS
    s_ch, s_sum, s_done = (k.sem("u1_" + x) for x in "chain summed done".split())
    ld = [k.sem(f"u1_loaded{b}") for b in range(2)]
    with ExitStack() as c, nc.Block() as block:
        two = lambda name, shape: [k.sb(c, f"u1_{name}{b}", shape) for b in range(2)]
        parts, total = two("parts", [P, ADDERS, NPG, W1COLS]), two("total", [P, NPG, W1COLS])
        den, rden, new = two("den", [P, NPG]), two("rden", [P, NPG]), two("new", [P, NPG, P])

        @block.sync
        def _(sp):
            def body(i):
                for b in range(2):
                    if not back(i, b, 0, n):
                        continue
                    if later(i):
                        sp.wait_ge(s_sum, nth(i, b, 2))
                    for t in range(ADDERS):
                        sp.dma_start(parts[b][:, t], k.ADD[t][ds(i * (2 * NG) + b * NG, NG), :].rearrange("(j p) d -> p j d", p=P)
                                     ).then_inc(ld[b], 16)
            pipelined(sp, n, body)

        @block.vector
        def _(dve):
            link = SlotChain(dve, s_ch, 3)

            def merge(i, b):
                dve.wait_ge(ld[b], (i + 1) * (16 * ADDERS))
                dve.tensor_reduce(total[b][:].rearrange("p j d -> p (j d)"), parts[b][:].rearrange("p t j d -> p (j d) t"), AX.X,
                                  ALU.add).then_inc(s_sum, 1)
                dve.wait_ge(s_sum, nth(i, b))
                link(dve.tensor_scalar(den[b][:], total[b][:, :, P], 1e-16, None, ALU.max), i, b, 1)
                link(dve.reciprocal(rden[b][:], den[b][:]), i, b, 2)
                for j in range(NPG):
                    last = dve.tensor_scalar(new[b][:, j, :], total[b][:, j, 0:P], rden[b][:, j:j + 1], 0.0, ALU.mult, ALU.max)
                link(last, i, b, 3)
                x = k.X[:, ds(i * (2 * NG) + b * NG, NG)]
                dve.tensor_tensor(x, x, new[b][:].rearrange("p j d -> p (j d)"), ALU.add).then_inc(s_done, 1)

            with dve.Fori(0, n) as i:
                for b in range(2):
                    merge(i, b)


def layer2_edges(k, a, plain, out_rows):
    nc, n = k.nc, k.STEPS4
    H, HV = 8, 16
    names = ("weights made wchain attrT attr_copied linear activated gated_mlp indices onehot summed weighted "
             "message alpha alpha_act gated score value maximum step_back shifted exponents pv running rows rowcopy").split()
    (s_ld, s_made, s_wch, s_At, s_atc, s_p12, s_t12, s_a12, s_idx, s_oh, s_M, s_mea, s_mT, s_al, s_x, s_z,
     s_S, s_V, s_scan, s_dr, s_d, s_e, s_pv, s_acc, s_T, s_row) = (k.sem("e2_" + x) for x in names)
    lda, ldr, lde, ldn = ([k.sem(f"e2_pair_{x}{h}") for h in range(SLOTS // 2)] for x in ("attr", "places", "weights", "masks"))
    ldw, gs, st = ([k.sem(f"e2_{x}{b}") for b in range(SLOTS)] for x in ("windows", "gathered", "stored"))
    DEEPEST = 11
    F = 64
    lo, hi = slice(0, F), slice(F, P)
    with ExitStack() as c, nc.Block() as block:
        two = lambda name, shape, dt=F32: [k.sb(c, f"e2_{name}{b}", shape, dt) for b in range(2)]
        one = lambda name, shape, dt=F32: k.sb(c, "e2_" + name, shape, dt)
        w1, w2, w3 = one("w1", [P, TPG, F]), one("w2", [P, F]), one("w3", [P, P])
        wa, wv, head = one("wa", [P, P]), one("wv", [P, P]), one("head", [P, P])
        pick = one("pick", [P, H])
        cols = one("cols", [P, 8])
        b12, b12h, b3, ba, bah, adot, adots = (cols[:, x:x + 1] for x in range(7))
        four = lambda name, shape, dt=F32: [k.sb(c, f"e2_{name}{b}", shape, dt) for b in range(SLOTS)]
        atT, a12 = two("atT", [P, P]), two("a12", [P, G])
        attr, rel = two("attr", [P, 2 * TPG, 32]), two("rel", [P, 2 * G], BF16)
        new, ea = two("new", [P, 2 * G], BF16), two("ea", [P, 2 * G])
        win, oh, got, idx = four("win", [P, TPG, P]), four("oh", [P, G]), four("got", [P, TPG, P]), four("idx", [P, TPG], I32)
        mT, z, top = four("mT", [P, G]), two("z", [P, G]), two("top", [P, 1 + G])
        acc, den, row = two("acc", [P, G]), two("den", [P, G]), two("row", [P, TPG, W2COLS])
        x12, t12, mea, xa, ta, d, dr, p, r, pv = (one(x, [P, G]) for x in "x12 t12 mea xa ta d dr p r pv".split())
        pM, pR, pS, pV, pA, pT, p12, pD = (k.ps(c, "e2_p" + x, [P, G]) for x in "M R S V A T 12 D".split())
        D3 = pD[:, P:P + TPG * H].rearrange("p (j h) -> p j h", h=H)

        def pair(t, b):
            return t[b // 2][:, (b % 2) * G:(b % 2 + 1) * G]

        @block.sync
        def _(sp):
            sep = a["L2_gnn_w_sep"].rearrange("c (h t v) -> t c h v", h=H, t=2)
            loads = [(w1[32 * j:32 * j + 32, j, :], a["L2_gnn_fc_w1"]) for j in range(TPG)]
            loads += [(w2[lo, :], a["L2_gnn_fc_w2"]), (w3[hi, :], a["L2_gnn_fc_w3"]),
                      (wa[:].rearrange("p (h v) -> p h v", h=H), sep[0]), (wv[:].rearrange("p (h v) -> p h v", h=H), sep[1]),
                      (b12[lo], a["L2_gnn_fc_b1"].unsqueeze(1)), (b12[hi], a["L2_gnn_fc_b2"].unsqueeze(1)),
                      (b3, a["L2_gnn_fc_b3"].unsqueeze(1)), (adot, a["L2_gnn_alpha_dot"].rearrange("o h v -> (h v) o"))]
            loads += [(ba[HV * h:HV * h + HV], a["L2_gnn_b_sep"][2 * HV * h:2 * HV * h + HV].unsqueeze(1)) for h in range(H)]
            sp.wait_ge(s_wch, 3)
            for to, of in loads:
                sp.dma_start(to, of).then_inc(s_ld, 16)
            sp.wait_ge(s_ld, 16 * len(loads))
            sp.sem_inc(s_made, 1)

            def attr_pair(i, b):
                if b % 2:
                    return
                e = ds(i * (SLOTS * G) + b * G, 2 * G)
                if after(i, b, SLOTS):
                    sp.wait_ge(s_At, nth4(i, b + 1, SLOTS))
                    k.settle(sp)
                sp.dma_start(attr[b // 2][:], k.EATT[e, :].rearrange("(j p) f -> p j f", p=P)).then_inc(lda[b // 2], 16)

            def line_pair(i, b, tile, table, used, loaded):
                if b % 2:
                    return
                if after(i, b, SLOTS):
                    sp.wait_ge(used, nth4(i, b + 1, SLOTS))
                    k.settle(sp)
                sp.dma_start(tile[b // 2][:], table[ds(i * (SLOTS * G) + b * G, 2 * G)].partition_broadcast(P)).then_inc(loaded[b // 2], 16)

            def place_pair(i, b):
                line_pair(i, b, rel, k.REL, s_oh, ldr)

            def weight_pair(i, b):
                line_pair(i, b, ea, k.EA, s_mea, lde)

            def mask_pair(i, b):
                line_pair(i, b, new, k.NEW, s_d, ldn)

            def windows(i, b):
                if after(i, b, SLOTS):
                    sp.wait_ge(s_M, nth4(i, b, SLOTS))
                    k.settle(sp)
                for j in range(TPG):
                    base = sp.value_load(k.base_row[0:1, ds(i * (SLOTS * TPG) + (b * TPG + j), 1)], min_val=0, max_val=k.NP)
                    sp.dma_start(win[b][:, j, :], k.TB2[ds(base, P), :]).then_inc(ldw[b], 16)

            def store(i, b):
                e = ds(i * (SLOTS * G) + b * G, G)
                sp.wait_ge(s_row, nth4(i, b))
                sp.dma_start(out_rows[e, :].rearrange("(j p) d -> p j d", p=P), row[b % 2][:]).then_inc(st[b], 16)

            pipelined4(sp, n, ((store, 11), (place_pair, 2), (windows, 3), (weight_pair, 4), (mask_pair, 7), (attr_pair, 0)), DEEPEST)
            for b in range(SLOTS):
                sp.wait_ge(st[b], 16 * n)

        @block.gpsimd
        def _(pool):
            h3 = head[:].rearrange("p (h v) -> p h v", h=H)
            pool.memset(head[:], 1.0).then_inc(s_wch, 1)
            pool.memset(pick[:], 0.0).then_inc(s_wch, 1)
            pool.memset(w1[:], 0.0).then_inc(s_wch, 1)
            pool.wait_ge(s_wch, 3)
            pool.affine_select(out=h3, in_=h3, compare_op=ALU.is_ge, fill=0.0, base=0, pattern=[[-HV, H], [0, HV]],
                               channel_multiplier=1).then_inc(s_wch, 1)
            pool.wait_ge(s_wch, 4)
            pool.affine_select(out=h3, in_=h3, compare_op=ALU.is_ge, fill=0.0, base=HV - 1, pattern=[[HV, H], [0, HV]],
                               channel_multiplier=-1).then_inc(s_wch, 1)
            pool.affine_select(out=pick[:], in_=pick[:], compare_op=ALU.not_equal, fill=1.0, base=0, pattern=[[-HV, H]],
                               channel_multiplier=1).then_inc(s_wch, 1)

            def gather(i, b):
                pool.wait_ge(s_idx, nth4(i, b))
                if after(i, b, SLOTS):
                    pool.wait_ge(s_M, nth4(i, b, SLOTS))
                k.settle(pool)
                for j in range(TPG):
                    pool.indirect_dma_start(out=got[b][:, j, :], out_offset=None, in_=plain,
                                            in_offset=bass.IndirectOffsetOnAxis(ap=idx[b][:, j:j + 1], axis=0)
                                            ).then_inc(gs[b], 16)

            pipelined4(pool, n, ((gather, 3),), DEEPEST)

        @block.vector
        def _(dve):
            for b in range(2):
                dve.memset(a12[b % 2][:], 0.0)
            dve.memset(w2[hi, :], 0.0)
            dve.memset(top[1][:, G:G + 1], BIG).then_inc(s_made, 1)
            dve.wait_ge(s_made, 2)
            dve.wait_ge(s_wch, 6)
            dve.tensor_scalar(w2[lo, :], w2[lo, :], 0.5, None, ALU.mult)
            dve.tensor_scalar(w3[hi, :], w3[hi, :], 0.5, None, ALU.mult)
            dve.tensor_scalar(b12h, b12, 0.5, None, ALU.mult)
            dve.tensor_scalar(bah, ba, 0.5, None, ALU.mult)
            dve.tensor_scalar(adots, adot, 0.4, None, ALU.mult).then_inc(s_made, 1)
            dve.wait_ge(s_made, 3)
            dve.tensor_scalar(head[:], head[:], adots, None, ALU.mult).then_inc(s_made, 1)

            def indices(i, b):
                if after(i, b, SLOTS):
                    dve.wait_ge(gs[b], i * (16 * TPG))
                dve.tensor_copy(idx[b][:], k.src_int[:, ds(i * (SLOTS * TPG) + b * TPG, TPG)]).then_inc(s_idx, 1)

            def mlp_gated(i, b):
                dve.wait_ge(s_t12, nth4(i, b))
                if after(i, b, 1):
                    dve.wait_ge(s_p12, nth4(i, b, 1))
                if after(i, b, 3):
                    dve.wait_ge(s_M, nth4(i, b, 3))
                dve.scalar_tensor_tensor(out=a12[b % 2][:], in0=t12[:], scalar=1.0, in1=x12[:], op0=ALU.add,
                                         op1=ALU.mult).then_inc(s_a12, 1)

            def onehot(i, b):
                dve.wait_ge(ldr[b // 2], (i + 1) * 16)
                if after(i, b, SLOTS):
                    dve.wait_ge(s_M, nth4(i, b, SLOTS))
                dve.tensor_scalar(oh[b][:], pair(rel, b), k.lane[:], None, ALU.is_equal).then_inc(s_oh, 1)

            def message(i, b):
                dve.wait_ge(s_M, nth4(i, b))
                dve.wait_ge(lde[b // 2], i * 16 + 16)
                if after(i, b, 1):
                    dve.wait_ge(s_mT, nth4(i, b, 1))
                dve.tensor_tensor(mea[:], pM[:], pair(ea, b), ALU.mult).then_inc(s_mea, 1)
                dve.wait_ge(s_mea, nth4(i, b))
                if after(i, b, SLOTS):
                    dve.wait_ge(s_V, nth4(i, b, SLOTS))
                dve.scalar_tensor_tensor(out=mT[b][:], in0=pR[:], scalar=b3, in1=mea[:], op0=ALU.add,
                                         op1=ALU.mult).then_inc(s_mT, 1)

            def gated(i, b):
                dve.wait_ge(s_x, nth4(i, b))
                if after(i, b, 2):
                    dve.wait_ge(s_S, nth4(i, b, 2))
                dve.scalar_tensor_tensor(out=z[b % 2][:], in0=ta[:], scalar=1.5, in1=xa[:], op0=ALU.add,
                                         op1=ALU.mult).then_inc(s_z, 1)

            def maxima(i, b):
                dve.wait_ge(s_S, nth4(i, b))
                dve.wait_ge(ldn[b // 2], i * 16 + 16)
                if after(i, b, 1):
                    dve.wait_ge(s_scan, nth4(i, b, 1))
                    dve.wait_ge(s_e, nth4(i, b, 1))
                before = top[(b + 1) % 2][:, G:G + 1]
                dve.tensor_copy(top[b % 2][:, 0:1], before)
                dve.tensor_tensor_scan(out=top[b % 2][:, 1:], data0=pair(new, b), data1=pS[:], op0=ALU.add, op1=ALU.max,
                                       initial=before).then_inc(s_scan, 1)
                dve.wait_ge(s_scan, nth4(i, b))
                dve.tensor_tensor(dr[:], top[b % 2][:, 0:G], top[b % 2][:, 1:], ALU.subtract).then_inc(s_dr, 1)
                dve.tensor_tensor(d[:], pS[:], top[b % 2][:, 1:], ALU.subtract)
                dve.wait_ge(s_dr, nth4(i, b))
                dve.tensor_tensor(dr[:], dr[:], pair(new, b), ALU.add).then_inc(s_d, 1)

            def sums(i, b):
                dve.wait_ge(s_e, nth4(i, b))
                dve.wait_ge(s_V, nth4(i, b))
                if after(i, b, 1):
                    dve.wait_ge(s_acc, nth4(i, b, 1))
                dve.tensor_tensor(pv[:], pV[:], p[:], ALU.mult).then_inc(s_pv, 1)
                if after(i, b, 2):
                    dve.wait_ge(s_T, nth4(i, b, 2))
                start = (lambda t: 0.0) if not after(i, b, 1) else (lambda t: t[(b + 1) % 2][:, G - 1:G])
                dve.tensor_tensor_scan(out=den[b % 2][:], data0=r[:], data1=p[:], op0=ALU.mult, op1=ALU.add, initial=start(den))
                dve.wait_ge(s_pv, nth4(i, b))
                dve.tensor_tensor_scan(out=acc[b % 2][:], data0=r[:], data1=pv[:], op0=ALU.mult, op1=ALU.add,
                                       initial=start(acc)).then_inc(s_acc, 1)

            pipelined4(dve, n, ((maxima, 9), (message, 6), (sums, 9), (gated, 7), (mlp_gated, 3, 1), (onehot, 4), (indices, 2)), DEEPEST)

        @block.scalar
        def _(act):
            act.wait_ge(s_made, 4)

            def attributes(i, b):
                act.wait_ge(s_At, nth4(i, b))
                if after(i, b, 2):
                    act.wait_ge(s_p12, nth4(i, b, 2))
                act.copy(atT[b % 2][:], pD[:, 0:P]).then_inc(s_atc, 1)

            def mlp_activated(i, b):
                act.wait_ge(s_p12, nth4(i, b))
                if after(i, b, 1):
                    act.wait_ge(s_a12, nth4(i, b, 1))
                act.activation(x12[:], p12[:], ACT.Identity, bias=b12[:])
                act.activation(t12[:], p12[:], ACT.Tanh, bias=b12h[:], scale=0.5).then_inc(s_t12, 1)

            def alphas(i, b):
                act.wait_ge(s_al, nth4(i, b))
                if after(i, b, 1):
                    act.wait_ge(s_z, nth4(i, b, 1))
                act.activation(xa[:], pA[:], ACT.Identity, bias=ba)
                act.activation(ta[:], pA[:], ACT.Tanh, bias=bah, scale=0.5).then_inc(s_x, 1)

            def exponents(i, b):
                act.wait_ge(s_d, nth4(i, b))
                if after(i, b, 1):
                    act.wait_ge(s_acc, nth4(i, b, 1))
                act.activation(p[:], d[:], ACT.Exp)
                act.activation(r[:], dr[:], ACT.Exp).then_inc(s_e, 1)

            def rows(i, b):
                act.wait_ge(s_T, nth4(i, b))
                if after(i, b, 2):
                    slot, times = uses(i, b, 2)
                    act.wait_ge(st[slot], times * 16)
                act.copy(row[b % 2][:, :, 0:P], pT[:].rearrange("p (j d) -> p j d", d=P))
                act.copy(row[b % 2][:, :, P:], D3).then_inc(s_row, 1)

            pipelined4(act, n, ((attributes, 3), (rows, 10), (alphas, 7), (exponents, 9), (mlp_activated, 3, 1)), DEEPEST)

        @block.tensor
        def _(pe):
            pe.wait_ge(s_made, 4)

            def attributes(i, b):
                pe.wait_ge(lda[b // 2], i * 16 + 16)
                if after(i, b, 1):
                    pe.wait_ge(s_atc, nth4(i, b, 1))
                if after(i, b, 8):
                    pe.wait_ge(s_row, nth4(i, b, 8))
                pe.transpose(pD[:, 0:P], attr[b // 2][:, (b % 2) * TPG:(b % 2 + 1) * TPG, :].rearrange("p j f -> p (j f)"), k.ident[:]).then_inc(s_At, 1)

            def mlp_linear(i, b):
                if after(i, b, 1):
                    pe.wait_ge(s_t12, nth4(i, b, 1))
                    pe.wait_ge(s_a12, nth4(i, b, 1))
                second = pe.matmul(p12[hi, :], w2[:], a12[(b + 1) % 2][:], start=True, stop=True)
                if isinstance(i, int) and i == n:
                    second.then_inc(s_p12, 1)
                    return
                pe.wait_ge(s_atc, nth4(i, b))
                for j in range(TPG):
                    last = pe.matmul(p12[lo, j * P:(j + 1) * P], w1[:, j, :], atT[b % 2][:], start=True, stop=True)
                last.then_inc(s_p12, 1)

            def summed(i, b):
                pe.wait_ge(ldw[b], (i + 1) * (16 * TPG))
                pe.wait_ge(s_oh, nth4(i, b))
                if after(i, b, 1):
                    pe.wait_ge(s_mT, nth4(i, b, 1))
                pe.wait_ge(gs[b], (i + 1) * (16 * TPG))
                for j in range(TPG):
                    at = slice(j * P, (j + 1) * P)
                    pe.matmul(pM[:, at], win[b][:, j, :], oh[b][:, at], start=True, stop=False)
                    pe.matmul(pM[:, at], got[b][:, j, :], k.ident[:], start=False, stop=True)
                pe.wait_ge(s_a12, nth4(i, b) + 1)
                pe.matmul(pR[:], w3[hi, :], a12[(b + 1) % 2][hi, :], start=True, stop=True).then_inc(s_M, 1)

            def alpha(i, b):
                pe.wait_ge(s_mT, nth4(i, b))
                if after(i, b, 1):
                    pe.wait_ge(s_x, nth4(i, b, 1))
                pe.matmul(pA[:], wa[:], mT[b][:], start=True, stop=True).then_inc(s_al, 1)

            def score(i, b):
                pe.wait_ge(s_z, nth4(i, b))
                if after(i, b, 1):
                    pe.wait_ge(s_d, nth4(i, b, 1))
                pe.matmul(pS[:], head[:], z[b % 2][:], start=True, stop=True).then_inc(s_S, 1)

            def value(i, b):
                if after(i, b, 1):
                    pe.wait_ge(s_pv, nth4(i, b, 1))
                pe.wait_ge(s_mT, nth4(i, b))
                pe.matmul(pV[:], wv[:], mT[b][:], start=True, stop=True).then_inc(s_V, 1)

            def to_rows(i, b):
                pe.wait_ge(s_acc, nth4(i, b))
                if after(i, b, 1):
                    pe.wait_ge(s_row, nth4(i, b, 1))
                newest = nth4(i, b) + 7
                pe.wait_ge(s_atc, min(newest, SLOTS * n) if isinstance(i, int) else newest)
                for j in range(TPG):
                    pe.transpose(pT[:, j * P:(j + 1) * P], acc[b % 2][:, j * P:(j + 1) * P], k.ident[:])
                    last = pe.matmul(D3[:, j, :], den[b % 2][:, j * P:(j + 1) * P], pick[:], start=True, stop=True)
                last.then_inc(s_T, 1)

            pipelined4(pe, n, ((to_rows, 10), (alpha, 7), (mlp_linear, 3, 1), (score, 8), (summed, 5), (value, 8), (attributes, 2)), DEEPEST)


def update2(k, a, rows):
    H, HV = 8, 16

    def setup(c):
        bv = k.sb(c, "u2_bv", [P, H, HV])
        rs, rc, rh = ([k.sb(c, f"u2_{x}{b}", [P, NPG, H]) for b in range(2)] for x in ("rs", "rc", "rh"))
        t = [k.sb(c, f"u2_t{b}", [P, NPG, H, HV]) for b in range(2)]
        return (bv, rs, rc, rh, t), [(bv[:], a["L2_gnn_b_sep"].rearrange("(h t v) -> t h v", h=H, t=2)[1].partition_broadcast(P))]

    def combine(dve, extra, link, i, b, got, ag, own):
        bv, rs, rc, rh, t = extra
        den = got[:, :, P:]
        link(dve.tensor_scalar(rs[b][:], den, 1e-16, None, ALU.add), i, b, 1)
        link(dve.reciprocal(rc[b][:], rs[b][:]), i, b, 2)
        link(dve.tensor_tensor(rh[b][:], rc[b][:], k.has[:, ds(i * (2 * NPG) + b * NPG, NPG)].unsqueeze(2).to_broadcast([P, NPG, H]),
                               ALU.mult), i, b, 3)
        for j in range(NPG):
            last = dve.tensor_tensor(t[b][:, j], bv[:], den[:, j, :].unsqueeze(2).to_broadcast([P, H, HV]), ALU.mult)
        link(last, i, b, 4)
        link(dve.tensor_tensor(t[b][:].rearrange("p j h v -> p j (h v)"), t[b][:].rearrange("p j h v -> p j (h v)"), got[:, :, 0:P],
                               ALU.add), i, b, 5)
        for j in range(NPG):
            last = dve.tensor_tensor(ag[:, j, :].rearrange("p (h v) -> p h v", h=H), t[b][:, j],
                                     rh[b][:, j, :].unsqueeze(2).to_broadcast([P, H, HV]), ALU.mult)
        return last
    add_rows(k, "u2", rows, W2COLS, 5, setup, combine, a["L2_gnn_w_proj"], a["L2_gnn_b_proj"])


def transpose_weight(k, w, to):
    s_l, s_p, s_c, s_o = (k.sem("w3_" + x) for x in "loaded transposed copied stored".split())
    with ExitStack() as c, k.nc.Block() as block:
        w_in, w_t, p_t = k.sb(c, "w3_in", [P, P]), k.sb(c, "w3_t", [P, P]), k.ps(c, "w3_p", [P, P])

        @block.sync
        def _(sp):
            sp.dma_start(w_in[:], w).then_inc(s_l, 16)
            sp.wait_ge(s_c, 1)
            sp.dma_start(to, w_t[:]).then_inc(s_o, 16)
            sp.wait_ge(s_o, 16)

        @block.tensor
        def _(pe):
            pe.wait_ge(s_l, 16)
            pe.transpose(p_t[:], w_in[:], k.ident[:]).then_inc(s_p, 1)

        @block.vector
        def _(dve):
            dve.wait_ge(s_p, 1)
            dve.tensor_copy(w_t[:], p_t[:]).then_inc(s_c, 1)


def layer3_edges(k, plain, out_rows):
    nc, n = k.nc, k.STEPS
    s_idx, s_C, s_scan, s_T, s_row = (k.sem("e3_" + x) for x in "indices columns scanned transposed rows".split())
    ld, gs, st = ([k.sem(f"e3_{x}{b}") for b in range(2)] for x in ("loaded", "gathered", "stored"))
    with ExitStack() as c, nc.Block() as block:
        two = lambda name, shape, dt=F32: [k.sb(c, f"e3_{name}{b}", shape, dt) for b in range(2)]
        keep, got, idx = two("keep", [P, G], BF16), two("got", [P, TPG, P]), two("idx", [P, TPG], I32)
        scan, row = two("scan", [P, G]), two("row", [P, TPG, P])
        pC, pT = ([k.ps(c, f"e3_p{x}{b}", [P, G]) for b in range(2)] for x in "CT")

        @block.sync
        def _(sp):
            def load(i, b):
                if later(i):
                    sp.wait_ge(s_scan, nth(i, b, 2))
                sp.dma_start(keep[b][:], k.KEEP[ds(i * (2 * G) + b * G, G)].partition_broadcast(P)).then_inc(ld[b], 16)

            def store(i, b):
                e = ds(i * (2 * G) + b * G, G)
                sp.wait_ge(s_row, nth(i, b))
                sp.dma_start(out_rows[e, :].rearrange("(j p) d -> p j d", p=P), row[b][:]).then_inc(st[b], 16)

            def body(i):
                for b in range(2):
                    if back(i, b, 0, n):
                        load(i, b)
                    if back(i, b, 3, n):
                        store(*back(i, b, 3, n))
            pipelined(sp, n, body, 3)
            for b in range(2):
                sp.wait_ge(st[b], 16 * n)

        @block.gpsimd
        def _(pool):
            def body(i):
                for b in range(2):
                    if not back(i, b, 0, n):
                        continue
                    pool.wait_ge(s_idx, nth(i, b))
                    if later(i):
                        pool.wait_ge(s_C, nth(i, b, 2))
                    k.settle(pool)
                    for j in range(TPG):
                        pool.indirect_dma_start(out=got[b][:, j, :], out_offset=None, in_=plain,
                                                in_offset=bass.IndirectOffsetOnAxis(ap=idx[b][:, j:j + 1], axis=0)
                                                ).then_inc(gs[b], 16)
            pipelined(pool, n, body, 3)

        @block.vector
        def _(dve):
            def indices(i, b):
                if later(i):
                    dve.wait_ge(gs[b], i * (16 * TPG))
                dve.tensor_copy(idx[b][:], k.src_int[:, ds(i * (2 * TPG) + b * TPG, TPG)]).then_inc(s_idx, 1)

            def running(i, b):
                first = isinstance(i, int) and i == 0 and b == 0
                dve.wait_ge(s_C, nth(i, b))
                dve.wait_ge(ld[b], i * 16 + 16)
                if later(i):
                    dve.wait_ge(s_T, nth(i, b, 2))
                if not first:
                    dve.wait_ge(s_scan, nth(i, b, 1))
                dve.tensor_tensor_scan(out=scan[b][:], data0=keep[b][:], data1=pC[b][:], op0=ALU.mult, op1=ALU.add,
                                       initial=0.0 if first else scan[1 - b][:, G - 1:G]).then_inc(s_scan, 1)

            def body(i):
                for b in range(2):
                    if back(i, b, 0, n):
                        indices(i, b)
                    if back(i, b, 2, n):
                        running(*back(i, b, 2, n))
            pipelined(dve, n, body, 3)

        @block.scalar
        def _(act):
            def rows(i, b):
                act.wait_ge(s_T, nth(i, b))
                if later(i):
                    act.wait_ge(st[b], i * 16)
                act.copy(row[b][:].rearrange("p j d -> p (j d)"), pT[b][:]).then_inc(s_row, 1)

            def body(i):
                for b in range(2):
                    if back(i, b, 3, n):
                        rows(*back(i, b, 3, n))
            pipelined(act, n, body, 3)

        @block.tensor
        def _(pe):
            def columns(i, b):
                pe.wait_ge(gs[b], (i + 1) * (16 * TPG))
                if later(i):
                    pe.wait_ge(s_scan, nth(i, b, 2))
                for j in range(TPG):
                    last = pe.transpose(pC[b][:, j * P:(j + 1) * P], got[b][:, j, :], k.ident[:])
                last.then_inc(s_C, 1)

            def to_rows(i, b):
                pe.wait_ge(s_scan, nth(i, b))
                if later(i):
                    pe.wait_ge(s_row, nth(i, b, 2))
                for j in range(TPG):
                    last = pe.transpose(pT[b][:, j * P:(j + 1) * P], scan[b][:, j * P:(j + 1) * P], k.ident[:])
                last.then_inc(s_T, 1)

            def body(i):
                for b in range(2):
                    if back(i, b, 1, n):
                        columns(*back(i, b, 1, n))
                    if back(i, b, 3, n):
                        to_rows(*back(i, b, 3, n))
            pipelined(pe, n, body, 3)


def update3(k, a, rows, own_rows, wt):
    def combine(dve, extra, link, i, b, got, ag, own):
        for j in range(NPG):
            last = dve.scalar_tensor_tensor(out=ag[:, j, :], in0=got[:, j, :], scalar=k.has[:, ds(i * (2 * NPG) + (b * NPG + j), 1)],
                                            in1=own[:, j, :], op0=ALU.mult, op1=ALU.add)
        return last
    add_rows(k, "u3", rows, P, 0, lambda c: (None, []), combine, wt, a["L3_gnn_b"], own_rows=own_rows)


def store_nodes(k, out):
    s_o = k.sem("x_stored")
    full, rest = k.N // P, k.N % P
    X3 = k.X[:].rearrange("p (t d) -> p t d", d=P)
    with k.nc.Block() as block:
        @block.sync
        def _(sp):
            sp.dma_start(out[0:full * P].rearrange("(t p) d -> p t d", p=P), X3[:, 0:full, :]).then_inc(s_o, 16)
            if rest:
                sp.dma_start(out[full * P:, :], X3[0:rest, full, :]).then_inc(s_o, 16)
            sp.wait_ge(s_o, 32 if rest else 16)


def gnn_program(nc, a, out):
    with ExitStack() as ctx:
        k = Kit(nc, ctx, a["x"].shape[0], a["src"].shape[0])
        k.constants(ctx)
        setup_edges(k, a)
        setup_nodes(k)
        k.X = k.sb(ctx, "X", [P, k.NP])
        k.S1 = k.sb(ctx, "s1_by_node", [P, k.TN])
        transposed = ctx.enter_context(ExitStack())
        k.HT = k.sb(transposed, "HT", [P, k.NP])
        load_nodes(k, a["x"])
        plain0, plain2, plain3 = (k.dram(f"by_node_{x}", (k.NP, P)) for x in (0, 2, 3))
        rows, rows2 = k.dram("edge_rows", (k.EP, P)), k.dram("edge_rows_2", (k.EP, W2COLS))
        wt = k.dram("w3_transposed", (P, P))
        pair_tables(k, "n0", a["L0_gnn_W1"][0:P, :], a["L0_gnn_W1"][P:2 * P, :], a["L0_gnn_b1"], plain0, k.TB0)
        layer0_edges(k, a, plain0, rows)
        update0(k, a, rows)
        k.release_semaphores()
        normalize_only(k, "n1")
        layer1_tables(k, a)
        transposed.close()
        k.HT = None
        layer1_edges(k)
        update1(k)
        k.release_semaphores()
        pair_tables(k, "n2", a["L2_gnn_w_src"], a["L2_gnn_w_dst"], a["L2_gnn_b_src"], plain2, k.TB2)
        layer2_edges(k, a, plain2, rows2)
        update2(k, a, rows2)
        transpose_weight(k, a["L3_gnn_W"], wt)
        normalize_only(k, "n3", plain3)
        layer3_edges(k, plain3, rows)
        update3(k, a, rows, plain3, wt)
        store_nodes(k, out)


_INS = ["x", "src", "dst", "edge_attr_32", "edge_weight", "edge_weight1", "L0_gnn_W1", "L0_gnn_b1", "L0_gnn_W2", "L0_gnn_b2",
        "L0_gnn_U1", "L0_gnn_c1", "L0_gnn_U2", "L0_gnn_c2", "L1_gnn_kernel", "L1_gnn_kernel1", "L1_gnn_kernel2", "L1_gnn_gamma",
        "L1_gnn_beta", "L2_gnn_w_src", "L2_gnn_b_src", "L2_gnn_w_dst", "L2_gnn_fc_w1", "L2_gnn_fc_b1", "L2_gnn_fc_w2",
        "L2_gnn_fc_b2", "L2_gnn_fc_w3", "L2_gnn_fc_b3", "L2_gnn_w_sep", "L2_gnn_b_sep", "L2_gnn_alpha_dot", "L2_gnn_w_proj",
        "L2_gnn_b_proj", "L3_gnn_W", "L3_gnn_b"]


def kernel(**inputs):
    import numpy as _np
    import concourse.bacc as _bacc
    from concourse import mybir as _mybir
    from concourse.bass_utils import run_bass_kernel_spmd as _run

    nc = _bacc.Bacc("TRN2", target_bir_lowering=False, num_devices=1)
    arrays, args = {}, {}
    for name in _INS:
        v = _np.ascontiguousarray(inputs[name])
        arrays[f"in_{name}_dram"] = v
        args[name] = nc.dram_tensor(f"in_{name}_dram", v.shape, _mybir.dt.from_np(v.dtype), kind="ExternalInput").ap()
    out = nc.dram_tensor("out_0_dram", arrays["in_x_dram"].shape, F32, kind="ExternalOutput").ap()
    gnn_program(nc, args, out)
    r = _run(nc, [arrays], core_ids=[0])
    return r.results[0]["out_0_dram"]
```

```python
from contextlib import ExitStack

import numpy as np
import concourse.bass as bass
from concourse import mybir

F32 = mybir.dt.float32
BF16 = mybir.dt.bfloat16
I32 = mybir.dt.int32
ALU = mybir.AluOpType
ACT = mybir.ActivationFunctionType
AX = mybir.AxisListType
ds = bass.ds

P = 128
TPG = 4
G = TPG * P
SLOTS = 4
NPG = 2
NG = NPG * P
ADDERS = TPG
W1COLS = P + 2
W2COLS = P + 8
BIG = -1.0e30


def later(i):
    return not isinstance(i, int) or i > 0


def back(i, b, d, n):
    at = i - (d - b + 1) // 2
    return None if isinstance(at, int) and not 0 <= at < n else (at, (b - d) % 2)


def nth(i, b, less=0):
    return i * 2 + (b + 1 - less)


def nth4(i, b, less=0):
    return i * SLOTS + (b + 1 - less)


def after(i, b, d):
    return not isinstance(i, int) or i * SLOTS + b >= d


def uses(i, b, d):
    steps = 1 - (d - b + SLOTS - 1) // SLOTS
    return (b - d) % SLOTS, i if steps == 0 else i + steps


def stages(i, n, lags):
    for b in range(SLOTS):
        for stage, lag, *past in lags:
            at, slot = i - (lag - b + SLOTS - 1) // SLOTS, (b - lag) % SLOTS
            if not isinstance(at, int) or (at >= 0 and at * SLOTS + slot < n * SLOTS + sum(past)):
                stage(at, slot)


def pipelined4(eng, n, lags, deepest, peel_last=False):
    extra = (deepest + SLOTS - 1) // SLOTS
    end = n - 1 if peel_last else n
    for i in range(min(end, extra + 1)):
        stages(i, n, lags)
    if end > extra + 1:
        with eng.Fori(extra + 1, end) as i:
            stages(i, n, lags)
    for i in range(end, n + extra):
        stages(i, n, lags)


def pipelined(eng, n, body, deepest=2):
    extra = (deepest + 1) // 2
    for i in range(min(n, extra + 1)):
        body(i)
    if n > extra + 1:
        with eng.Fori(extra + 1, n) as i:
            body(i)
    for i in range(n, n + extra):
        body(i)


class Kit:

    def __init__(self, nc, ctx, n, e):
        self.nc, self.ctx, self.N, self.E = nc, ctx, n, e
        self.held = []
        self.EP = -(-e // 2048) * 2048
        self.Q = self.EP // 2048
        self.NT = self.EP // P
        self.STEPS4 = self.EP // (SLOTS * G)
        self.STEPS = self.EP // (2 * G)
        self.NP = -(-(n + 1) // (SLOTS * NG)) * SLOTS * NG
        self.TN = self.NP // P
        self.NSTEPS = self.NP // (SLOTS * NG)

    def dram(self, name, shape, dt=F32):
        return self.nc.dram_tensor(name, shape, dt, kind="Internal").ap()

    def sb(self, ctx, name, shape, dt=F32):
        return ctx.enter_context(self.nc.sbuf_tensor(name, shape, dt))

    def ps(self, ctx, name, shape):
        t = ctx.enter_context(self.nc.psum_tensor(name, [P, 512], F32))
        t = t[0:shape[0], 0:int(np.prod(shape[1:]))]
        return t if len(shape) == 2 else t.rearrange("p (a b) -> p a b", a=shape[1])

    def sem(self, name):
        self.held.append(self.nc.alloc_semaphore(name=name))
        return self.held[-1]

    def release_semaphores(self):
        self.nc.all_engine_barrier()
        self.nc.clear_and_free_semaphores(self.held)
        self.nc.all_engine_barrier()
        self.held = []

    def constants(self, ctx):
        self.ident, self.below, self.ones = (self.sb(ctx, x, [P, P]) for x in ("ident", "below", "ones"))
        self.above = self.sb(ctx, "above", [P, P])
        self.lane, self.spare = self.sb(ctx, "lane", [P, 1]), self.sb(ctx, "spare", [P, 1])
        self.base_row = self.sb(ctx, "base_row", [1, self.NT], I32)
        self.src_col, self.src_int = self.sb(ctx, "src_col", [P, self.NT]), self.sb(ctx, "src_int", [P, self.NT], I32)
        self.rank_of, self.last_of = (self.sb(ctx, x, [P, self.TN], I32) for x in ("rank_of", "last_of"))
        self.has = self.sb(ctx, "has_edges", [P, self.TN])
        self.settled = ctx.enter_context(self.nc.semaphore("settled"))

    def settle(self, pool):
        pool.sem_inc(self.settled, 1)


def chain(eng, sem):
    count = [0]

    def link(instruction):
        count[0] += 1
        instruction.then_inc(sem, 1)
        eng.wait_ge(sem, count[0])
    return link


def setup_edges(k, a):
    nc, Q, N, E, EP, NT = k.nc, k.Q, k.N, k.E, k.EP, k.NT
    k.SRC, k.DST = k.dram("src_padded", (EP,), I32), k.dram("dst_padded", (1 + EP,), I32)
    k.SRCF, k.DSTF = k.dram("src_float", (EP,)), k.dram("dst_float", (NT, P))
    k.HEADS = k.dram("tile_heads", (NT,))
    k.KEEP, k.NEW = k.dram("same_run", (EP,), BF16), k.dram("new_run", (EP,), BF16)
    k.REL, k.BASE = k.dram("rank_in_window", (EP,), BF16), k.dram("window_base", (NT,), I32)
    k.LOW = k.dram("src_low", (EP,), BF16)
    k.EW, k.EA, k.EATT = k.dram("w0_padded", (EP,)), k.dram("w1_padded", (EP,)), k.dram("attr_tail", (2048, 32))
    k.ADD = [k.dram(f"added{t}", (k.NP + P, W1COLS)) for t in range(ADDERS)]
    k.TB0, k.TB1, k.TB2 = (k.dram(f"by_rank_{n}", (k.NP + P, w)) for n, w in enumerate((P, W1COLS, P)))
    s_fill, s_edge, s_in, s_f, s_dve, s_off, s_mask, s_out, s_tr, s_cp, s_head, s_ident = (
        k.sem("se_" + x) for x in "fill edge in float dve off mask out tr cp head ident".split())
    with ExitStack() as c, nc.Block() as block:
        pad = EP - E
        fill_i = k.sb(c, "fill_i", [1, pad + 1], I32)
        fill_0 = k.sb(c, "fill_0", [32, pad])
        cur, prv, srci = (k.sb(c, f"q_int{n}", [Q, 2048], I32) for n in range(3))
        curf, prvf, srcf, new, rank, nul = (k.sb(c, f"q_f{n}", [Q, 2048]) for n in range(6))
        keep_b, new_b, rel_b = (k.sb(c, f"q_b{n}", [Q, 2048], BF16) for n in range(3))
        low_i, low_b = k.sb(c, "q_low_int", [Q, 2048], I32), k.sb(c, "q_low", [Q, 2048], BF16)
        off = k.sb(c, "off", [Q, 1])
        base_f, heads = k.sb(c, "base_f", [Q, 16]), k.sb(c, "heads_q", [Q, 16])
        base_i = k.sb(c, "base_i", [Q, 16], I32)
        p_off = k.ps(c, "p_off", [Q, 1])
        p_tr = [k.ps(c, f"p_tr{n}", [P, Q]) for n in range(2)]

        @block.gpsimd
        def _(pool):
            pool.memset(fill_i[:, 0:pad], N).then_inc(s_fill, 1)
            pool.memset(fill_i[:, pad:pad + 1], -1).then_inc(s_fill, 1)
            pool.memset(fill_0[:], 0.0).then_inc(s_fill, 1)
            pool.memset(nul[:], 0.0).then_inc(s_fill, 1)
            pool.memset(k.ident[:], 0.0).then_inc(s_ident, 1)
            pool.memset(k.below[:], 1.0).then_inc(s_ident, 1)
            pool.memset(k.above[:], 1.0).then_inc(s_ident, 1)
            pool.memset(k.ones[:], 1.0).then_inc(s_ident, 1)
            pool.wait_ge(s_ident, 4)
            pool.affine_select(out=k.ident[:], in_=k.ident[:], compare_op=ALU.not_equal, fill=1.0,
                               base=0, pattern=[[-1, P]], channel_multiplier=1).then_inc(s_ident, 1)
            pool.affine_select(out=k.below[:], in_=k.below[:], compare_op=ALU.is_gt, fill=0.0,
                               base=0, pattern=[[1, P]], channel_multiplier=-1).then_inc(s_ident, 1)
            pool.affine_select(out=k.above[:], in_=k.above[:], compare_op=ALU.is_gt, fill=0.0,
                               base=0, pattern=[[-1, P]], channel_multiplier=1).then_inc(s_ident, 1)
            pool.iota(k.lane[:], pattern=[[0, 1]], base=0, channel_multiplier=1,
                      allow_small_or_imprecise_dtypes=True).then_inc(s_ident, 1)
            pool.iota(k.spare[:], pattern=[[0, 1]], base=k.NP, channel_multiplier=1,
                      allow_small_or_imprecise_dtypes=True).then_inc(s_ident, 1)

        @block.sync
        def _(sp):
            sp.dma_start(k.SRC[0:E], a["src"]).then_inc(s_edge, 16)
            sp.dma_start(k.DST[1:1 + E], a["dst"]).then_inc(s_edge, 16)
            sp.dma_start(k.EATT[0:2048 - pad], a["edge_attr_32"][EP - 2048:E]).then_inc(s_out, 16)
            sp.wait_ge(s_fill, 4)
            sp.dma_start(k.SRC[E:EP].unsqueeze(0), fill_i[:, 0:pad]).then_inc(s_edge, 16)
            sp.dma_start(k.DST[1 + E:].unsqueeze(0), fill_i[:, 0:pad]).then_inc(s_edge, 16)
            sp.dma_start(k.DST[0:1].unsqueeze(0), fill_i[:, pad:pad + 1]).then_inc(s_edge, 16)
            sp.dma_start(k.EW[E:].unsqueeze(0), fill_0[0:1, :]).then_inc(s_out, 16)
            sp.dma_start(k.EA[E:].unsqueeze(0), fill_0[0:1, :]).then_inc(s_out, 16)
            sp.dma_start(k.EATT[2048 - pad:].rearrange("e f -> (e f)").rearrange("(p c) -> p c", p=32), fill_0[:]).then_inc(s_out, 16)
            sp.wait_ge(s_edge, 80)
            sp.dma_start(cur[:], k.DST[1:].rearrange("(q c) -> q c", q=Q)).then_inc(s_in, 16)
            sp.dma_start(prv[:], k.DST[0:EP].rearrange("(q c) -> q c", q=Q)).then_inc(s_in, 16)
            sp.dma_start(srci[:], k.SRC.rearrange("(q c) -> q c", q=Q)).then_inc(s_in, 16)
            sp.dma_start(k.EW[0:E], a["edge_weight"]).then_inc(s_out, 16)
            sp.dma_start(k.EA[0:E], a["edge_weight1"].rearrange("e o -> (e o)")).then_inc(s_out, 16)
            sp.wait_ge(s_mask, 1)
            q2 = lambda t: t.rearrange("(q c) -> q c", q=Q)
            for to, of in ((q2(k.KEEP), keep_b), (q2(k.NEW), new_b), (q2(k.REL), rel_b), (q2(k.LOW), low_b), (q2(k.BASE), base_i),
                           (q2(k.SRCF), srcf), (k.DSTF.rearrange("(q t) p -> q (t p)", q=Q), curf)):
                sp.dma_start(to, of[:]).then_inc(s_out, 16)
            sp.dma_start(q2(k.HEADS), heads[:]).then_inc(s_head, 16)
            sp.wait_ge(s_head, 16)
            sp.wait_ge(s_out, 13 * 16)
            sp.dma_start(k.base_row[:], k.BASE.unsqueeze(0)).then_inc(s_in, 16)
            sp.wait_ge(s_in, 64)

        @block.scalar
        def _(act):
            for t in range(16):
                act.wait_ge(s_tr, t + 1)
                act.copy(k.src_col[:].rearrange("p (q t) -> p q t", t=16)[:, :, t], p_tr[t % 2][:]).then_inc(s_cp, 1)

        @block.vector
        def _(dve):
            link = chain(dve, s_dve)
            dve.wait_ge(s_in, 48)
            dve.tensor_copy(curf[:], cur[:])
            dve.tensor_copy(prvf[:], prv[:])
            dve.tensor_scalar(low_i[:], srci[:], P - 1, None, ALU.bitwise_and)
            link(dve.tensor_copy(srcf[:], srci[:]))
            dve.tensor_copy(low_b[:], low_i[:])
            dve.tensor_scalar(heads[:], curf[:].rearrange("q (t p) -> q t p", p=P)[:, :, 0], 1.0, None, ALU.mult)
            dve.tensor_tensor(keep_b[:], curf[:], prvf[:], ALU.is_equal)
            link(dve.tensor_tensor(new[:], curf[:], prvf[:], ALU.not_equal))
            dve.tensor_scalar(new_b[:], new[:], BIG, None, ALU.mult)
            dve.wait_ge(s_fill, 4)
            dve.tensor_tensor_scan(out=rank[:], data0=new[:], data1=nul[:], initial=0.0,
                                   op0=ALU.add, op1=ALU.add).then_inc(s_off, 1)
            dve.wait_ge(s_tr, 17)
            link(dve.tensor_scalar(off[:], p_off[:], 1.0, None, ALU.subtract))
            link(dve.tensor_scalar(rank[:], rank[:], off[:], None, ALU.add))
            r3 = rank[:].rearrange("q (t p) -> q t p", p=P)
            link(dve.tensor_scalar(base_f[:], r3[:, :, 0], 1.0, None, ALU.mult))
            dve.tensor_copy(base_i[:], base_f[:])
            dve.tensor_tensor(rel_b[:].rearrange("q (t p) -> q t p", p=P), r3,
                              base_f[:].unsqueeze(2).to_broadcast([Q, 16, P]), ALU.subtract).then_inc(s_mask, 1)
            dve.wait_ge(s_cp, 16)
            dve.tensor_copy(k.src_int[:], k.src_col[:])

        @block.tensor
        def _(pe):
            pe.wait_ge(s_ident, 9)
            pe.wait_ge(s_dve, 1)
            for t in range(16):
                if t >= 2:
                    pe.wait_ge(s_cp, t - 1)
                pe.transpose(p_tr[t % 2][:], srcf[:, t * P:(t + 1) * P], k.ident[0:Q, 0:Q]).then_inc(s_tr, 1)
            pe.wait_ge(s_off, 1)
            pe.matmul(p_off[:], k.below[0:Q, 0:Q], rank[:, 2047:2048], start=True, stop=True).then_inc(s_tr, 1)


def setup_nodes(k):
    nc, NT, TN = k.nc, k.NT, k.TN
    ENDS = k.dram("run_ends", (1 + k.NP,))
    s_c1, s_ac1, s_row, s_in, s_id, s_idx, s_c2, s_dve, s_tr, s_st, s_mm, s_cp, s_zero, s_nil = (
        k.sem("sn_" + x) for x in "headed headed_by_act row in id idx counted dve tr starts mm cp zeroed nil".split())
    s_got = [k.sem(f"sn_got{b}") for b in range(SLOTS)]
    n = TN // SLOTS
    with ExitStack() as c, nc.Block() as block:
        heads = k.sb(c, "heads", [P, NT])
        junk, junk_a = k.sb(c, "junk", [P, NT]), k.sb(c, "junk_a", [P, NT])
        nid_half = k.sb(c, "node_id_half", [P, TN])
        nid = k.sb(c, "node_id", [P, TN])
        c1, c2, rowf, ends = (k.sb(c, f"nd_{n}", [P, TN]) for n in range(4))
        idx = [k.sb(c, f"ends_idx{b}", [P, 1], I32) for b in range(SLOTS)]
        got = [k.sb(c, f"ends_row{b}", [P, P]) for b in range(SLOTS)]
        zero = k.sb(c, "zero", [P, 13 * W1COLS])
        junk2 = k.sb(c, "junk2", [P, P])
        endq, startq, flagq, preq, nq, t0, t1, zq = (k.sb(c, f"nq_{n}", [TN, P]) for n in range(8))
        offq = k.sb(c, "offq", [TN, 2])
        first = k.sb(c, "first_end", [1, 1])
        p_t = k.ps(c, "pn_t", [TN, P])
        p_o = k.ps(c, "pn_o", [TN, 2])
        p_b = [k.ps(c, f"pn_b{n}", [P, TN]) for n in range(3)]

        @block.gpsimd
        def _(pool):
            pool.memset(zero[:], 0.0).then_inc(s_nil, 1)
            pool.iota(nid[:], pattern=[[P, TN]], base=0, channel_multiplier=1,
                      allow_small_or_imprecise_dtypes=True).then_inc(s_id, 1)
            pool.iota(nq[:], pattern=[[1, P]], base=0, channel_multiplier=P,
                      allow_small_or_imprecise_dtypes=True).then_inc(s_id, 1)
            pool.memset(first[:], 0.0).then_inc(s_id, 1)
            pool.memset(zq[:], 0.0).then_inc(s_id, 1)
            with pool.Fori(0, n) as i:
                for b in range(SLOTS):
                    pool.wait_ge(s_idx, nth4(i, b))
                    k.settle(pool)
                    pool.indirect_dma_start(out=got[b][:], out_offset=None, in_=k.DSTF,
                                            in_offset=bass.IndirectOffsetOnAxis(ap=idx[b][:], axis=0)
                                            ).then_inc(s_got[b], 16)

        @block.scalar
        def _(act):
            act.wait_ge(s_nil, 1)
            rows, writes = (k.NP + P) // P, 0
            for t in range(ADDERS):
                flat = k.ADD[t].rearrange("(p a) d -> p (a d)", p=P)
                for r in range(0, rows, 13):
                    w = min(13, rows - r) * W1COLS
                    act.dma_start(flat[:, r * W1COLS:r * W1COLS + w], zero[:, 0:w]).then_inc(s_zero, 16)
                    writes += 1
            for t in (k.TB0, k.TB1, k.TB2):
                act.dma_start(t[k.NP:, :], zero[:, 0:t.shape[1]]).then_inc(s_zero, 16)
                writes += 1
            act.wait_ge(s_in, 16)
            act.wait_ge(s_mm, 1)
            with act.Fori(0, TN // 2) as i:
                act.activation(junk_a[:], heads[:], ACT.Sign, bias=nid_half[:, ds(i * 2 + 1, 1)], scale=-1.0,
                               accum_out=c1[:, ds(i * 2 + 1, 1)]).then_inc(s_ac1, 1)
                act.wait_ge(s_ac1, i + 1)
            act.wait_ge(s_zero, 16 * writes)

        @block.sync
        def _(sp):
            sp.dma_start(heads[:], k.HEADS.partition_broadcast(P)).then_inc(s_in, 16)
            sp.wait_ge(s_id, 4)
            sp.wait_ge(s_cp, 1)
            sp.dma_start(ENDS[1:].rearrange("(t p) -> t p", p=P), endq[:]).then_inc(s_st, 16)
            sp.dma_start(ENDS[0:1].unsqueeze(0), first[:]).then_inc(s_st, 16)
            sp.wait_ge(s_st, 32)
            sp.dma_start(startq[:], ENDS[0:k.NP].rearrange("(t p) -> t p", p=P)).then_inc(s_in, 16)

        @block.vector
        def _(dve):
            link = chain(dve, s_dve)
            dve.wait_ge(s_in, 16)
            dve.wait_ge(s_id, 4)
            dve.tensor_scalar(nid_half[:], nid[:], 0.5, None, ALU.add).then_inc(s_mm, 1)

            def tiles(i, b):
                t = ds(i * SLOTS + b, 1)
                if b % 2:
                    return
                if after(i, b, 2):
                    dve.wait_ge(s_c1, i * 2 + b // 2)
                dve.tensor_scalar(junk[:], heads[:], nid[:, t], 0.0, ALU.is_le, ALU.add, accum_out=c1[:, t]).then_inc(s_c1, 1)

            def row(i, b):
                t = ds(i * SLOTS + b, 1)
                if b % 2:
                    dve.wait_ge(s_ac1, i * 2 + (b // 2 + 1))
                    dve.tensor_scalar(rowf[:, t], c1[:, t], float(2 - NT), float(NT - 2), ALU.max, ALU.add).then_inc(s_row, 1)
                else:
                    dve.wait_ge(s_c1, i * 2 + (b // 2 + 1))
                    dve.tensor_scalar(rowf[:, t], c1[:, t], 1.0, 0.0, ALU.subtract, ALU.max).then_inc(s_row, 1)
                dve.wait_ge(s_row, nth4(i, b))
                if after(i, b, SLOTS):
                    dve.wait_ge(s_got[b], i * 16)
                    k.settle(dve)
                if b % 2:
                    dve.tensor_scalar(idx[b][:], rowf[:, t], 0.5, None, ALU.mult).then_inc(s_idx, 1)
                else:
                    dve.tensor_copy(idx[b][:], rowf[:, t]).then_inc(s_idx, 1)

            def count(i, b):
                t = ds(i * SLOTS + b, 1)
                dve.wait_ge(s_got[b], i * 16 + 16)
                if after(i, b, 1):
                    dve.wait_ge(s_c2, nth4(i, b, 1))
                dve.tensor_scalar(junk2[:], got[b][:], nid[:, t], 0.0, ALU.is_le, ALU.add, accum_out=c2[:, t]).then_inc(s_c2, 1)
            pipelined4(dve, n, ((count, 3), (tiles, 0), (row, 0)), 3)
            dve.wait_ge(s_c2, TN)
            columns = lambda t, odd: t[:].rearrange("p (t two) -> p t two", two=2)[:, :, odd]
            for odd in range(2):
                last = dve.scalar_tensor_tensor(out=columns(ends, odd), in0=columns(rowf, odd), scalar=float(P // (1 + odd)),
                                                in1=columns(c2, odd), op0=ALU.mult, op1=ALU.add)
            last.then_inc(s_mm, 1)
            dve.wait_ge(s_tr, 1)
            link(dve.tensor_copy(endq[:], p_t[:]))
            dve.sem_inc(s_cp, 1)
            dve.wait_ge(s_in, 32)
            link(dve.tensor_tensor(flagq[:], endq[:], startq[:], ALU.is_gt))
            dve.tensor_tensor_scan(out=preq[:], data0=flagq[:], data1=zq[:], initial=0.0, op0=ALU.add,
                                   op1=ALU.add).then_inc(s_mm, 1)
            dve.wait_ge(s_tr, 2)
            link(dve.tensor_copy(offq[:], p_o[:]))
            link(dve.tensor_scalar(preq[:], preq[:], offq[:, 0:1], None, ALU.add))
            link(dve.tensor_tensor(preq[:], preq[:], flagq[:], ALU.subtract))
            link(dve.tensor_tensor(t0[:], nq[:], preq[:], ALU.subtract))
            link(dve.tensor_scalar(t0[:], t0[:], offq[:, 1:2], None, ALU.add))
            link(dve.tensor_tensor(t1[:], preq[:], t0[:], ALU.subtract))
            link(dve.tensor_tensor(t1[:], t1[:], flagq[:], ALU.mult))
            link(dve.tensor_tensor(t0[:], t0[:], t1[:], ALU.add))
            dve.tensor_scalar(t1[:], endq[:], 1.0, 0.0, ALU.subtract, ALU.max).then_inc(s_mm, 1)
            dve.wait_ge(s_tr, 3)
            dve.tensor_copy(k.rank_of[:], p_b[0][:])
            dve.tensor_copy(k.last_of[:], p_b[1][:])
            dve.tensor_copy(k.has[:], p_b[2][:])

        @block.tensor
        def _(pe):
            pe.wait_ge(s_mm, 2)
            pe.transpose(p_t[:], ends[:], k.ident[:]).then_inc(s_tr, 1)
            pe.wait_ge(s_mm, 3)
            pe.matmul(p_o[:, 0:1], k.below[0:TN, 0:TN], preq[:, P - 1:P], start=True, stop=True)
            pe.matmul(p_o[:, 1:2], k.ones[0:TN, 0:TN], preq[:, P - 1:P], start=True, stop=True).then_inc(s_tr, 1)
            pe.wait_ge(s_mm, 4)
            pe.transpose(p_b[0][:], t0[:], k.ident[0:TN, 0:TN])
            pe.transpose(p_b[1][:], t1[:], k.ident[0:TN, 0:TN])
            pe.transpose(p_b[2][:], flagq[:], k.ident[0:TN, 0:TN]).then_inc(s_tr, 1)


def load_nodes(k, x):
    s_z, s_x = k.sem("x_zeroed"), k.sem("x_loaded")
    full, rest = k.N // P, k.N % P
    X3 = k.X[:].rearrange("p (t d) -> p t d", d=P)
    with k.nc.Block() as block:
        @block.vector
        def _(dve):
            dve.memset(k.X[:, full * P:], 0.0).then_inc(s_z, 1)

        @block.sync
        def _(sp):
            for t in range(0, full, 8):
                u = min(t + 8, full)
                sp.dma_start(X3[:, t:u, :], x[t * P:u * P].rearrange("(t p) d -> p t d", p=P)).then_inc(s_x, 16)
            sp.wait_ge(s_z, 1)
            if rest:
                sp.dma_start(X3[0:rest, full, :], x[full * P:, :]).then_inc(s_x, 16)
            sp.wait_ge(s_x, 16 * (-(-full // 8) + (rest > 0)))


class Norm:

    def __init__(self, k, c, tag, s_used):
        TN = k.TN
        self.s_used = s_used
        self.k = k
        self.st = k.sb(c, tag + "_stats", [P, TN * 6])
        self.mean, self.rstd, self.t0, self.t1 = (k.sb(c, f"{tag}_ln{n}", [P, TN]) for n in range(4))
        self.y = [k.sb(c, f"{tag}_y{b}", [P, NG]) for b in range(SLOTS)]
        self.hT = [k.sb(c, f"{tag}_hT{b}", [P, NG]) for b in range(SLOTS)]
        self.pT = [k.ps(c, f"{tag}_pT{b}", [P, NG]) for b in range(2)]
        self.s_dve, self.s_var, self.s_std, self.s_y, self.s_T, self.s_h = (
            k.sem(f"{tag}_{x}") for x in "chain variance deviation normalized transposed clipped".split())

    def statistics(self, dve):
        k = self.k
        link = chain(dve, self.s_dve)
        with dve.Fori(0, k.TN) as t:
            dve.bn_stats(self.st[:, ds(t * 6, 6)], k.X[:, ds(t * P, P)])
        link(dve.memset(self.t0[:], 0.0))
        s = self.st[:].rearrange("p (t s) -> p t s", s=6)
        dve.tensor_tensor(self.mean[:], s[:, :, 1], s[:, :, 4], ALU.add)
        link(dve.tensor_tensor(self.t0[:], s[:, :, 1], s[:, :, 4], ALU.subtract))
        link(dve.tensor_tensor(self.t1[:], s[:, :, 2], s[:, :, 5], ALU.add))
        link(dve.tensor_scalar(self.mean[:], self.mean[:], 0.5, None, ALU.mult))
        link(dve.tensor_tensor(self.t0[:], self.t0[:], self.t0[:], ALU.mult))
        link(dve.tensor_scalar(self.t1[:], self.t1[:], 1.0 / P, 1e-5, ALU.mult, ALU.add))
        dve.scalar_tensor_tensor(out=self.t1[:], in0=self.t0[:], scalar=0.25, in1=self.t1[:], op0=ALU.mult,
                                 op1=ALU.add).then_inc(self.s_var, 1)
        dve.wait_ge(self.s_std, 1)
        link(dve.reciprocal(self.rstd[:], self.t0[:]))

    def deviation(self, act):
        act.wait_ge(self.s_var, 1)
        act.activation(self.t0[:], self.t1[:], ACT.Sqrt).then_inc(self.s_std, 1)

    def normalize(self, dve, i, b, used=None):
        k = self.k
        if after(i, b, SLOTS):
            dve.wait_ge(used or self.s_T, nth4(i, b, SLOTS))
        for j in range(NPG):
            t = i * (SLOTS * NPG) + (b * NPG + j)
            last = dve.tensor_scalar(self.y[b][:, j * P:(j + 1) * P], k.X[:, ds(t * P, P)],
                                     self.mean[:, ds(t, 1)], self.rstd[:, ds(t, 1)], ALU.subtract, ALU.mult)
        last.then_inc(self.s_y, 1)

    def transpose(self, pe, i, b):
        pe.wait_ge(self.s_y, nth4(i, b))
        if after(i, b, 2):
            pe.wait_ge(self.s_h, nth4(i, b, 2))
        for j in range(NPG):
            last = pe.transpose(self.pT[b % 2][:, j * P:(j + 1) * P], self.y[b][:, j * P:(j + 1) * P], self.k.ident[:])
        last.then_inc(self.s_T, 1)

    def clip(self, act, i, b):
        act.wait_ge(self.s_T, nth4(i, b))
        if after(i, b, SLOTS):
            act.wait_ge(self.s_used, nth4(i, b, SLOTS))
        last = act.activation(self.hT[b][:], self.pT[b % 2][:], ACT.Relu)
        if self.k.HT is None:
            last.then_inc(self.s_h, 1)
            return
        act.activation(self.k.HT[:, ds(i * (SLOTS * NG) + b * NG, NG)], self.pT[b % 2][:], ACT.Relu).then_inc(self.s_h, 1)


def pair_tables(k, tag, wa, wb, bias, plain, ranked):
    nc, n = k.nc, k.NSTEPS
    s_ld, s_R, s_A, s_B = (k.sem(f"{tag}_{x}") for x in "weights rows plain ranked".split())
    st = [k.sem(f"{tag}_stored{b}") for b in range(SLOTS)]
    sc = [k.sem(f"{tag}_scattered{b}") for b in range(SLOTS)]
    with ExitStack() as c, nc.Block() as block:
        m = Norm(k, c, tag, s_R)
        w = k.sb(c, tag + "_w", [P, 2 * P])
        bias_t = k.sb(c, tag + "_bias", [P, P])
        rowA = [k.sb(c, f"{tag}_A{b}", [P, NPG, P]) for b in range(SLOTS)]
        rowB = [k.sb(c, f"{tag}_B{b}", [P, NPG, P]) for b in range(SLOTS)]
        idx = [k.sb(c, f"{tag}_idx{b}", [P, NPG], I32) for b in range(SLOTS)]
        pA, pB = ([k.ps(c, f"{tag}_p{x}{b}", [P, NPG, P]) for b in range(2)] for x in "AB")

        @block.sync
        def _(sp):
            sp.dma_start(w[:, 0:P], wa).then_inc(s_ld, 16)
            sp.dma_start(w[:, P:], wb).then_inc(s_ld, 16)
            sp.dma_start(bias_t[:], bias.partition_broadcast(P)).then_inc(s_ld, 16)
            with sp.Fori(0, n) as i:
                for b in range(SLOTS):
                    sp.wait_ge(s_A, nth4(i, b))
                    sp.dma_start(plain[ds(i * (SLOTS * NG) + b * NG, NG), :].rearrange("(j p) d -> p j d", p=P),
                                 rowA[b][:]).then_inc(st[b], 16)
            for b in range(SLOTS):
                sp.wait_ge(st[b], 16 * n)

        @block.gpsimd
        def _(pool):
            with pool.Fori(0, n) as i:
                for b in range(SLOTS):
                    pool.wait_ge(s_B, nth4(i, b))
                    k.settle(pool)
                    for j in range(NPG):
                        pool.indirect_dma_start(out=ranked, out_offset=bass.IndirectOffsetOnAxis(ap=idx[b][:, j:j + 1], axis=0),
                                                in_=rowB[b][:, j, :], in_offset=None).then_inc(sc[b], 16)
            for b in range(SLOTS):
                pool.wait_ge(sc[b], 16 * NPG * n)

        @block.vector
        def _(dve):
            m.statistics(dve)
            dve.wait_ge(s_ld, 48)

            def ranked_rows(i, b):
                dve.wait_ge(s_R, nth4(i, b))
                if after(i, b, SLOTS):
                    dve.wait_ge(sc[b], i * (16 * NPG))
                dve.tensor_tensor(rowB[b][:], pB[b % 2][:], bias_t[:].unsqueeze(1).to_broadcast([P, NPG, P]), ALU.add)
                dve.tensor_copy(idx[b][:], k.rank_of[:, ds(i * (SLOTS * NPG) + b * NPG, NPG)]).then_inc(s_B, 1)

            pipelined4(dve, n, ((lambda i, b: m.normalize(dve, i, b), 0), (ranked_rows, 3)), 3)

        @block.scalar
        def _(act):
            m.deviation(act)

            def plain_rows(i, b):
                act.wait_ge(s_R, nth4(i, b))
                if after(i, b, SLOTS):
                    act.wait_ge(st[b], i * 16)
                act.copy(rowA[b][:], pA[b % 2][:]).then_inc(s_A, 1)

            pipelined4(act, n, ((plain_rows, 3), (lambda i, b: m.clip(act, i, b), 1)), 3)

        @block.tensor
        def _(pe):
            pe.wait_ge(s_ld, 48)

            def rows(i, b):
                pe.wait_ge(m.s_h, nth4(i, b))
                if after(i, b, 2):
                    pe.wait_ge(s_A, nth4(i, b, 2))
                    pe.wait_ge(s_B, nth4(i, b, 2))
                for j in range(NPG):
                    pe.matmul(pA[b % 2][:, j, :], m.hT[b][:, j * P:(j + 1) * P], w[:, 0:P], start=True, stop=True)
                    last = pe.matmul(pB[b % 2][:, j, :], m.hT[b][:, j * P:(j + 1) * P], w[:, P:], start=True, stop=True)
                last.then_inc(s_R, 1)

            pipelined4(pe, n, ((rows, 2), (lambda i, b: m.transpose(pe, i, b), 1)), 3)


def layer0_edges(k, a, plain, out_rows):
    nc, n = k.nc, k.STEPS4
    (s_w, s_idx, s_oh, s_A, s_hid, s_B, s_scan, s_T, s_row) = (k.sem("e0_" + x) for x in
        "weights indices onehot summed hidden message scanned transposed rows".split())
    lw, gs, st = ([k.sem(f"e0_{x}{b}") for b in range(SLOTS)] for x in ("window", "gathered", "stored"))
    ld, ldn = ([k.sem(f"e0_{x}{h}") for h in range(SLOTS // 2)] for x in ("pair_loaded", "pair_masks"))
    DEEPEST = 9
    with ExitStack() as c, nc.Block() as block:
        w1w, w2 = k.sb(c, "e0_w1w", [1, P]), k.sb(c, "e0_w2", [P, P])
        two = lambda name, shape, dt=F32: [k.sb(c, f"e0_{name}{b}", shape, dt) for b in range(2)]
        four = lambda name, shape, dt=F32: [k.sb(c, f"e0_{name}{b}", shape, dt) for b in range(SLOTS)]
        new, rel, wrow = two("new", [P, 2 * G], BF16), two("rel", [P, 2 * G], BF16), two("wrow", [1, 2 * G])
        win, oh, got, idx = four("win", [P, TPG, P]), four("oh", [P, G]), four("got", [P, TPG, P]), four("idx", [P, TPG], I32)
        hid, scan, row = two("hid", [P, G]), two("scan", [P, G]), two("row", [P, TPG, P])
        pA, pB, pT = ([k.ps(c, f"e0_p{x}{b}", [P, G]) for b in range(2)] for x in "ABT")

        def load_windows(eng, i, b, tiles):
            if after(i, b, SLOTS):
                eng.wait_ge(s_A, nth4(i, b, SLOTS))
                k.settle(eng)
            for j in tiles:
                base = eng.value_load(k.base_row[0:1, ds(i * (SLOTS * TPG) + (b * TPG + j), 1)], min_val=0, max_val=k.NP)
                eng.dma_start(win[b][:, j, :], k.TB0[ds(base, P), :]).then_inc(lw[b], 16)

        @block.sync
        def _(sp):
            sp.dma_start(w1w[:], a["L0_gnn_W1"][2 * P:2 * P + 1, :]).then_inc(s_w, 16)
            sp.dma_start(w2[:], a["L0_gnn_W2"]).then_inc(s_w, 16)

            def load_pair(i, b):
                if b % 2:
                    return
                e = ds(i * (SLOTS * G) + b * G, 2 * G)
                if after(i, b, SLOTS):
                    sp.wait_ge(s_A, nth4(i, b + 1, SLOTS))
                    sp.wait_ge(s_oh, nth4(i, b + 1, SLOTS))
                    k.settle(sp)
                sp.dma_start(rel[b // 2][:], k.REL[e].partition_broadcast(P)).then_inc(ld[b // 2], 16)
                sp.dma_start(wrow[b // 2][:], k.EW[e].unsqueeze(0)).then_inc(ld[b // 2], 16)

            def load_masks(i, b):
                if b % 2:
                    return
                if after(i, b, SLOTS):
                    sp.wait_ge(s_scan, nth4(i, b + 1, SLOTS))
                    k.settle(sp)
                sp.dma_start(new[b // 2][:], k.NEW[ds(i * (SLOTS * G) + b * G, 2 * G)].partition_broadcast(P)).then_inc(ldn[b // 2], 16)

            def windows(i, b):
                load_windows(sp, i, b, (0, 1))

            def store(i, b):
                sp.wait_ge(s_row, nth4(i, b))
                sp.dma_start(out_rows[ds(i * (SLOTS * G) + b * G, G), :].rearrange("(j p) d -> p j d", p=P),
                             row[b % 2][:]).then_inc(st[b], 16)

            pipelined4(sp, n, ((store, 9), (load_masks, 4), (load_pair, 0), (windows, 0)), DEEPEST)
            for b in range(SLOTS):
                sp.wait_ge(st[b], 16 * n)

        @block.gpsimd
        def _(pool):
            def gather(i, b):
                pool.wait_ge(s_idx, nth4(i, b))
                if after(i, b, SLOTS):
                    pool.wait_ge(s_A, nth4(i, b, SLOTS))
                k.settle(pool)
                for j in range(TPG):
                    pool.indirect_dma_start(out=got[b][:, j, :], out_offset=None, in_=plain,
                                            in_offset=bass.IndirectOffsetOnAxis(ap=idx[b][:, j:j + 1], axis=0)
                                            ).then_inc(gs[b], 16)
            pipelined4(pool, n, ((gather, 0),), DEEPEST)

        @block.vector
        def _(dve):
            def indices(i, b):
                if after(i, b, SLOTS):
                    dve.wait_ge(gs[b], i * (16 * TPG))
                dve.tensor_copy(idx[b][:], k.src_int[:, ds(i * (SLOTS * TPG) + b * TPG, TPG)]).then_inc(s_idx, 1)

            def onehot(i, b):
                dve.wait_ge(ld[b // 2], (i + 1) * 32)
                if after(i, b, SLOTS):
                    dve.wait_ge(s_A, nth4(i, b, SLOTS))
                dve.tensor_scalar(oh[b][:], rel[b // 2][:, (b % 2) * G:(b % 2 + 1) * G], k.lane[:], None, ALU.is_equal).then_inc(s_oh, 1)

            def running_max(i, b):
                dve.wait_ge(s_B, nth4(i, b))
                dve.wait_ge(ldn[b // 2], i * 16 + 16)
                first = isinstance(i, int) and i == 0 and b == 0
                if after(i, b, 2):
                    dve.wait_ge(s_T, nth4(i, b, 2))
                if not first:
                    dve.wait_ge(s_scan, nth4(i, b, 1))
                dve.tensor_tensor_scan(out=scan[b % 2][:], data0=new[b // 2][:, (b % 2) * G:(b % 2 + 1) * G], data1=pB[b % 2][:], op0=ALU.add, op1=ALU.max,
                                       initial=BIG if first else scan[(b + 1) % 2][:, G - 1:G]).then_inc(s_scan, 1)

            pipelined4(dve, n, ((indices, 0), (running_max, 6), (onehot, 2)), DEEPEST)

        @block.scalar
        def _(act):
            def windows(i, b):
                load_windows(act, i, b, (2, 3))

            def hidden(i, b):
                act.wait_ge(s_A, nth4(i, b))
                if after(i, b, 2):
                    act.wait_ge(s_B, nth4(i, b, 2))
                act.activation(hid[b % 2][:], pA[b % 2][:], ACT.Relu).then_inc(s_hid, 1)

            def rows(i, b):
                act.wait_ge(s_T, nth4(i, b))
                if after(i, b, 2):
                    slot, times = uses(i, b, 2)
                    act.wait_ge(st[slot], times * 16)
                act.copy(row[b % 2][:].rearrange("p j d -> p (j d)"), pT[b % 2][:]).then_inc(s_row, 1)

            pipelined4(act, n, ((rows, 8), (hidden, 3), (windows, 0)), DEEPEST)

        @block.tensor
        def _(pe):
            pe.wait_ge(s_w, 32)

            def summed(i, b):
                pe.wait_ge(ld[b // 2], (i + 1) * 32)
                if after(i, b, 2):
                    pe.wait_ge(s_hid, nth4(i, b, 2))
                pe.matmul(pA[b % 2][:], w1w[:], wrow[b // 2][:, (b % 2) * G:(b % 2 + 1) * G], start=True, stop=False)
                pe.wait_ge(s_oh, nth4(i, b))
                pe.wait_ge(lw[b], (i + 1) * (16 * TPG))
                for j in range(TPG):
                    at = slice(j * P, (j + 1) * P)
                    pe.matmul(pA[b % 2][:, at], win[b][:, j, :], oh[b][:, at], start=False, stop=False)
                pe.wait_ge(gs[b], (i + 1) * (16 * TPG))
                for j in range(TPG):
                    at = slice(j * P, (j + 1) * P)
                    last = pe.matmul(pA[b % 2][:, at], got[b][:, j, :], k.ident[:], start=False, stop=(j == TPG - 1))
                last.then_inc(s_A, 1)

            def message(i, b):
                pe.wait_ge(s_hid, nth4(i, b))
                if after(i, b, 2):
                    pe.wait_ge(s_scan, nth4(i, b, 2))
                pe.matmul(pB[b % 2][:], w2[:], hid[b % 2][:], start=True, stop=True).then_inc(s_B, 1)

            def to_rows(i, b):
                pe.wait_ge(s_scan, nth4(i, b))
                if after(i, b, 2):
                    pe.wait_ge(s_row, nth4(i, b, 2))
                for j in range(TPG):
                    at = slice(j * P, (j + 1) * P)
                    last = pe.transpose(pT[b % 2][:, at], scan[b % 2][:, at], k.ident[:])
                last.then_inc(s_T, 1)

            pipelined4(pe, n, ((message, 5), (to_rows, 7), (summed, 3)), DEEPEST)


class SlotChain:

    def __init__(self, eng, sem, each):
        self.eng, self.sem, self.each = eng, sem, each

    def __call__(self, instruction, i, b, nth_of_slot):
        instruction.then_inc(self.sem, 1)
        self.eng.wait_ge(self.sem, i * (SLOTS * self.each) + (b * self.each + nth_of_slot))


def add_rows(k, tag, rows, width, each, setup, combine, project, bias, hidden=None, own_rows=None):
    nc, n = k.nc, k.NSTEPS
    (s_ld, s_idx, s_t, s_ag, s_T, s_c, s_u, s_hid, s_v, s_ch, s_b, s_own) = (k.sem(f"{tag}_{x}") for x in
        "weights indices temp combined transposed copied upper hidden projected chain bias own".split())
    gs = [k.sem(f"{tag}_gathered{b}") for b in range(SLOTS)]
    own_s = [k.sem(f"{tag}_ownrows{b}") for b in range(SLOTS)]
    with ExitStack() as c, nc.Block() as block:
        four = lambda name, shape, dt=F32: [k.sb(c, f"{tag}_{name}{b}", shape, dt) for b in range(SLOTS)]
        idx, got, ag, aT, t2 = four("idx", [P, NPG], I32), four("got", [P, NPG, width]), four("ag", [P, NPG, P]), four("aT", [P, NG]), four("t2", [P, NPG, P])
        own = four("own", [P, NPG, P]) if own_rows is not None else None
        wp, bias_t = k.sb(c, tag + "_wp", [P, P]), k.sb(c, tag + "_bias", [P, P])
        extra, loads = setup(c)
        loads = loads + [(bias_t[:], bias.partition_broadcast(P)), (wp[:], project)]
        if hidden:
            uh, ua, c1 = k.sb(c, tag + "_uh", [P, P]), k.sb(c, tag + "_ua", [P, P]), k.sb(c, tag + "_c1", [P, 1])
            uT = four("uT", [P, NG])
            loads += [(uh[:], hidden[0][0:P, :]), (ua[:], hidden[0][P:, :]), (c1[:], hidden[1].unsqueeze(1))]
            pU = [k.ps(c, f"{tag}_pU{b}", [P, NG]) for b in range(2)]
        pT = [k.ps(c, f"{tag}_pT{b}", [P, NG]) for b in range(2)]
        pV = [k.ps(c, f"{tag}_pV{b}", [P, NPG, P]) for b in range(2)]
        last_lag = 6 if hidden else 5
        seen, aT_read = (s_hid, s_u) if hidden else (s_c, s_v)

        @block.sync
        def _(sp):
            for to, of in loads:
                sp.dma_start(to, of).then_inc(s_ld, 16)
            if own_rows is not None:
                def load(i, b):
                    if after(i, b, SLOTS):
                        sp.wait_ge(s_ag, nth4(i, b, SLOTS))
                    sp.dma_start(own[b][:], own_rows[ds(i * (SLOTS * NG) + b * NG, NG), :].rearrange("(j p) d -> p j d", p=P)
                                 ).then_inc(own_s[b], 16)

                pipelined4(sp, n, ((load, 0),), last_lag)
            sp.wait_ge(s_ld, 16 * len(loads))

        @block.gpsimd
        def _(pool):
            with pool.Fori(0, n) as i:
                for b in range(SLOTS):
                    pool.wait_ge(s_idx, nth4(i, b))
                    k.settle(pool)
                    for j in range(NPG):
                        pool.indirect_dma_start(out=got[b][:, j, :], out_offset=None, in_=rows,
                                                in_offset=bass.IndirectOffsetOnAxis(ap=idx[b][:, j:j + 1], axis=0)
                                                ).then_inc(gs[b], 16)

        @block.vector
        def _(dve):
            slot_chain = SlotChain(dve, s_ch, each)
            dve.wait_ge(s_ld, 16 * len(loads))

            def indices(i, b):
                if after(i, b, SLOTS):
                    dve.wait_ge(gs[b], i * (16 * NPG))
                    dve.wait_ge(s_ag, nth4(i, b, SLOTS))
                dve.tensor_copy(idx[b][:], k.last_of[:, ds(i * (SLOTS * NPG) + b * NPG, NPG)]).then_inc(s_idx, 1)

            def combined(i, b):
                dve.wait_ge(gs[b], (i + 1) * (16 * NPG))
                if own_rows is not None:
                    dve.wait_ge(own_s[b], i * 16 + 16)
                if after(i, b, 2):
                    dve.wait_ge(s_T, nth4(i, b, 2))
                combine(dve, extra, slot_chain, i, b, got[b], ag[b], own[b] if own else None).then_inc(s_ag, 1)

            def add(i, b):
                dve.wait_ge(s_v, nth4(i, b))
                if after(i, b, SLOTS):
                    dve.wait_ge(s_b, nth4(i, b, SLOTS))
                dve.tensor_tensor(t2[b][:], pV[b % 2][:], bias_t[:].unsqueeze(1).to_broadcast([P, NPG, P]), ALU.add).then_inc(s_t, 1)
                dve.wait_ge(s_t, nth4(i, b))
                x = k.X[:, ds(i * (SLOTS * NG) + b * NG, NG)]
                dve.tensor_tensor(x, x, t2[b][:].rearrange("p j d -> p (j d)"), ALU.add).then_inc(s_b, 1)

            pipelined4(dve, n, ((indices, 0), (add, last_lag), (combined, 3)), last_lag)

        @block.scalar
        def _(act):
            act.wait_ge(s_ld, 16 * len(loads))

            def copied(i, b):
                act.wait_ge(s_T, nth4(i, b))
                if after(i, b, 2):
                    act.wait_ge(aT_read, nth4(i, b, 2))
                act.copy(aT[b][:], pT[b % 2][:]).then_inc(s_c, 1)

            def hid(i, b):
                act.wait_ge(s_u, nth4(i, b))
                if after(i, b, 2):
                    act.wait_ge(s_v, nth4(i, b, 2))
                act.activation(uT[b][:], pU[b % 2][:], ACT.Relu, bias=c1[:]).then_inc(s_hid, 1)

            pipelined4(act, n, ((hid, 4), (copied, 3)) if hidden else ((copied, 3),), last_lag)

        @block.tensor
        def _(pe):
            pe.wait_ge(s_ld, 16 * len(loads))

            def transposed(i, b):
                pe.wait_ge(s_ag, nth4(i, b))
                if after(i, b, 2):
                    pe.wait_ge(s_c, nth4(i, b, 2))
                for j in range(NPG):
                    last = pe.transpose(pT[b % 2][:, j * P:(j + 1) * P], ag[b][:, j, :], k.ident[:])
                last.then_inc(s_T, 1)

            def upper(i, b):
                pe.wait_ge(s_c, nth4(i, b))
                if after(i, b, 2):
                    pe.wait_ge(s_hid, nth4(i, b, 2))
                pe.matmul(pU[b % 2][:], ua[:], aT[b][:], start=True, stop=False)
                pe.matmul(pU[b % 2][:], uh[:], k.HT[:, ds(i * (SLOTS * NG) + b * NG, NG)], start=False, stop=True).then_inc(s_u, 1)

            def projected(i, b):
                pe.wait_ge(seen, nth4(i, b))
                if after(i, b, 2):
                    pe.wait_ge(s_t, nth4(i, b, 2))
                src = uT if hidden else aT
                for j in range(NPG):
                    last = pe.matmul(pV[b % 2][:, j, :], src[b][:, j * P:(j + 1) * P], wp[:], start=True, stop=True)
                last.then_inc(s_v, 1)

            pipelined4(pe, n, ((projected, 5), (upper, 4), (transposed, 3)) if hidden else ((projected, 4), (transposed, 3)), last_lag)


def update0(k, a, rows):
    def setup(c):
        b2 = k.sb(c, "u0_b2", [P, P])
        tmp = [k.sb(c, f"u0_tmp{b}", [P, NPG, P]) for b in range(SLOTS)]
        return (b2, tmp), [(b2[:], a["L0_gnn_b2"].partition_broadcast(P))]

    def combine(dve, extra, link, i, b, got, ag, own):
        b2, tmp = extra
        link(dve.tensor_tensor(tmp[b][:], got[:], b2[:].unsqueeze(1).to_broadcast([P, NPG, P]), ALU.add), i, b, 1)
        t = i * (SLOTS * NPG) + b * NPG
        return dve.tensor_tensor(ag[:], tmp[b][:], k.has[:, ds(t, NPG)].unsqueeze(2).to_broadcast([P, NPG, P]), ALU.mult)
    add_rows(k, "u0", rows, P, 1, setup, combine, a["L0_gnn_U2"], a["L0_gnn_c2"], hidden=(a["L0_gnn_U1"], a["L0_gnn_c1"]))


def normalize_only(k, tag, rows=None):
    nc, n = k.nc, k.NSTEPS
    s_r = k.sem(tag + "_rows")
    st = [k.sem(f"{tag}_stored{b}") for b in range(SLOTS)]
    with ExitStack() as c, nc.Block() as block:
        m = Norm(k, c, tag, None)
        h = [k.sb(c, f"{tag}_h{b}", [P, NG]) for b in range(SLOTS)]

        @block.sync
        def _(sp):
            if rows is None:
                return
            with sp.Fori(0, n) as i:
                for b in range(SLOTS):
                    sp.wait_ge(s_r, nth4(i, b))
                    sp.dma_start(rows[ds(i * (SLOTS * NG) + b * NG, NG), :].rearrange("(j p) d -> p j d", p=P),
                                 h[b][:].rearrange("p (j d) -> p j d", d=P)).then_inc(st[b], 16)
            for b in range(SLOTS):
                sp.wait_ge(st[b], 16 * n)

        @block.vector
        def _(dve):
            m.statistics(dve)

            def clipped(i, b):
                dve.wait_ge(m.s_y, nth4(i, b))
                if after(i, b, SLOTS):
                    dve.wait_ge(st[b], i * 16)
                dve.tensor_scalar(h[b][:], m.y[b][:], 0.0, None, ALU.max).then_inc(s_r, 1)

            def normalized(i, b):
                m.normalize(dve, i, b, s_r if rows is not None else m.s_T)
            pipelined4(dve, n, ((normalized, 0), (clipped, 0)) if rows is not None else ((normalized, 0),), 1)

        @block.scalar
        def _(act):
            m.deviation(act)
            if k.HT is None:
                return
            with act.Fori(0, n) as i:
                for b in range(SLOTS):
                    act.wait_ge(m.s_T, nth4(i, b))
                    k.settle(act)
                    act.activation(k.HT[:, ds(i * (SLOTS * NG) + b * NG, NG)], m.pT[b % 2][:], ACT.Relu).then_inc(m.s_h, 1)

        @block.tensor
        def _(pe):
            if k.HT is None:
                return
            pipelined4(pe, n, ((lambda i, b: m.transpose(pe, i, b), 0),), 1)


def layer1_tables(k, a):
    nc, n = k.nc, k.NSTEPS
    (s_ld, s_ch, s_var, s_std, s_one, s_xs, s_p, s_q, s_R, s_row, s_idx) = (k.sem("t1_" + x) for x in
        "weights chain variance deviation ones xn products squares rows done indices".split())
    sc = [k.sem(f"t1_scattered{b}") for b in range(SLOTS)]
    chunks = -(-k.N // 512)
    size = -(-k.N // chunks)
    cuts = [(at, min(at + size, k.N)) for at in range(0, k.N, size)]
    with ExitStack() as c, nc.Block() as block:
        four = lambda name, shape, dt=F32: [k.sb(c, f"t1_{name}{b}", shape, dt) for b in range(SLOTS)]
        k0, k1, k2 = (k.sb(c, f"t1_k{x}", [P, P]) for x in range(3))
        gamma, beta, dev, scale, shift, ms = (k.sb(c, "t1_" + x, [P, 1]) for x in "gamma beta dev scale shift ms".split())
        stats, agg = k.sb(c, "t1_stats", [P, len(cuts) * 6]), k.sb(c, "t1_agg", [P, 2])
        xs, q, row, idx = four("xs", [P, NG]), four("q", [P, 2, NG]), four("row", [P, NPG, W1COLS]), four("idx", [P, NPG], I32)
        pP = [k.ps(c, f"t1_pP{b}", [P, 2, NG]) for b in range(2)]
        pR = [k.ps(c, f"t1_pR{b}", [P, NG + 2 * NPG]) for b in range(2)]

        @block.sync
        def _(sp):
            for to, of in ((k0, a["L1_gnn_kernel"]), (k1, a["L1_gnn_kernel1"]), (k2, a["L1_gnn_kernel2"]),
                           (gamma, a["L1_gnn_gamma"].unsqueeze(1)), (beta, a["L1_gnn_beta"].unsqueeze(1))):
                sp.dma_start(to[:], of).then_inc(s_ld, 16)
            sp.wait_ge(s_ld, 80)

        @block.gpsimd
        def _(pool):
            with pool.Fori(0, n) as i:
                for b in range(SLOTS):
                    pool.wait_ge(s_row, nth4(i, b))
                    pool.wait_ge(s_idx, nth4(i, b))
                    k.settle(pool)
                    for j in range(NPG):
                        pool.indirect_dma_start(out=k.TB1, out_offset=bass.IndirectOffsetOnAxis(ap=idx[b][:, j:j + 1], axis=0),
                                                in_=row[b][:, j, :], in_offset=None).then_inc(sc[b], 16)
            for b in range(SLOTS):
                pool.wait_ge(sc[b], 16 * NPG * n)

        @block.vector
        def _(dve):
            link = chain(dve, s_ch)
            for b in range(SLOTS):
                dve.memset(row[b][:, :, P:P + 1], 1.0).then_inc(s_one, 1)
            for x, (at, to) in enumerate(cuts):
                last = dve.bn_stats(stats[:, x * 6:(x + 1) * 6], k.HT[:, at:to])
            link(last)
            link(dve.bn_aggr(agg[:], stats[:]))
            dve.tensor_scalar(dev[:], agg[:, 1:2], 1e-5, None, ALU.add).then_inc(s_var, 1)
            dve.wait_ge(s_std, 1)
            dve.wait_ge(s_ld, 80)
            link(dve.reciprocal(scale[:], shift[:]))
            link(dve.tensor_tensor(scale[:], scale[:], gamma[:], ALU.mult))
            link(dve.tensor_tensor(ms[:], agg[:, 0:1], scale[:], ALU.mult))
            link(dve.tensor_tensor(shift[:], beta[:], ms[:], ALU.subtract))

            def normed(i, b):
                if after(i, b, SLOTS):
                    dve.wait_ge(s_R, nth4(i, b, SLOTS))
                    dve.wait_ge(sc[b], i * (16 * NPG))
                dve.tensor_scalar(xs[b][:], k.HT[:, ds(i * (SLOTS * NG) + b * NG, NG)], scale[:], shift[:], ALU.mult,
                                  ALU.add).then_inc(s_xs, 1)
                dve.tensor_copy(idx[b][:], k.rank_of[:, ds(i * (SLOTS * NPG) + b * NPG, NPG)]).then_inc(s_idx, 1)

            def products(i, b):
                dve.wait_ge(s_p, nth4(i, b))
                if after(i, b, 2):
                    dve.wait_ge(s_R, nth4(i, b, 2))
                dve.tensor_tensor(q[b][:], pP[b % 2][:], xs[b][:].unsqueeze(1).to_broadcast([P, 2, NG]), ALU.mult).then_inc(s_q, 1)

            pipelined4(dve, n, ((normed, 0), (products, 2)), 4)

        @block.scalar
        def _(act):
            act.wait_ge(s_var, 1)
            act.activation(shift[:], dev[:], ACT.Sqrt).then_inc(s_std, 1)
            act.wait_ge(s_one, SLOTS)

            def finish(i, b):
                act.wait_ge(s_R, nth4(i, b))
                if after(i, b, SLOTS):
                    act.wait_ge(sc[b], i * (16 * NPG))
                act.copy(row[b][:, :, 0:P], pR[b % 2][:, 0:NG].rearrange("p (j d) -> p j d", d=P))
                s = pR[b % 2][:, NG:].rearrange("p (j w) -> p j w", w=2)
                act.activation(k.S1[:, ds(i * (SLOTS * NPG) + b * NPG, NPG)], s[:, :, 0], ACT.Tanh)
                act.activation(row[b][:, :, P + 1], s[:, :, 1], ACT.Tanh).then_inc(s_row, 1)

            pipelined4(act, n, ((finish, 4),), 4)

        @block.tensor
        def _(pe):
            pe.wait_ge(s_ld, 80)

            def product(i, b):
                pe.wait_ge(s_xs, nth4(i, b))
                if after(i, b, 2):
                    pe.wait_ge(s_q, nth4(i, b, 2))
                pe.matmul(pP[b % 2][:, 0, :], k1[:], xs[b][:], start=True, stop=True)
                pe.matmul(pP[b % 2][:, 1, :], k2[:], xs[b][:], start=True, stop=True).then_inc(s_p, 1)

            def rows(i, b):
                pe.wait_ge(s_q, nth4(i, b))
                if after(i, b, 2):
                    pe.wait_ge(s_row, nth4(i, b, 2))
                for j in range(NPG):
                    at = slice(j * P, (j + 1) * P)
                    pe.matmul(pR[b % 2][:, at], xs[b][:, at], k0[:], start=True, stop=True)
                    for w in range(2):
                        last = pe.matmul(pR[b % 2][:, NG + 2 * j + w:NG + 2 * j + w + 1], q[b][:, w, at], k.ones[:, 0:1],
                                         start=True, stop=True)
                last.then_inc(s_R, 1)

            pipelined4(pe, n, ((rows, 3), (product, 1)), 4)


def layer1_edges(k):
    nc, n, TN = k.nc, k.STEPS4, k.TN
    (s_const, s_cch, s_oh, s_sq, s_eq, s_dup, s_away, s_to, s_X, s_sel, s_u, s_l, s_ee, s_mx, s_Y, s_py) = (k.sem("e1_" + x) for x in
        "constants const_chain onehots squares equal twins spared targets expanded selected sum leaky weight weighted joined copied".split())
    ld = [k.sem(f"e1_pair_loaded{h}") for h in range(SLOTS // 2)]
    lw = [k.sem(f"e1_windows{b}") for b in range(SLOTS)]
    sc = [[k.sem(f"e1_added{b}{j}") for j in range(TPG)] for b in range(SLOTS)]
    DEEPEST = 6
    H = TPG // 2
    with ExitStack() as c, nc.Block() as block:
        two = lambda name, shape, dt=F32: [k.sb(c, f"e1_{name}{b}", shape, dt) for b in range(2)]
        four = lambda name, shape, dt=F32: [k.sb(c, f"e1_{name}{b}", shape, dt) for b in range(SLOTS)]
        high_i = k.sb(c, "e1_high_int", [P, k.NT], I32)
        iota_t, high, away_all = k.sb(c, "e1_iota", [P, TN]), k.sb(c, "e1_high", [P, k.NT]), k.sb(c, "e1_away", [P, k.NT])
        rel, lrow, srow = two("rel", [P, 2 * G], BF16), two("lrow", [P, 2 * G], BF16), two("srow", [P, 2 * G])
        win, eq, py = four("win", [P, TPG, W1COLS]), four("eq", [P, TPG, P]), four("py", [P, TPG, W1COLS])
        oh, low, mx = two("oh", [P, G]), two("low", [P, G]), two("mx", [P, TPG, W1COLS])
        minus, squares = k.sb(c, "e1_minus_src", [P, k.NT]), k.sb(c, "e1_squares", [P, TPG, P])
        junk, unused = k.sb(c, "e1_junk", [P, TPG, P]), k.sb(c, "e1_unused", [P, TPG, TN])
        to = four("to", [P, TPG], I32)
        s1, u, l, ee, dup, away = (four(x, [P, TPG]) for x in "s1 u l ee dup away".split())
        pX = [[k.ps(c, f"e1_pX{b}{h}", [P, H, W1COLS + TN]) for h in range(2)] for b in range(2)]
        pY = [[k.ps(c, f"e1_pY{b}{h}", [P, H, W1COLS]) for h in range(2)] for b in range(2)]
        half = lambda t, h: t[:, h * H:(h + 1) * H]
        pair = lambda t, b: t[b // 2][:, (b % 2) * G:(b % 2 + 1) * G]

        def load_windows(eng, i, b, tiles):
            if after(i, b, SLOTS):
                eng.wait_ge(s_X, nth4(i, b, SLOTS))
                k.settle(eng)
            for j in tiles:
                base = eng.value_load(k.base_row[0:1, ds(i * (SLOTS * TPG) + (b * TPG + j), 1)], min_val=0, max_val=k.NP)
                eng.dma_start(win[b][:, j, :], k.TB1[ds(base, P), :]).then_inc(lw[b], 16)

        @block.sync
        def _(sp):
            def line_pair(i, b):
                if b % 2:
                    return
                e = ds(i * (SLOTS * G) + b * G, 2 * G)
                if after(i, b, SLOTS):
                    sp.wait_ge(s_dup, nth4(i, b + 1, SLOTS))
                    sp.wait_ge(s_eq, nth4(i, b + 1, SLOTS))
                    k.settle(sp)
                sp.dma_start(rel[b // 2][:], k.REL[e].partition_broadcast(P)).then_inc(ld[b // 2], 16)
                sp.dma_start(lrow[b // 2][:], k.LOW[e].partition_broadcast(P)).then_inc(ld[b // 2], 16)
                sp.dma_start(srow[b // 2][:], k.SRCF[e].partition_broadcast(P)).then_inc(ld[b // 2], 16)

            def windows(i, b):
                load_windows(sp, i, b, (0, 1, 2))
            pipelined4(sp, n, ((line_pair, 0), (windows, 0)), DEEPEST)

        @block.gpsimd
        def _(pool):
            pool.iota(iota_t[:], pattern=[[1, TN]], base=0, channel_multiplier=0,
                      allow_small_or_imprecise_dtypes=True).then_inc(s_const, 1)

            def add(i, b):
                pool.wait_ge(s_to, nth4(i, b))
                pool.wait_ge(s_py, nth4(i, b))
                k.settle(pool)
                for j in range(TPG):
                    if after(i, b, 1):
                        slot, times = uses(i, b, 1)
                        pool.wait_ge(sc[slot][j], times * 16)
                        k.settle(pool)
                    pool.indirect_dma_start(out=k.ADD[j],
                                            out_offset=bass.IndirectOffsetOnAxis(ap=to[b][:, j:j + 1], axis=0),
                                            in_=py[b][:, j, :], in_offset=None, compute_op=ALU.add).then_inc(sc[b][j], 16)
            pipelined4(pool, n, ((add, 6),), DEEPEST)
            for b in range(SLOTS):
                for j in range(TPG):
                    pool.wait_ge(sc[b][j], 16 * n)

        @block.vector
        def _(dve):
            fixed = chain(dve, s_cch)
            fixed(dve.tensor_scalar(high_i[:], k.src_int[:], P.bit_length() - 1, None, ALU.logical_shift_right))
            dve.tensor_copy(high[:], high_i[:])
            fixed(dve.tensor_scalar(away_all[:], k.src_col[:], -1.0, k.spare[:], ALU.mult, ALU.add))
            dve.tensor_scalar(minus[:], k.src_col[:], -1.0, None, ALU.mult).then_inc(s_const, 1)
            dve.wait_ge(s_const, 2)

            def prepare(i, b):
                t = i * (SLOTS * TPG) + b * TPG
                dve.wait_ge(ld[b // 2], (i + 1) * 48)
                if after(i, b, 2):
                    dve.wait_ge(s_X, nth4(i, b, 2))
                dve.tensor_scalar(oh[b % 2][:], pair(rel, b), k.lane[:], None, ALU.is_equal)
                dve.tensor_scalar(low[b % 2][:], pair(lrow, b), k.lane[:], None, ALU.is_equal).then_inc(s_oh, 1)
                if after(i, b, 1):
                    dve.wait_ge(s_dup, nth4(i, b, 1))
                for j in range(TPG):
                    last = dve.scalar_tensor_tensor(out=junk[:, j, :], in0=pair(srow, b)[:, j * P:(j + 1) * P], scalar=k.src_col[:, ds(t + j, 1)], in1=k.above[:],
                                                    op0=ALU.is_equal, op1=ALU.mult, accum_out=dup[b][:, j:j + 1])
                last.then_inc(s_dup, 1)

            def spared(i, b):
                dve.wait_ge(s_dup, nth4(i, b))
                dve.scalar_tensor_tensor(out=away[b][:], in0=dup[b][:], scalar=0.0,
                                         in1=away_all[:, ds(i * (SLOTS * TPG) + b * TPG, TPG)], op0=ALU.is_gt,
                                         op1=ALU.mult).then_inc(s_away, 1)

            def targets(i, b):
                dve.wait_ge(s_away, nth4(i, b))
                if after(i, b, SLOTS):
                    for j in range(TPG):
                        dve.wait_ge(sc[b][j], i * 16)
                dve.tensor_tensor(to[b][:], away[b][:], k.src_col[:, ds(i * (SLOTS * TPG) + b * TPG, TPG)], ALU.add).then_inc(s_to, 1)

            def select(i, b):
                t = i * (SLOTS * TPG) + b * TPG
                dve.wait_ge(s_X, nth4(i, b))
                if after(i, b, 1):
                    dve.wait_ge(s_sel, nth4(i, b, 1))
                for j in range(TPG):
                    last = dve.scalar_tensor_tensor(out=unused[:, j, :], in0=iota_t[:], scalar=high[:, ds(t + j, 1)],
                                                    in1=pX[b % 2][j // H][:, j % H, W1COLS:], op0=ALU.is_equal, op1=ALU.mult,
                                                    accum_out=s1[b][:, j:j + 1])
                last.then_inc(s_sel, 1)

            def scores(i, b):
                dve.wait_ge(s_sel, nth4(i, b))
                for h in range(2):
                    last = dve.tensor_tensor(half(u[b], h), pX[b % 2][h][:, :, P + 1], half(s1[b], h), ALU.add)
                last.then_inc(s_u, 1)

            def leaky(i, b):
                dve.wait_ge(s_u, nth4(i, b))
                if after(i, b, SLOTS):
                    dve.wait_ge(s_ee, nth4(i, b, SLOTS))
                dve.scalar_tensor_tensor(out=l[b][:], in0=u[b][:], scalar=0.01, in1=u[b][:], op0=ALU.mult,
                                         op1=ALU.max).then_inc(s_l, 1)

            def weigh(i, b):
                dve.wait_ge(s_ee, nth4(i, b))
                if after(i, b, 2):
                    dve.wait_ge(s_Y, nth4(i, b, 2))
                for h in range(2):
                    last = dve.tensor_tensor(half(mx[b % 2], h), pX[b % 2][h][:, :, 0:W1COLS],
                                             half(ee[b], h).unsqueeze(2).to_broadcast([P, H, W1COLS]), ALU.mult)
                last.then_inc(s_mx, 1)
            pipelined4(dve, n, ((select, 4), (spared, 4), (scores, 4), (targets, 4), (leaky, 4), (prepare, 2), (weigh, 4)), DEEPEST)

        @block.scalar
        def _(act):
            def windows(i, b):
                load_windows(act, i, b, (3,))

            act.wait_ge(s_const, 2)

            def equal(i, b):
                t = i * (SLOTS * TPG) + b * TPG
                act.wait_ge(ld[b // 2], i * 48 + 48)
                if after(i, b, SLOTS):
                    act.wait_ge(s_Y, nth4(i, b, SLOTS))
                if after(i, b, 1):
                    act.wait_ge(s_eq, nth4(i, b, 1))
                k.settle(act)
                for j in range(TPG):
                    last = act.activation(squares[:, j, :], pair(srow, b)[:, j * P:(j + 1) * P], ACT.Square,
                                          bias=minus[:, ds(t + j, 1)])
                last.then_inc(s_sq, 1)
                act.wait_ge(s_sq, nth4(i, b))
                act.activation(eq[b][:], squares[:], ACT.Relu, bias=k.ones[:, 0:1], scale=-1.0).then_inc(s_eq, 1)

            def weight(i, b):
                act.wait_ge(s_l, nth4(i, b))
                if after(i, b, SLOTS):
                    act.wait_ge(s_mx, nth4(i, b, SLOTS))
                act.activation(ee[b][:], l[b][:], ACT.Exp).then_inc(s_ee, 1)

            def rows(i, b):
                act.wait_ge(s_Y, nth4(i, b))
                if after(i, b, SLOTS):
                    for j in range(TPG):
                        act.wait_ge(sc[b][j], i * 16)
                for h in range(2):
                    last = act.copy(half(py[b], h), pY[b % 2][h][:])
                last.then_inc(s_py, 1)
            pipelined4(act, n, ((weight, 4), (rows, 5), (equal, 2), (windows, 0)), DEEPEST)

        @block.tensor
        def _(pe):
            def expand(i, b):
                pe.wait_ge(s_oh, nth4(i, b))
                pe.wait_ge(lw[b], (i + 1) * (16 * TPG))
                if after(i, b, 2):
                    pe.wait_ge(s_mx, nth4(i, b, 2))
                for j in range(TPG):
                    at, bank = slice(j * P, (j + 1) * P), pX[b % 2][j // H]
                    pe.matmul(bank[:, j % H, 0:W1COLS], oh[b % 2][:, at], win[b][:, j, :], start=True, stop=True)
                    last = pe.matmul(bank[:, j % H, W1COLS:], low[b % 2][:, at], k.S1[:], start=True, stop=True)
                last.then_inc(s_X, 1)

            def join(i, b):
                pe.wait_ge(s_mx, nth4(i, b))
                pe.wait_ge(s_eq, nth4(i, b))
                if after(i, b, 2):
                    pe.wait_ge(s_py, nth4(i, b, 2))
                for j in range(TPG):
                    last = pe.matmul(pY[b % 2][j // H][:, j % H, :], eq[b][:, j, :], mx[b % 2][:, j, :], start=True, stop=True)
                last.then_inc(s_Y, 1)
            pipelined4(pe, n, ((join, 5), (expand, 3)), DEEPEST)


def update1(k):
    nc, n = k.nc, k.NSTEPS
    s_ch, s_sum, s_done = (k.sem("u1_" + x) for x in "chain summed done".split())
    ld = [k.sem(f"u1_loaded{b}") for b in range(SLOTS)]
    with ExitStack() as c, nc.Block() as block:
        four = lambda name, shape: [k.sb(c, f"u1_{name}{b}", shape) for b in range(SLOTS)]
        parts, total = four("parts", [P, ADDERS, NPG, W1COLS]), four("total", [P, NPG, W1COLS])
        den, rden, new = four("den", [P, NPG]), four("rden", [P, NPG]), four("new", [P, NPG, P])

        @block.sync
        def _(sp):
            def load(i, b):
                if after(i, b, SLOTS):
                    sp.wait_ge(s_sum, nth4(i, b, SLOTS))
                for t in range(ADDERS):
                    sp.dma_start(parts[b][:, t], k.ADD[t][ds(i * (SLOTS * NG) + b * NG, NG), :].rearrange("(j p) d -> p j d", p=P)
                                 ).then_inc(ld[b], 16)
            pipelined4(sp, n, ((load, 0),), 1)

        @block.vector
        def _(dve):
            link = SlotChain(dve, s_ch, 3)

            def merge(i, b):
                dve.wait_ge(ld[b], (i + 1) * (16 * ADDERS))
                dve.tensor_reduce(total[b][:].rearrange("p j d -> p (j d)"), parts[b][:].rearrange("p t j d -> p (j d) t"), AX.X,
                                  ALU.add).then_inc(s_sum, 1)
                dve.wait_ge(s_sum, nth4(i, b))
                link(dve.tensor_scalar(den[b][:], total[b][:, :, P], 1e-16, None, ALU.max), i, b, 1)
                link(dve.reciprocal(rden[b][:], den[b][:]), i, b, 2)
                for j in range(NPG):
                    last = dve.tensor_scalar(new[b][:, j, :], total[b][:, j, 0:P], rden[b][:, j:j + 1], 0.0, ALU.mult, ALU.max)
                link(last, i, b, 3)
                x = k.X[:, ds(i * (SLOTS * NG) + b * NG, NG)]
                dve.tensor_tensor(x, x, new[b][:].rearrange("p j d -> p (j d)"), ALU.add).then_inc(s_done, 1)

            with dve.Fori(0, n) as i:
                for b in range(SLOTS):
                    merge(i, b)


def layer2_edges(k, a, plain, out_rows):
    nc, n = k.nc, k.STEPS4
    H, HV = 8, 16
    names = ("weights made wchain attrT attr_copied linear activated gated_mlp indices onehot summed weighted "
             "message alpha alpha_act gated score value maximum step_back shifted subtracted exponents pv running rows rowcopy").split()
    (s_ld, s_made, s_wch, s_At, s_atc, s_p12, s_t12, s_a12, s_idx, s_oh, s_M, s_mea, s_mT, s_al, s_x, s_z,
     s_S, s_V, s_scan, s_dr, s_d, s_sub, s_e, s_pv, s_acc, s_T, s_row) = (k.sem("e2_" + x) for x in names)
    lda, ldr, lde, ldn = ([k.sem(f"e2_pair_{x}{h}") for h in range(SLOTS // 2)] for x in ("attr", "places", "weights", "masks"))
    ldw, gs, st = ([k.sem(f"e2_{x}{b}") for b in range(SLOTS)] for x in ("windows", "gathered", "stored"))
    DEEPEST = 11
    F = 64
    lo, hi = slice(0, F), slice(F, P)
    with ExitStack() as c, nc.Block() as block:
        two = lambda name, shape, dt=F32: [k.sb(c, f"e2_{name}{b}", shape, dt) for b in range(2)]
        one = lambda name, shape, dt=F32: k.sb(c, "e2_" + name, shape, dt)
        w1, w2, w3 = one("w1", [P, TPG, F]), one("w2", [P, F]), one("w3", [P, P])
        wa, wv, head = one("wa", [P, P]), one("wv", [P, P]), one("head", [P, P])
        pick = one("pick", [P, H])
        cols = one("cols", [P, 8])
        b12, b12h, b3, ba, bah, adot, adots = (cols[:, x:x + 1] for x in range(7))
        four = lambda name, shape, dt=F32: [k.sb(c, f"e2_{name}{b}", shape, dt) for b in range(SLOTS)]
        atT, a12 = two("atT", [P, P]), two("a12", [P, G])
        attr, rel = two("attr", [P, 2 * TPG, 32]), two("rel", [P, 2 * G], BF16)
        new, ea = two("new", [P, 2 * G], BF16), two("ea", [P, 2 * G])
        win, oh, got, idx = four("win", [P, TPG, P]), four("oh", [P, G]), four("got", [P, TPG, P]), four("idx", [P, TPG], I32)
        mT, z, top = four("mT", [P, G]), two("z", [P, G]), two("top", [P, 1 + G])
        acc, den, row = two("acc", [P, G]), two("den", [P, G]), two("row", [P, TPG, W2COLS])
        x12, t12, mea, xa, ta, d, dr, p, r, pv = (one(x, [P, G]) for x in "x12 t12 mea xa ta d dr p r pv".split())
        pM, pR, pS, pV, pA, pT, p12, pD = (k.ps(c, "e2_p" + x, [P, G]) for x in "M R S V A T 12 D".split())
        D3 = pD[:, P:P + TPG * H].rearrange("p (j h) -> p j h", h=H)

        def pair(t, b):
            return t[b // 2][:, (b % 2) * G:(b % 2 + 1) * G]

        @block.sync
        def _(sp):
            sep = a["L2_gnn_w_sep"].rearrange("c (h t v) -> t c h v", h=H, t=2)
            loads = [(w1[32 * j:32 * j + 32, j, :], a["L2_gnn_fc_w1"]) for j in range(TPG)]
            loads += [(w2[lo, :], a["L2_gnn_fc_w2"]), (w3[hi, :], a["L2_gnn_fc_w3"]),
                      (wa[:].rearrange("p (h v) -> p h v", h=H), sep[0]), (wv[:].rearrange("p (h v) -> p h v", h=H), sep[1]),
                      (b12[lo], a["L2_gnn_fc_b1"].unsqueeze(1)), (b12[hi], a["L2_gnn_fc_b2"].unsqueeze(1)),
                      (b3, a["L2_gnn_fc_b3"].unsqueeze(1)), (adot, a["L2_gnn_alpha_dot"].rearrange("o h v -> (h v) o"))]
            loads += [(ba[HV * h:HV * h + HV], a["L2_gnn_b_sep"][2 * HV * h:2 * HV * h + HV].unsqueeze(1)) for h in range(H)]
            sp.wait_ge(s_wch, 3)
            for to, of in loads:
                sp.dma_start(to, of).then_inc(s_ld, 16)
            sp.wait_ge(s_ld, 16 * len(loads))
            sp.sem_inc(s_made, 1)

            def attr_pair(i, b):
                if b % 2:
                    return
                last = isinstance(i, int) and i == n - 1
                e = slice(b * G, (b + 2) * G) if last else ds(i * (SLOTS * G) + b * G, 2 * G)
                if after(i, b, SLOTS):
                    sp.wait_ge(s_At, nth4(i, b + 1, SLOTS))
                    k.settle(sp)
                sp.dma_start(attr[b // 2][:], (k.EATT if last else a["edge_attr_32"])[e, :].rearrange("(j p) f -> p j f", p=P)).then_inc(lda[b // 2], 16)

            def line_pair(i, b, tile, table, used, loaded):
                if b % 2:
                    return
                if after(i, b, SLOTS):
                    sp.wait_ge(used, nth4(i, b + 1, SLOTS))
                    k.settle(sp)
                sp.dma_start(tile[b // 2][:], table[ds(i * (SLOTS * G) + b * G, 2 * G)].partition_broadcast(P)).then_inc(loaded[b // 2], 16)

            def place_pair(i, b):
                line_pair(i, b, rel, k.REL, s_oh, ldr)

            def weight_pair(i, b):
                line_pair(i, b, ea, k.EA, s_mea, lde)

            def mask_pair(i, b):
                line_pair(i, b, new, k.NEW, s_dr, ldn)

            def windows(i, b):
                if after(i, b, SLOTS):
                    sp.wait_ge(s_M, nth4(i, b, SLOTS))
                    k.settle(sp)
                for j in range(TPG):
                    base = sp.value_load(k.base_row[0:1, ds(i * (SLOTS * TPG) + (b * TPG + j), 1)], min_val=0, max_val=k.NP)
                    sp.dma_start(win[b][:, j, :], k.TB2[ds(base, P), :]).then_inc(ldw[b], 16)

            def store(i, b):
                e = ds(i * (SLOTS * G) + b * G, G)
                sp.wait_ge(s_row, nth4(i, b))
                sp.dma_start(out_rows[e, :].rearrange("(j p) d -> p j d", p=P), row[b % 2][:]).then_inc(st[b], 16)

            pipelined4(sp, n, ((store, 11), (place_pair, 2), (windows, 3), (weight_pair, 4), (mask_pair, 7), (attr_pair, 0)), DEEPEST, peel_last=True)
            for b in range(SLOTS):
                sp.wait_ge(st[b], 16 * n)

        @block.gpsimd
        def _(pool):
            h3 = head[:].rearrange("p (h v) -> p h v", h=H)
            pool.memset(head[:], 1.0).then_inc(s_wch, 1)
            pool.memset(pick[:], 0.0).then_inc(s_wch, 1)
            pool.memset(w1[:], 0.0).then_inc(s_wch, 1)
            pool.wait_ge(s_wch, 3)
            pool.affine_select(out=h3, in_=h3, compare_op=ALU.is_ge, fill=0.0, base=0, pattern=[[-HV, H], [0, HV]],
                               channel_multiplier=1).then_inc(s_wch, 1)
            pool.wait_ge(s_wch, 4)
            pool.affine_select(out=h3, in_=h3, compare_op=ALU.is_ge, fill=0.0, base=HV - 1, pattern=[[HV, H], [0, HV]],
                               channel_multiplier=-1).then_inc(s_wch, 1)
            pool.affine_select(out=pick[:], in_=pick[:], compare_op=ALU.not_equal, fill=1.0, base=0, pattern=[[-HV, H]],
                               channel_multiplier=1).then_inc(s_wch, 1)

            def gather(i, b):
                pool.wait_ge(s_idx, nth4(i, b))
                if after(i, b, SLOTS):
                    pool.wait_ge(s_M, nth4(i, b, SLOTS))
                k.settle(pool)
                for j in range(TPG):
                    pool.indirect_dma_start(out=got[b][:, j, :], out_offset=None, in_=plain,
                                            in_offset=bass.IndirectOffsetOnAxis(ap=idx[b][:, j:j + 1], axis=0)
                                            ).then_inc(gs[b], 16)

            def steps_back(i, b):
                pool.wait_ge(s_scan, nth4(i, b))
                if after(i, b, 1):
                    pool.wait_ge(s_e, nth4(i, b, 1))
                pool.tensor_tensor(dr[:], top[b % 2][:, 0:G], top[b % 2][:, 1:], ALU.subtract).then_inc(s_sub, 1)
                pool.wait_ge(s_sub, nth4(i, b))
                pool.tensor_tensor(dr[:], dr[:], pair(new, b), ALU.add).then_inc(s_dr, 1)
            pipelined4(pool, n, ((steps_back, 9), (gather, 3)), DEEPEST)

        @block.vector
        def _(dve):
            for b in range(2):
                dve.memset(a12[b % 2][:], 0.0)
            dve.memset(w2[hi, :], 0.0)
            dve.memset(top[1][:, G:G + 1], BIG).then_inc(s_made, 1)
            dve.wait_ge(s_made, 2)
            dve.wait_ge(s_wch, 6)
            dve.tensor_scalar(w2[lo, :], w2[lo, :], 0.5, None, ALU.mult)
            dve.tensor_scalar(w3[hi, :], w3[hi, :], 0.5, None, ALU.mult)
            dve.tensor_scalar(b12h, b12, 0.5, None, ALU.mult)
            dve.tensor_scalar(bah, ba, 0.5, None, ALU.mult)
            dve.tensor_scalar(adots, adot, 0.4, None, ALU.mult).then_inc(s_made, 1)
            dve.wait_ge(s_made, 3)
            dve.tensor_scalar(head[:], head[:], adots, None, ALU.mult).then_inc(s_made, 1)

            def indices(i, b):
                if after(i, b, SLOTS):
                    dve.wait_ge(gs[b], i * (16 * TPG))
                dve.tensor_copy(idx[b][:], k.src_int[:, ds(i * (SLOTS * TPG) + b * TPG, TPG)]).then_inc(s_idx, 1)

            def mlp_gated(i, b):
                dve.wait_ge(s_t12, nth4(i, b))
                if after(i, b, 1):
                    dve.wait_ge(s_p12, nth4(i, b, 1))
                if after(i, b, 3):
                    dve.wait_ge(s_M, nth4(i, b, 3))
                dve.scalar_tensor_tensor(out=a12[b % 2][:], in0=t12[:], scalar=1.0, in1=x12[:], op0=ALU.add,
                                         op1=ALU.mult).then_inc(s_a12, 1)

            def onehot(i, b):
                dve.wait_ge(ldr[b // 2], (i + 1) * 16)
                if after(i, b, SLOTS):
                    dve.wait_ge(s_M, nth4(i, b, SLOTS))
                dve.tensor_scalar(oh[b][:], pair(rel, b), k.lane[:], None, ALU.is_equal).then_inc(s_oh, 1)

            def message(i, b):
                dve.wait_ge(s_M, nth4(i, b))
                dve.wait_ge(lde[b // 2], i * 16 + 16)
                if after(i, b, 1):
                    dve.wait_ge(s_mT, nth4(i, b, 1))
                dve.tensor_tensor(mea[:], pM[:], pair(ea, b), ALU.mult).then_inc(s_mea, 1)
                dve.wait_ge(s_mea, nth4(i, b))
                if after(i, b, SLOTS):
                    dve.wait_ge(s_V, nth4(i, b, SLOTS))
                dve.scalar_tensor_tensor(out=mT[b][:], in0=pR[:], scalar=b3, in1=mea[:], op0=ALU.add,
                                         op1=ALU.mult).then_inc(s_mT, 1)

            def gated(i, b):
                dve.wait_ge(s_x, nth4(i, b))
                if after(i, b, 2):
                    dve.wait_ge(s_S, nth4(i, b, 2))
                dve.scalar_tensor_tensor(out=z[b % 2][:], in0=ta[:], scalar=1.5, in1=xa[:], op0=ALU.add,
                                         op1=ALU.mult).then_inc(s_z, 1)

            def maxima(i, b):
                dve.wait_ge(s_S, nth4(i, b))
                dve.wait_ge(ldn[b // 2], i * 16 + 16)
                if after(i, b, 1):
                    dve.wait_ge(s_scan, nth4(i, b, 1))
                    dve.wait_ge(s_e, nth4(i, b, 1))
                if after(i, b, 2):
                    dve.wait_ge(s_dr, nth4(i, b, 2))
                before = top[(b + 1) % 2][:, G:G + 1]
                dve.tensor_copy(top[b % 2][:, 0:1], before)
                dve.tensor_tensor_scan(out=top[b % 2][:, 1:], data0=pair(new, b), data1=pS[:], op0=ALU.add, op1=ALU.max,
                                       initial=before).then_inc(s_scan, 1)
                dve.wait_ge(s_scan, nth4(i, b))
                dve.tensor_tensor(d[:], pS[:], top[b % 2][:, 1:], ALU.subtract).then_inc(s_d, 1)

            def sums(i, b):
                dve.wait_ge(s_e, nth4(i, b))
                dve.wait_ge(s_V, nth4(i, b))
                if after(i, b, 1):
                    dve.wait_ge(s_acc, nth4(i, b, 1))
                dve.tensor_tensor(pv[:], pV[:], p[:], ALU.mult).then_inc(s_pv, 1)
                if after(i, b, 2):
                    dve.wait_ge(s_T, nth4(i, b, 2))
                start = (lambda t: 0.0) if not after(i, b, 1) else (lambda t: t[(b + 1) % 2][:, G - 1:G])
                dve.tensor_tensor_scan(out=den[b % 2][:], data0=r[:], data1=p[:], op0=ALU.mult, op1=ALU.add, initial=start(den))
                dve.wait_ge(s_pv, nth4(i, b))
                dve.tensor_tensor_scan(out=acc[b % 2][:], data0=r[:], data1=pv[:], op0=ALU.mult, op1=ALU.add,
                                       initial=start(acc)).then_inc(s_acc, 1)

            pipelined4(dve, n, ((maxima, 9), (message, 6), (gated, 7), (onehot, 4), (sums, 9), (mlp_gated, 3, 1), (indices, 2)), DEEPEST)

        @block.scalar
        def _(act):
            act.wait_ge(s_made, 4)

            def attributes(i, b):
                act.wait_ge(s_At, nth4(i, b))
                if after(i, b, 2):
                    act.wait_ge(s_p12, nth4(i, b, 2))
                act.copy(atT[b % 2][:], pD[:, 0:P]).then_inc(s_atc, 1)

            def mlp_activated(i, b):
                act.wait_ge(s_p12, nth4(i, b))
                if after(i, b, 1):
                    act.wait_ge(s_a12, nth4(i, b, 1))
                act.activation(x12[:], p12[:], ACT.Identity, bias=b12[:])
                act.activation(t12[:], p12[:], ACT.Tanh, bias=b12h[:], scale=0.5).then_inc(s_t12, 1)

            def alphas(i, b):
                act.wait_ge(s_al, nth4(i, b))
                if after(i, b, 1):
                    act.wait_ge(s_z, nth4(i, b, 1))
                act.activation(xa[:], pA[:], ACT.Identity, bias=ba)
                act.activation(ta[:], pA[:], ACT.Tanh, bias=bah, scale=0.5).then_inc(s_x, 1)

            def exponents(i, b):
                act.wait_ge(s_d, nth4(i, b))
                if after(i, b, 1):
                    act.wait_ge(s_acc, nth4(i, b, 1))
                act.activation(p[:], d[:], ACT.Exp)
                act.wait_ge(s_dr, nth4(i, b))
                act.activation(r[:], dr[:], ACT.Exp).then_inc(s_e, 1)

            def rows(i, b):
                act.wait_ge(s_T, nth4(i, b))
                if after(i, b, 2):
                    slot, times = uses(i, b, 2)
                    act.wait_ge(st[slot], times * 16)
                act.copy(row[b % 2][:, :, 0:P], pT[:].rearrange("p (j d) -> p j d", d=P))
                act.copy(row[b % 2][:, :, P:], D3).then_inc(s_row, 1)

            pipelined4(act, n, ((attributes, 3), (alphas, 7), (rows, 10), (exponents, 9), (mlp_activated, 3, 1)), DEEPEST)

        @block.tensor
        def _(pe):
            pe.wait_ge(s_made, 4)

            def attributes(i, b):
                pe.wait_ge(lda[b // 2], i * 16 + 16)
                if after(i, b, 1):
                    pe.wait_ge(s_atc, nth4(i, b, 1))
                if after(i, b, 8):
                    pe.wait_ge(s_row, nth4(i, b, 8))
                pe.transpose(pD[:, 0:P], attr[b // 2][:, (b % 2) * TPG:(b % 2 + 1) * TPG, :].rearrange("p j f -> p (j f)"), k.ident[:]).then_inc(s_At, 1)

            def mlp_linear(i, b):
                if after(i, b, 1):
                    pe.wait_ge(s_t12, nth4(i, b, 1))
                    pe.wait_ge(s_a12, nth4(i, b, 1))
                second = pe.matmul(p12[hi, :], w2[:], a12[(b + 1) % 2][:], start=True, stop=True)
                if isinstance(i, int) and i == n:
                    second.then_inc(s_p12, 1)
                    return
                pe.wait_ge(s_atc, nth4(i, b))
                for j in range(TPG):
                    last = pe.matmul(p12[lo, j * P:(j + 1) * P], w1[:, j, :], atT[b % 2][:], start=True, stop=True)
                last.then_inc(s_p12, 1)

            def summed(i, b):
                pe.wait_ge(ldw[b], (i + 1) * (16 * TPG))
                pe.wait_ge(s_oh, nth4(i, b))
                if after(i, b, 1):
                    pe.wait_ge(s_mT, nth4(i, b, 1))
                pe.wait_ge(gs[b], (i + 1) * (16 * TPG))
                for j in range(TPG):
                    at = slice(j * P, (j + 1) * P)
                    pe.matmul(pM[:, at], win[b][:, j, :], oh[b][:, at], start=True, stop=False)
                    pe.matmul(pM[:, at], got[b][:, j, :], k.ident[:], start=False, stop=True)
                pe.wait_ge(s_a12, nth4(i, b) + 1)
                pe.matmul(pR[:], w3[hi, :], a12[(b + 1) % 2][hi, :], start=True, stop=True).then_inc(s_M, 1)

            def alpha(i, b):
                pe.wait_ge(s_mT, nth4(i, b))
                if after(i, b, 1):
                    pe.wait_ge(s_x, nth4(i, b, 1))
                pe.matmul(pA[:], wa[:], mT[b][:], start=True, stop=True).then_inc(s_al, 1)

            def score(i, b):
                pe.wait_ge(s_z, nth4(i, b))
                if after(i, b, 1):
                    pe.wait_ge(s_d, nth4(i, b, 1))
                pe.matmul(pS[:], head[:], z[b % 2][:], start=True, stop=True).then_inc(s_S, 1)

            def value(i, b):
                if after(i, b, 1):
                    pe.wait_ge(s_pv, nth4(i, b, 1))
                pe.wait_ge(s_mT, nth4(i, b))
                pe.matmul(pV[:], wv[:], mT[b][:], start=True, stop=True).then_inc(s_V, 1)

            def to_rows(i, b):
                pe.wait_ge(s_acc, nth4(i, b))
                if after(i, b, 1):
                    pe.wait_ge(s_row, nth4(i, b, 1))
                newest = nth4(i, b) + 7
                pe.wait_ge(s_atc, min(newest, SLOTS * n) if isinstance(i, int) else newest)
                for j in range(TPG):
                    pe.transpose(pT[:, j * P:(j + 1) * P], acc[b % 2][:, j * P:(j + 1) * P], k.ident[:])
                    last = pe.matmul(D3[:, j, :], den[b % 2][:, j * P:(j + 1) * P], pick[:], start=True, stop=True)
                last.then_inc(s_T, 1)

            pipelined4(pe, n, ((alpha, 7), (to_rows, 10), (mlp_linear, 3, 1), (score, 8), (summed, 5), (value, 8), (attributes, 2)), DEEPEST)


def update2(k, a, rows):
    H, HV = 8, 16

    def setup(c):
        bv = k.sb(c, "u2_bv", [P, H, HV])
        rs, rc, rh = ([k.sb(c, f"u2_{x}{b}", [P, NPG, H]) for b in range(SLOTS)] for x in ("rs", "rc", "rh"))
        t = [k.sb(c, f"u2_t{b}", [P, NPG, H, HV]) for b in range(SLOTS)]
        return (bv, rs, rc, rh, t), [(bv[:], a["L2_gnn_b_sep"].rearrange("(h t v) -> t h v", h=H, t=2)[1].partition_broadcast(P))]

    def combine(dve, extra, link, i, b, got, ag, own):
        bv, rs, rc, rh, t = extra
        den = got[:, :, P:]
        link(dve.tensor_scalar(rs[b][:], den, 1e-16, None, ALU.add), i, b, 1)
        link(dve.reciprocal(rc[b][:], rs[b][:]), i, b, 2)
        link(dve.tensor_tensor(rh[b][:], rc[b][:], k.has[:, ds(i * (SLOTS * NPG) + b * NPG, NPG)].unsqueeze(2).to_broadcast([P, NPG, H]),
                               ALU.mult), i, b, 3)
        for j in range(NPG):
            last = dve.tensor_tensor(t[b][:, j], bv[:], den[:, j, :].unsqueeze(2).to_broadcast([P, H, HV]), ALU.mult)
        link(last, i, b, 4)
        link(dve.tensor_tensor(t[b][:].rearrange("p j h v -> p j (h v)"), t[b][:].rearrange("p j h v -> p j (h v)"), got[:, :, 0:P],
                               ALU.add), i, b, 5)
        for j in range(NPG):
            last = dve.tensor_tensor(ag[:, j, :].rearrange("p (h v) -> p h v", h=H), t[b][:, j],
                                     rh[b][:, j, :].unsqueeze(2).to_broadcast([P, H, HV]), ALU.mult)
        return last
    add_rows(k, "u2", rows, W2COLS, 5, setup, combine, a["L2_gnn_w_proj"], a["L2_gnn_b_proj"])


def transpose_weight(k, w, to):
    s_l, s_p, s_c, s_o = (k.sem("w3_" + x) for x in "loaded transposed copied stored".split())
    with ExitStack() as c, k.nc.Block() as block:
        w_in, w_t, p_t = k.sb(c, "w3_in", [P, P]), k.sb(c, "w3_t", [P, P]), k.ps(c, "w3_p", [P, P])

        @block.sync
        def _(sp):
            sp.dma_start(w_in[:], w).then_inc(s_l, 16)
            sp.wait_ge(s_c, 1)
            sp.dma_start(to, w_t[:]).then_inc(s_o, 16)
            sp.wait_ge(s_o, 16)

        @block.tensor
        def _(pe):
            pe.wait_ge(s_l, 16)
            pe.transpose(p_t[:], w_in[:], k.ident[:]).then_inc(s_p, 1)

        @block.vector
        def _(dve):
            dve.wait_ge(s_p, 1)
            dve.tensor_copy(w_t[:], p_t[:]).then_inc(s_c, 1)


def layer3_edges(k, plain, out_rows):
    nc, n = k.nc, k.STEPS
    s_idx, s_C, s_scan, s_T, s_row = (k.sem("e3_" + x) for x in "indices columns scanned transposed rows".split())
    ld, gs, st = ([k.sem(f"e3_{x}{b}") for b in range(2)] for x in ("loaded", "gathered", "stored"))
    with ExitStack() as c, nc.Block() as block:
        two = lambda name, shape, dt=F32: [k.sb(c, f"e3_{name}{b}", shape, dt) for b in range(2)]
        keep, got, idx = two("keep", [P, G], BF16), two("got", [P, TPG, P]), two("idx", [P, TPG], I32)
        scan, row = two("scan", [P, G]), two("row", [P, TPG, P])
        pC, pT = ([k.ps(c, f"e3_p{x}{b}", [P, G]) for b in range(2)] for x in "CT")

        @block.sync
        def _(sp):
            def load(i, b):
                if later(i):
                    sp.wait_ge(s_scan, nth(i, b, 2))
                sp.dma_start(keep[b][:], k.KEEP[ds(i * (2 * G) + b * G, G)].partition_broadcast(P)).then_inc(ld[b], 16)

            def store(i, b):
                e = ds(i * (2 * G) + b * G, G)
                sp.wait_ge(s_row, nth(i, b))
                sp.dma_start(out_rows[e, :].rearrange("(j p) d -> p j d", p=P), row[b][:]).then_inc(st[b], 16)

            def body(i):
                for b in range(2):
                    if back(i, b, 0, n):
                        load(i, b)
                    if back(i, b, 3, n):
                        store(*back(i, b, 3, n))
            pipelined(sp, n, body, 3)
            for b in range(2):
                sp.wait_ge(st[b], 16 * n)

        @block.gpsimd
        def _(pool):
            def body(i):
                for b in range(2):
                    if not back(i, b, 0, n):
                        continue
                    pool.wait_ge(s_idx, nth(i, b))
                    if later(i):
                        pool.wait_ge(s_C, nth(i, b, 2))
                    k.settle(pool)
                    for j in range(TPG):
                        pool.indirect_dma_start(out=got[b][:, j, :], out_offset=None, in_=plain,
                                                in_offset=bass.IndirectOffsetOnAxis(ap=idx[b][:, j:j + 1], axis=0)
                                                ).then_inc(gs[b], 16)
            pipelined(pool, n, body, 3)

        @block.vector
        def _(dve):
            def indices(i, b):
                if later(i):
                    dve.wait_ge(gs[b], i * (16 * TPG))
                dve.tensor_copy(idx[b][:], k.src_int[:, ds(i * (2 * TPG) + b * TPG, TPG)]).then_inc(s_idx, 1)

            def running(i, b):
                first = isinstance(i, int) and i == 0 and b == 0
                dve.wait_ge(s_C, nth(i, b))
                dve.wait_ge(ld[b], i * 16 + 16)
                if later(i):
                    dve.wait_ge(s_T, nth(i, b, 2))
                if not first:
                    dve.wait_ge(s_scan, nth(i, b, 1))
                dve.tensor_tensor_scan(out=scan[b][:], data0=keep[b][:], data1=pC[b][:], op0=ALU.mult, op1=ALU.add,
                                       initial=0.0 if first else scan[1 - b][:, G - 1:G]).then_inc(s_scan, 1)

            def body(i):
                for b in range(2):
                    if back(i, b, 0, n):
                        indices(i, b)
                    if back(i, b, 2, n):
                        running(*back(i, b, 2, n))
            pipelined(dve, n, body, 3)

        @block.scalar
        def _(act):
            def rows(i, b):
                act.wait_ge(s_T, nth(i, b))
                if later(i):
                    act.wait_ge(st[b], i * 16)
                act.copy(row[b][:].rearrange("p j d -> p (j d)"), pT[b][:]).then_inc(s_row, 1)

            def body(i):
                for b in range(2):
                    if back(i, b, 3, n):
                        rows(*back(i, b, 3, n))
            pipelined(act, n, body, 3)

        @block.tensor
        def _(pe):
            def columns(i, b):
                pe.wait_ge(gs[b], (i + 1) * (16 * TPG))
                if later(i):
                    pe.wait_ge(s_scan, nth(i, b, 2))
                for j in range(TPG):
                    last = pe.transpose(pC[b][:, j * P:(j + 1) * P], got[b][:, j, :], k.ident[:])
                last.then_inc(s_C, 1)

            def to_rows(i, b):
                pe.wait_ge(s_scan, nth(i, b))
                if later(i):
                    pe.wait_ge(s_row, nth(i, b, 2))
                for j in range(TPG):
                    last = pe.transpose(pT[b][:, j * P:(j + 1) * P], scan[b][:, j * P:(j + 1) * P], k.ident[:])
                last.then_inc(s_T, 1)

            def body(i):
                for b in range(2):
                    if back(i, b, 1, n):
                        columns(*back(i, b, 1, n))
                    if back(i, b, 3, n):
                        to_rows(*back(i, b, 3, n))
            pipelined(pe, n, body, 3)


def update3(k, a, rows, own_rows, wt):
    def combine(dve, extra, link, i, b, got, ag, own):
        for j in range(NPG):
            last = dve.scalar_tensor_tensor(out=ag[:, j, :], in0=got[:, j, :], scalar=k.has[:, ds(i * (SLOTS * NPG) + (b * NPG + j), 1)],
                                            in1=own[:, j, :], op0=ALU.mult, op1=ALU.add)
        return last
    add_rows(k, "u3", rows, P, 0, lambda c: (None, []), combine, wt, a["L3_gnn_b"], own_rows=own_rows)


def store_nodes(k, out):
    s_o = k.sem("x_stored")
    full, rest = k.N // P, k.N % P
    X3 = k.X[:].rearrange("p (t d) -> p t d", d=P)
    with k.nc.Block() as block:
        @block.sync
        def _(sp):
            sp.dma_start(out[0:full * P].rearrange("(t p) d -> p t d", p=P), X3[:, 0:full, :]).then_inc(s_o, 16)
            if rest:
                sp.dma_start(out[full * P:, :], X3[0:rest, full, :]).then_inc(s_o, 16)
            sp.wait_ge(s_o, 32 if rest else 16)


def gnn_program(nc, a, out):
    with ExitStack() as ctx:
        k = Kit(nc, ctx, a["x"].shape[0], a["src"].shape[0])
        k.constants(ctx)
        setup_edges(k, a)
        setup_nodes(k)
        k.X = k.sb(ctx, "X", [P, k.NP])
        k.S1 = k.sb(ctx, "s1_by_node", [P, k.TN])
        transposed = ctx.enter_context(ExitStack())
        k.HT = k.sb(transposed, "HT", [P, k.NP])
        load_nodes(k, a["x"])
        plain0, plain2, plain3 = (k.dram(f"by_node_{x}", (k.NP, P)) for x in (0, 2, 3))
        rows, rows2 = k.dram("edge_rows", (k.EP, P)), k.dram("edge_rows_2", (k.EP, W2COLS))
        wt = k.dram("w3_transposed", (P, P))
        pair_tables(k, "n0", a["L0_gnn_W1"][0:P, :], a["L0_gnn_W1"][P:2 * P, :], a["L0_gnn_b1"], plain0, k.TB0)
        layer0_edges(k, a, plain0, rows)
        update0(k, a, rows)
        k.release_semaphores()
        normalize_only(k, "n1")
        layer1_tables(k, a)
        transposed.close()
        k.HT = None
        layer1_edges(k)
        update1(k)
        k.release_semaphores()
        pair_tables(k, "n2", a["L2_gnn_w_src"], a["L2_gnn_w_dst"], a["L2_gnn_b_src"], plain2, k.TB2)
        layer2_edges(k, a, plain2, rows2)
        update2(k, a, rows2)
        transpose_weight(k, a["L3_gnn_W"], wt)
        normalize_only(k, "n3", plain3)
        layer3_edges(k, plain3, rows)
        update3(k, a, rows, plain3, wt)
        store_nodes(k, out)


_INS = ["x", "src", "dst", "edge_attr_32", "edge_weight", "edge_weight1", "L0_gnn_W1", "L0_gnn_b1", "L0_gnn_W2", "L0_gnn_b2",
        "L0_gnn_U1", "L0_gnn_c1", "L0_gnn_U2", "L0_gnn_c2", "L1_gnn_kernel", "L1_gnn_kernel1", "L1_gnn_kernel2", "L1_gnn_gamma",
        "L1_gnn_beta", "L2_gnn_w_src", "L2_gnn_b_src", "L2_gnn_w_dst", "L2_gnn_fc_w1", "L2_gnn_fc_b1", "L2_gnn_fc_w2",
        "L2_gnn_fc_b2", "L2_gnn_fc_w3", "L2_gnn_fc_b3", "L2_gnn_w_sep", "L2_gnn_b_sep", "L2_gnn_alpha_dot", "L2_gnn_w_proj",
        "L2_gnn_b_proj", "L3_gnn_W", "L3_gnn_b"]


def kernel(**inputs):
    import numpy as _np
    import concourse.bacc as _bacc
    from concourse import mybir as _mybir
    from concourse.bass_utils import run_bass_kernel_spmd as _run

    nc = _bacc.Bacc("TRN2", target_bir_lowering=False, num_devices=1)
    arrays, args = {}, {}
    for name in _INS:
        v = _np.ascontiguousarray(inputs[name])
        arrays[f"in_{name}_dram"] = v
        args[name] = nc.dram_tensor(f"in_{name}_dram", v.shape, _mybir.dt.from_np(v.dtype), kind="ExternalInput").ap()
    out = nc.dram_tensor("out_0_dram", arrays["in_x_dram"].shape, F32, kind="ExternalOutput").ap()
    gnn_program(nc, args, out)
    r = _run(nc, [arrays], core_ids=[0])
    return r.results[0]["out_0_dram"]
```
